# Optimizing a Trainium2 kernel written in Bass

```python
import numpy as np
import jax
import jax.numpy as jnp

def _softmax(x, axis=-1):
    return jax.nn.softmax(x, axis=axis)

def _gelu(x):
    return jax.nn.gelu(x, approximate=True)

def _silu(x):
    return jax.nn.silu(x)

def _sigmoid(x):
    return jax.nn.sigmoid(x)

def _layernorm(x, axis=-1, eps=1e-05):
    m = jnp.mean(x, axis=axis, keepdims=True)
    v = jnp.var(x, axis=axis, keepdims=True)
    return (x - m) / jnp.sqrt(v + eps)

def _scatter_add(tgt, idx, src, axis=0):
    return tgt.at[idx].add(src)

def _segment_sum(src, seg, n):
    return jax.ops.segment_sum(src, seg, n)
kernel_name = 'mk_gnn_resnorm_d4_gnn_r64_3e30e2'

def setup_inputs(seed: int=0):
    np.random.seed(seed)
    _w = jnp.asarray

    def _rec_inputs():
        import jax
        import jax.numpy as jnp
        _gk = jax.random.key(seed)
        x = -0.0002117 + 1 * jax.random.normal(jax.random.fold_in(_gk, 1), (50000, 256), jnp.float32)
        _s = jax.random.randint(jax.random.fold_in(_gk, 2), (12500,), 0, 50000, jnp.int32)
        _d = jax.random.randint(jax.random.fold_in(_gk, 3), (12500,), 0, 50000, jnp.int32)
        _loop = jnp.arange(50000, dtype=jnp.int32)
        src = jnp.concatenate([_s, _d, _loop])
        dst = jnp.concatenate([_d, _s, _loop])
        _o = jnp.argsort(dst, stable=True)
        src = src[_o]
        dst = dst[_o]
        return (x, src, dst)
    x, src, dst = _rec_inputs()

    def _L0_gnn_setup():
        import jax, jax.numpy as jnp
        import numpy as np
        N = 100000
        E = 25000
        D = 256
        BN_EPS = 1e-05
        key = jax.random.key(seed)
        ks = jax.random.split(key, 6)
        node_feats = jax.random.normal(ks[0], (N, D), dtype=jnp.float32)
        src = jax.random.randint(ks[1], (E,), 0, N, dtype=jnp.int64)
        dst = jax.random.randint(ks[2], (E,), 0, N, dtype=jnp.int64)
        eps = jnp.zeros((1,), dtype=jnp.float32)
        W1 = jax.random.normal(ks[3], (D, 2 * D), dtype=jnp.float32) * (1.0 / np.sqrt(D))
        b1 = jnp.zeros((2 * D,), dtype=jnp.float32)
        W2 = jax.random.normal(ks[4], (2 * D, D), dtype=jnp.float32) * (1.0 / np.sqrt(2 * D))
        b2 = jnp.zeros((D,), dtype=jnp.float32)
        gamma = jnp.ones((D,), dtype=jnp.float32)
        beta = jnp.zeros((D,), dtype=jnp.float32)
        return {'node_feats': node_feats, 'src': src, 'dst': dst, 'eps': eps, 'W1': W1, 'b1': b1, 'W2': W2, 'b2': b2, 'gamma': gamma, 'beta': beta}
    _L0_gnn_all = _L0_gnn_setup()
    _L0_gnn_in = {k: v for k, v in _L0_gnn_all.items() if k in ('eps', 'W1', 'b1', 'W2', 'b2', 'gamma', 'beta')}
    del _L0_gnn_all

    def _L1_gnn_setup():
        import jax, jax.numpy as jnp
        import numpy as np
        N = 20000
        E = 5000
        D_IN = 256
        HID = 64
        HEADS = 4
        D_OUT = 256
        EPS = 1e-05
        SLOPE = 0.2

        def _gat(x, src, dst, W, a_src, a_dst, b, heads, ch, concat):
            n = x.shape[0]
            h = (x @ W).reshape(n, heads, ch)
            es = (h * a_src).sum(-1)
            ed = (h * a_dst).sum(-1)
            e = jax.nn.leaky_relu(es[src] + ed[dst], SLOPE)
            m = jax.ops.segment_max(e, dst, num_segments=n)
            w = jnp.exp(e - m[dst])
            den = jax.ops.segment_sum(w, dst, num_segments=n)
            alpha = w / den[dst]
            msg = h[src] * alpha[:, :, None]
            out = jax.ops.segment_sum(msg, dst, num_segments=n)
            out = out.reshape(n, heads * ch) if concat else out.mean(axis=1)
            return out + b

        def _layernorm(x, g, b):
            mu = x.mean(-1, keepdims=True)
            v = ((x - mu) ** 2).mean(-1, keepdims=True)
            return (x - mu) * jax.lax.rsqrt(v + EPS) * g + b
        key = jax.random.key(seed)
        ks = jax.random.split(key, 10)

        def glorot(k, shape):
            fan_in, fan_out = (shape[0], int(np.prod(shape[1:])))
            s = np.sqrt(2.0 / (fan_in + fan_out)).astype(np.float32)
            return jax.random.normal(k, shape, dtype=jnp.float32) * s
        x = jax.random.normal(ks[0], (N, D_IN), dtype=jnp.float32)
        edge_index = jax.random.randint(ks[1], (2, E), 0, N, dtype=jnp.int64)
        return {'x': x, 'edge_index': edge_index, 'W1': glorot(ks[2], (D_IN, HEADS * HID)), 'a1_src': glorot(ks[3], (HEADS, HID)), 'a1_dst': glorot(ks[4], (HEADS, HID)), 'b1': jnp.zeros((HEADS * HID,), jnp.float32), 'ln_g': jnp.ones((HEADS * HID,), jnp.float32), 'ln_b': jnp.zeros((HEADS * HID,), jnp.float32), 'W2': glorot(ks[5], (HEADS * HID, D_OUT)), 'a2_src': glorot(ks[6], (1, D_OUT)), 'a2_dst': glorot(ks[7], (1, D_OUT)), 'b2': jnp.zeros((D_OUT,), jnp.float32)}
    _L1_gnn_all = _L1_gnn_setup()
    _L1_gnn_in = {k: v for k, v in _L1_gnn_all.items() if k in ('W1', 'a1_src', 'a1_dst', 'b1', 'ln_g', 'ln_b', 'W2', 'a2_src', 'a2_dst', 'b2')}
    del _L1_gnn_all

    def _L2_gnn_setup():
        import jax, jax.numpy as jnp
        import numpy as np
        N_NODES = 50000
        N_EDGES = 12500
        IN_FEAT = 256
        HEADS = 4
        OUT_FEAT = 64
        NEG_SLOPE = 0.2
        key = jax.random.key(seed)
        k1, k2, k3, k4, k5, k6 = jax.random.split(key, 6)
        x = jax.random.normal(k1, (N_NODES, IN_FEAT), dtype=jnp.float32)
        edge_index = jax.random.randint(k2, (2, N_EDGES), 0, N_NODES, dtype=jnp.int64)
        scale = 1.0 / np.sqrt(IN_FEAT)
        W = jax.random.normal(k3, (IN_FEAT, HEADS * OUT_FEAT), dtype=jnp.float32) * scale
        att_src = jax.random.normal(k4, (HEADS, OUT_FEAT), dtype=jnp.float32) * scale
        att_dst = jax.random.normal(k5, (HEADS, OUT_FEAT), dtype=jnp.float32) * scale
        bias = jax.random.normal(k6, (HEADS * OUT_FEAT,), dtype=jnp.float32) * 0.01
        return {'x': x, 'edge_index': edge_index, 'W': W, 'att_src': att_src, 'att_dst': att_dst, 'bias': bias}
    _L2_gnn_all = _L2_gnn_setup()
    _L2_gnn_in = {k: v for k, v in _L2_gnn_all.items() if k in ('W', 'att_src', 'att_dst', 'bias')}
    del _L2_gnn_all

    def _L3_gnn_setup():
        import jax, jax.numpy as jnp
        import numpy as np
        N_NODES = 50000
        N_EDGES = 12500
        IN_CH = 256
        OUT_CH = 64
        HEADS = 4
        key = jax.random.key(seed)
        k1, k2, k3, k4, k5 = jax.random.split(key, 5)
        x = jax.random.normal(k1, (N_NODES, IN_CH), dtype=jnp.float32)
        edge_index = jax.random.randint(k2, (2, N_EDGES), 0, N_NODES, dtype=jnp.int64)
        weight = jax.random.normal(k3, (HEADS, IN_CH, OUT_CH), dtype=jnp.float32) * (2.0 / (IN_CH + OUT_CH)) ** 0.5
        att_src = jax.random.normal(k4, (1, HEADS, OUT_CH), dtype=jnp.float32) * 0.1
        att_dst = jax.random.normal(k5, (1, HEADS, OUT_CH), dtype=jnp.float32) * 0.1
        bias = jnp.zeros((HEADS * OUT_CH,), dtype=jnp.float32)
        return {'x': x, 'edge_index': edge_index, 'weight': weight, 'att_src': att_src, 'att_dst': att_dst, 'bias': bias}
    _L3_gnn_all = _L3_gnn_setup()
    _L3_gnn_in = {k: v for k, v in _L3_gnn_all.items() if k in ('weight', 'att_src', 'att_dst', 'bias')}
    del _L3_gnn_all
    return {'x': x, 'src': src, 'dst': dst, 'L0_gnn_eps': _L0_gnn_in['eps'], 'L0_gnn_W1': _L0_gnn_in['W1'], 'L0_gnn_b1': _L0_gnn_in['b1'], 'L0_gnn_W2': _L0_gnn_in['W2'], 'L0_gnn_b2': _L0_gnn_in['b2'], 'L0_gnn_gamma': _L0_gnn_in['gamma'], 'L0_gnn_beta': _L0_gnn_in['beta'], 'L1_gnn_W1': _L1_gnn_in['W1'], 'L1_gnn_a1_src': _L1_gnn_in['a1_src'], 'L1_gnn_a1_dst': _L1_gnn_in['a1_dst'], 'L1_gnn_b1': _L1_gnn_in['b1'], 'L1_gnn_ln_g': _L1_gnn_in['ln_g'], 'L1_gnn_ln_b': _L1_gnn_in['ln_b'], 'L1_gnn_W2': _L1_gnn_in['W2'], 'L1_gnn_a2_src': _L1_gnn_in['a2_src'], 'L1_gnn_a2_dst': _L1_gnn_in['a2_dst'], 'L1_gnn_b2': _L1_gnn_in['b2'], 'L2_gnn_W': _L2_gnn_in['W'], 'L2_gnn_att_src': _L2_gnn_in['att_src'], 'L2_gnn_att_dst': _L2_gnn_in['att_dst'], 'L2_gnn_bias': _L2_gnn_in['bias'], 'L3_gnn_weight': _L3_gnn_in['weight'], 'L3_gnn_att_src': _L3_gnn_in['att_src'], 'L3_gnn_att_dst': _L3_gnn_in['att_dst'], 'L3_gnn_bias': _L3_gnn_in['bias']}

def reference(x, src, dst, L0_gnn_eps, L0_gnn_W1, L0_gnn_b1, L0_gnn_W2, L0_gnn_b2, L0_gnn_gamma, L0_gnn_beta, L1_gnn_W1, L1_gnn_a1_src, L1_gnn_a1_dst, L1_gnn_b1, L1_gnn_ln_g, L1_gnn_ln_b, L1_gnn_W2, L1_gnn_a2_src, L1_gnn_a2_dst, L1_gnn_b2, L2_gnn_W, L2_gnn_att_src, L2_gnn_att_dst, L2_gnn_bias, L3_gnn_weight, L3_gnn_att_src, L3_gnn_att_dst, L3_gnn_bias):
    import jax
    import jax.numpy as jnp

    def _L0_gnn_ref(node_feats, src, dst, eps, W1, b1, W2, b2, gamma, beta):
        import jax, jax.numpy as jnp
        import numpy as np
        N = 100000
        E = 25000
        D = 256
        BN_EPS = 1e-05
        n = node_feats.shape[0]
        neigh = jax.ops.segment_sum(node_feats[src], dst, num_segments=n)
        h = (1.0 + eps) * node_feats + neigh
        h = jax.nn.relu(h @ W1 + b1) @ W2 + b2
        mean = jnp.mean(h, axis=0)
        var = jnp.mean(jnp.square(h - mean), axis=0)
        h = (h - mean) * jax.lax.rsqrt(var + BN_EPS) * gamma + beta
        return h

    def _L1_gnn_ref(x, edge_index, W1, a1_src, a1_dst, b1, ln_g, ln_b, W2, a2_src, a2_dst, b2):
        import jax, jax.numpy as jnp
        import numpy as np
        N = 20000
        E = 5000
        D_IN = 256
        HID = 64
        HEADS = 4
        D_OUT = 256
        EPS = 1e-05
        SLOPE = 0.2

        def _gat(x, src, dst, W, a_src, a_dst, b, heads, ch, concat):
            n = x.shape[0]
            h = (x @ W).reshape(n, heads, ch)
            es = (h * a_src).sum(-1)
            ed = (h * a_dst).sum(-1)
            e = jax.nn.leaky_relu(es[src] + ed[dst], SLOPE)
            m = jax.ops.segment_max(e, dst, num_segments=n)
            w = jnp.exp(e - m[dst])
            den = jax.ops.segment_sum(w, dst, num_segments=n)
            alpha = w / den[dst]
            msg = h[src] * alpha[:, :, None]
            out = jax.ops.segment_sum(msg, dst, num_segments=n)
            out = out.reshape(n, heads * ch) if concat else out.mean(axis=1)
            return out + b

        def _layernorm(x, g, b):
            mu = x.mean(-1, keepdims=True)
            v = ((x - mu) ** 2).mean(-1, keepdims=True)
            return (x - mu) * jax.lax.rsqrt(v + EPS) * g + b
        loops = jnp.arange(N, dtype=edge_index.dtype)
        src = jnp.concatenate([edge_index[0], loops])
        dst = jnp.concatenate([edge_index[1], loops])
        h = _gat(x, src, dst, W1, a1_src, a1_dst, b1, HEADS, HID, True)
        h = jax.nn.relu(_layernorm(h, ln_g, ln_b))
        out = _gat(h, src, dst, W2, a2_src, a2_dst, b2, 1, D_OUT, False)
        return out

    def _L2_gnn_ref(x, edge_index, W, att_src, att_dst, bias):
        import jax, jax.numpy as jnp
        import numpy as np
        N_NODES = 50000
        N_EDGES = 12500
        IN_FEAT = 256
        HEADS = 4
        OUT_FEAT = 64
        NEG_SLOPE = 0.2
        N = x.shape[0]
        H, C = att_src.shape
        h = (x @ W).reshape(N, H, C)
        a_src = jnp.sum(h * att_src[None], axis=-1)
        a_dst = jnp.sum(h * att_dst[None], axis=-1)
        loop = jnp.arange(N, dtype=edge_index.dtype)
        src = jnp.concatenate([edge_index[0], loop])
        dst = jnp.concatenate([edge_index[1], loop])
        alpha = jax.nn.leaky_relu(a_src[src] + a_dst[dst], NEG_SLOPE)
        m = jax.ops.segment_max(alpha, dst, num_segments=N)
        alpha = jnp.exp(alpha - jax.lax.stop_gradient(m)[dst])
        denom = jax.ops.segment_sum(alpha, dst, num_segments=N)
        alpha = alpha / (denom[dst] + 1e-16)
        msg = h[src] * alpha[:, :, None]
        out = jax.ops.segment_sum(msg, dst, num_segments=N)
        out = out.reshape(N, H * C) + bias
        return jax.nn.relu(out)

    def _L3_gnn_ref(x, edge_index, weight, att_src, att_dst, bias):
        import jax, jax.numpy as jnp
        import numpy as np
        N_NODES = 50000
        N_EDGES = 12500
        IN_CH = 256
        OUT_CH = 64
        HEADS = 4
        num_nodes = x.shape[0]
        row, col = (edge_index[0], edge_index[1])
        x_h = jnp.einsum('nf,hfc->nhc', x, weight)
        alpha_src = jnp.sum(x_h * att_src[0], axis=-1)
        alpha_dst = jnp.sum(x_h * att_dst[0], axis=-1)
        alpha = alpha_src[row] + alpha_dst[col]
        alpha = jax.nn.leaky_relu(alpha, negative_slope=0.2)
        alpha_max = jax.ops.segment_max(alpha, row, num_segments=num_nodes)
        alpha = jnp.exp(alpha - alpha_max[row])
        alpha_sum = jax.ops.segment_sum(alpha, row, num_segments=num_nodes)
        alpha = alpha / jnp.clip(alpha_sum[row], 1e-16)
        messages = alpha[:, :, None] * x_h[col]
        out = jax.ops.segment_sum(messages, row, num_segments=num_nodes)
        out = out.reshape(num_nodes, -1) + bias
        return out
    edge_index = jnp.stack([src, dst])
    x = _layernorm(x + _L0_gnn_ref(x, src, dst, L0_gnn_eps, L0_gnn_W1, L0_gnn_b1, L0_gnn_W2, L0_gnn_b2, L0_gnn_gamma, L0_gnn_beta), axis=-1)
    x = _layernorm(x + _L1_gnn_ref(x, edge_index, L1_gnn_W1, L1_gnn_a1_src, L1_gnn_a1_dst, L1_gnn_b1, L1_gnn_ln_g, L1_gnn_ln_b, L1_gnn_W2, L1_gnn_a2_src, L1_gnn_a2_dst, L1_gnn_b2), axis=-1)
    x = _layernorm(x + _L2_gnn_ref(x, edge_index, L2_gnn_W, L2_gnn_att_src, L2_gnn_att_dst, L2_gnn_bias), axis=-1)
    x = _layernorm(x + _L3_gnn_ref(x, edge_index, L3_gnn_weight, L3_gnn_att_src, L3_gnn_att_dst, L3_gnn_bias), axis=-1)
    return x

_drawn_inputs = setup_inputs


def setup_inputs(seed=0):
    import zlib

    import numpy as np

    out = dict(_drawn_inputs(seed))
    spreads = {'L0_gnn_b1': (0.0, 0.1),
     'L0_gnn_b2': (0.0, 2.0),
     'L0_gnn_gamma': (1.0, 0.2),
     'L0_gnn_beta': (0.0, 0.1),
     'L1_gnn_b1': (0.0, 0.1),
     'L1_gnn_ln_g': (1.0, 0.2),
     'L1_gnn_ln_b': (0.0, 0.1),
     'L1_gnn_b2': (0.0, 0.1),
     'L3_gnn_bias': (0.0, 0.1)}
    factors = {'L1_gnn_a2_src': 2.704,
     'L1_gnn_a2_dst': 17.674,
     'L2_gnn_att_dst': 31.957,
     'L2_gnn_bias': 8.0}
    for name, (base, spread) in spreads.items():
        noise = np.random.default_rng([zlib.crc32(name.encode()), seed]).standard_normal(out[name].shape)
        drawn = base * np.exp(spread * noise) if base else spread * noise
        out[name] = jnp.asarray(drawn.astype(out[name].dtype))
    for name, factor in factors.items():
        out[name] = (out[name] * factor).astype(out[name].dtype)
    return out
```

```python
import concourse.bass as bass
from concourse import mybir
from contextlib import ExitStack

F32 = mybir.dt.float32
F16 = mybir.dt.float16
BF16 = mybir.dt.bfloat16
I32 = mybir.dt.int32
ALU = mybir.AluOpType
ACT = mybir.ActivationFunctionType
AX = mybir.AxisListType.X

P = 128
C = 256
KC = C // P
HID = 2 * C
FC = HID // P
NB = 8
EPS = 1e-5
FAR = 1e30
SLOPE = 0.2


def graph_layers(nc, a, out, n_nodes, n_loops):
    NP = a["x"].shape[0]
    T = NP // P
    G = T // NB
    J = a["src"].shape[0] // P
    LEVELS = (J * P) // P + 1
    assert T % NB == 0 and G >= 3 and J % 2 == 0 and T <= 512
    x_in = a["x"]

    def dram(name, rows, cols):
        return nc.dram_tensor(name, (rows, cols), F32).ap()

    RWMAX = C + 4 + 3 * 4 + 1
    h_dram = dram("h_dram", NP, C)
    x1_dram = dram("x1_dram", NP, C)
    x2_dram = dram("x2_dram", NP, C)
    x3_dram = dram("x3_dram", NP, C)
    heads = [4, 1, 4, 4]
    row_w = [C + 4 * h + 1 for h in heads]
    rows_dram = [dram(f"rows{q}_dram", NP, row_w[q]) for q in range(4)]
    state_dram = [dram(f"state{q}_dram", NP, row_w[q]) for q in range(4)]
    xstate_dram = dram("xstate_dram", NP, C)
    table_dram = [dram(f"table{k}_dram", LEVELS * P, T) for k in range(2)]

    ctx = ExitStack()
    with ctx:
        def sb(name, shape, dt=F32):
            return ctx.enter_context(nc.sbuf_tensor(name, shape, dt))

        def bufs(name, shape, dt=F32, n=NB):
            return [sb(f"{name}{i}", shape, dt) for i in range(n)]

        sems = {}

        def sem(name):
            if name not in sems:
                sems[name] = ctx.enter_context(nc.semaphore(name))
            return sems[name]

        ident = sb("ident", [P, P])
        iota_n = sb("iota_n", [P, P])
        iota_t = sb("iota_t", [P, T], F16)
        before = sb("before", [P, P], F16)
        not_before = sb("not_before", [P, P], F16)
        ones16 = sb("ones16", [P, P], F16)
        ones = sb("ones", [P, P])
        minus_half = sb("minus_half", [P, 1])
        tab_idx = [sb(f"tab_idx{k}", [P, T], I32) for k in range(2)]
        tab_loc = [sb(f"tab_loc{k}", [P, T]) for k in range(2)]
        loops = [sb(f"loops{i}", [P, T]) for i in range(3)]
        gone = [sb(f"gone{i}", [P, T]) for i in range(3)]
        valid = sb("valid", [P, T])
        fac = sb("fac", [P, T])
        n_levels = sb("n_levels", [P, 2], I32)
        n_further = sb("n_further", [P, 2], I32)
        W1 = sb("W1", [P, KC, HID])
        W2 = sb("W2", [P, FC, C])
        b1_col = sb("b1_col", [P, FC])
        b2_bc = sb("b2_bc", [P, C])
        WG = [sb(f"WG{q}", [P, KC, C + 2 * heads[q]]) for q in range(4)]
        bias_bc = [sb(f"bias_bc{q}", [P, C]) for q in range(4)]
        gam_bc = sb("gam_bc", [P, C])
        bet_bc = sb("bet_bc", [P, C])
        lng_col = sb("lng_col", [P, KC])
        lnb_col = sb("lnb_col", [P, KC])
        sum_h = sb("sum_h", [P, C])
        sum_hh = sb("sum_hh", [P, C])

        bank = [ctx.enter_context(nc.psum_tensor(f"bank{i}", [P, 512], F32)) for i in range(8)]

        stands = {}

        def upto(name, n):
            return stands.get(name, 0) + n

        def settled(e):
            e.sem_inc(sem("settled"), 1)

        def wait(e, name, g, u, back=0, scale=1, settle=False):
            n = (g * NB + u + 1 - back) * scale
            if isinstance(n, int) and n <= 0:
                return
            e.wait_ge(sem(name), n + stands.get(name, 0))
            if settle or e.engine == nc.gpsimd.engine:
                settled(e)

        def wait_dma(e, name, g, u, back=0):
            n = g + 1 - back
            if isinstance(n, int) and n <= 0:
                return
            e.wait_ge(sem(f"{name}{u}"), n * 16 + stands.get(name, 0))
            if e.engine == nc.gpsimd.engine:
                settled(e)

        def clear(prefix):
            with nc.Block() as block:
                @block.gpsimd
                def _(e):
                    for name in sorted(sems):
                        if name.startswith(prefix):
                            e.sem_clear(sems[name])

        def inc(ins, name):
            ins.then_inc(sem(name), 1)

        def inc_dma(ins, name, u):
            ins.then_inc(sem(f"{name}{u}"), 16)

        def pass_over(steps, dmas):
            for name in steps:
                stands[name] = stands.get(name, 0) + T
            for name in dmas:
                stands[name] = stands.get(name, 0) + 16 * G

        def skewed(e, stages, fresh=False):
            deepest = max(d for d, _ in stages)
            first = max(1, -(-(deepest + NB * fresh) // NB))
            for s in range(first * NB):
                for d, f in stages:
                    if s >= d:
                        f((s - d) // NB, (s - d) % NB)
            with e.Fori(first, G) as g:
                for u in range(NB):
                    for d, f in stages:
                        f(g + (u - d) // NB, (u - d) % NB)
            for s in range(T, T + deepest):
                for d, f in stages:
                    if s - d < T:
                        f((s - d) // NB, (s - d) % NB)

        def rows_of(dr, g, u):
            return dr[bass.ds((g * NB + u) * P, P), :]

        def col(t_sb, g, u):
            return t_sb[:, bass.ds(g * NB + u, 1)]

        prep = ExitStack()
        with prep:
            def pb(name, shape, dt=F32):
                return prep.enter_context(nc.sbuf_tensor(name, shape, dt))

            src_i = pb("src_i", [P, J], I32)
            dst_i = pb("dst_i", [P, J], I32)
            src_f = pb("src_f", [P, J])
            dst_f = pb("dst_f", [P, J])
            other = pb("other", [P, J])
            itself = pb("itself", [P, J])
            tmp_i = pb("tmp_i", [P, J], I32)
            tmp_f = pb("tmp_f", [P, J])
            code = pb("code", [P, J])
            code_i = pb("code_i", [P, J], I32)
            dst_loc = pb("dst_loc", [P, J])
            dst_tile = pb("dst_tile", [P, J])
            tile_of = [pb(f"tile_of{k}", [P, J]) for k in range(2)]
            piece = [[pb(f"piece{k}{i}", [P, J]) for i in range(3)] for k in range(2)]
            rank = [pb(f"rank{k}", [P, J]) for k in range(2)]
            level_rank = pb("level_rank", [P, J])
            hit = [pb(f"hit{i}", [P, T], F16) for i in range(2)]
            hit_all = [pb(f"hit_all{i}", [P, T], F16) for i in range(2)]
            picked = [pb(f"picked{i}", [P, T]) for i in range(2)]
            slot1 = [pb(f"slot_f{i}", [P, P]) for i in range(2)]
            slot = [[pb(f"slot{i}{k}", [P, P], BF16) for k in range(3)] for i in range(2)]
            counts = pb("counts", [P, T])
            most = pb("most", [P, 2])
            tab_f = pb("tab_f", [P, T])
            tab_c = pb("tab_c", [P, T], I32)
            tab_d = pb("tab_d", [P, 1], I32)
            node_i = pb("node_i", [P, T], I32)
            node_f = pb("node_f", [P, T])
            iota_i = pb("iota_i", [P, max(T, P)], I32)
            eps_bc = pb("eps_bc", [P, 1])
            att_bc = [[pb(f"att_bc{q}{i}", [P, C]) for i in range(2)] for q in range(4)]
            prod = pb("prod", [P, C])

            gat_w = [a["L1_gnn_W1"], a["L1_gnn_W2"], a["L2_gnn_W"], None]
            gat_b = [a["L1_gnn_b1"], a["L1_gnn_b2"], a["L2_gnn_bias"], a["L3_gnn_bias"]]
            gat_a = [(a["L1_gnn_a1_src"], a["L1_gnn_a1_dst"]), (a["L1_gnn_a2_src"], a["L1_gnn_a2_dst"]),
                     (a["L2_gnn_att_src"], a["L2_gnn_att_dst"]), (a["L3_gnn_att_dst"], a["L3_gnn_att_src"])]

            def bcast(v):
                if len(v.shape) == 3:
                    v = v.rearrange("a h c -> (a h c)")
                elif len(v.shape) == 2:
                    v = v.rearrange("h c -> (h c)")
                return v.partition_broadcast(P)

            with nc.Block() as block:
                @block.sync
                def _(e):
                    e.dma_start(src_i[:], a["src"].rearrange("(p j) -> p j", p=P)).then_inc(sem("edges_in"), 16)
                    e.dma_start(dst_i[:], a["dst"].rearrange("(p j) -> p j", p=P)).then_inc(sem("edges_in"), 16)
                    n = 0
                    for dst, s in ([(W1[:], a["L0_gnn_W1"].rearrange("(k p) n -> p k n", p=P)),
                                    (W2[:], a["L0_gnn_W2"].rearrange("(k p) n -> p k n", p=P)),
                                    (b2_bc[:], bcast(a["L0_gnn_b2"])), (gam_bc[:], bcast(a["L0_gnn_gamma"])),
                                    (bet_bc[:], bcast(a["L0_gnn_beta"])), (eps_bc[:], bcast(a["L0_gnn_eps"]))]
                                   + [(bias_bc[q][:], bcast(gat_b[q])) for q in range(4)]
                                   + [(att_bc[q][i][:], bcast(gat_a[q][i])) for q in range(4) for i in range(2)]
                                   + [(WG[q][:, :, 0:C], gat_w[q].rearrange("(k p) n -> p k n", p=P)) for q in range(3)]
                                   + [(WG[3][:, k, 0:C].rearrange("p (h c) -> p h c", h=4),
                                       a["L3_gnn_weight"][:, k * P:(k + 1) * P, :].rearrange("h p c -> p h c"))
                                      for k in range(KC)]):
                        e.dma_start(dst, s).then_inc(sem("weights_in"), 16)
                        n += 16
                    with nc.allow_non_contiguous_dma("a few columns of 128"):
                        for dst, s in [(b1_col[:], a["L0_gnn_b1"].rearrange("(k p) -> p k", p=P)),
                                       (lng_col[:], a["L1_gnn_ln_g"].rearrange("(k p) -> p k", p=P)),
                                       (lnb_col[:], a["L1_gnn_ln_b"].rearrange("(k p) -> p k", p=P))]:
                            e.dma_start(dst, s).then_inc(sem("weights_in"), 16)
                            n += 16
                    e.wait_ge(sem("edges_in"), 32)
                    e.wait_ge(sem("weights_in"), n)

                @block.gpsimd
                def _(e):
                    e.memset(ident[:], 0.0).then_inc(sem("consts"), 1)
                    e.memset(ones[:], 1.0).then_inc(sem("consts"), 1)
                    e.memset(ones16[:], 1.0).then_inc(sem("consts"), 1)
                    e.memset(minus_half[:], -0.5).then_inc(sem("consts"), 1)
                    e.memset(sum_h[:], 0.0).then_inc(sem("consts"), 1)
                    e.memset(sum_hh[:], 0.0).then_inc(sem("consts"), 1)
                    e.iota(iota_i[:], pattern=[[1, max(T, P)]], base=0, channel_multiplier=0).then_inc(sem("consts"), 1)
                    e.iota(node_i[:], pattern=[[P, T]], base=0, channel_multiplier=1).then_inc(sem("consts"), 1)
                    e.wait_ge(sem("consts"), 8)
                    e.affine_select(out=ident[:], in_=ident[:], compare_op=ALU.not_equal, fill=1.0,
                                    base=0, pattern=[[-1, P]], channel_multiplier=1).then_inc(sem("consts"), 1)
                    e.affine_select(out=before[:], in_=ones16[:], compare_op=ALU.is_ge, fill=0.0,
                                    base=-1, pattern=[[1, P]], channel_multiplier=-1).then_inc(sem("consts"), 1)
                    e.affine_select(out=not_before[:], in_=ones16[:], compare_op=ALU.is_ge, fill=0.0,
                                    base=0, pattern=[[-1, P]], channel_multiplier=1).then_inc(sem("consts"), 1)

            with nc.Block() as block:
                @block.vector
                def _(e):
                    k = [0]

                    def link(ins):
                        k[0] += 1
                        ins.then_inc(sem("dve_setup"), 1)
                        e.wait_ge(sem("dve_setup"), k[0])

                    link(e.tensor_copy(iota_t[:], iota_i[:, 0:T]))
                    link(e.tensor_copy(iota_n[:], iota_i[:, 0:P]))
                    link(e.tensor_copy(node_f[:], node_i[:]))
                    link(e.tensor_scalar(valid[:], node_f[:], float(n_nodes), None, ALU.is_lt))
                    link(e.tensor_scalar(loops[1][:], node_f[:], float(n_loops), None, ALU.is_lt))
                    link(e.tensor_copy(src_f[:], src_i[:]))
                    link(e.tensor_copy(dst_f[:], dst_i[:]))
                    link(e.tensor_tensor(other[:], src_f[:], dst_f[:], ALU.not_equal))
                    link(e.tensor_tensor(itself[:], src_f[:], dst_f[:], ALU.is_equal))
                    for key, own, far in ((0, dst_i, src_f), (1, src_i, dst_f)):
                        link(e.tensor_scalar(tmp_i[:], own[:], 127, None, ALU.bitwise_and))
                        link(e.tensor_copy(tmp_f[:], tmp_i[:]))
                        if key == 0:
                            link(e.tensor_copy(dst_loc[:], tmp_f[:]))
                        link(e.scalar_tensor_tensor(out=code[:], in0=far[:], scalar=256.0, in1=tmp_f[:],
                                                    op0=ALU.mult, op1=ALU.add))
                        link(e.scalar_tensor_tensor(out=code[:], in0=code[:], scalar=1.0, in1=other[:],
                                                    op0=ALU.add, op1=ALU.mult))
                        link(e.tensor_copy(code_i[:], code[:]))
                        for i in range(3):
                            link(e.tensor_scalar(tmp_i[:], code_i[:], 0xFF << (8 * i), None, ALU.bitwise_and))
                            link(e.tensor_copy(piece[key][i][:], tmp_i[:]))
                        link(e.tensor_scalar(tmp_i[:], own[:], 7, None, ALU.logical_shift_right))
                        link(e.tensor_copy(tmp_f[:], tmp_i[:]))
                        if key == 0:
                            link(e.tensor_copy(dst_tile[:], tmp_f[:]))
                        link(e.scalar_tensor_tensor(out=tile_of[key][:], in0=itself[:], scalar=1024.0, in1=tmp_f[:],
                                                    op0=ALU.mult, op1=ALU.add))
                    for q in range(4):
                        H = heads[q]
                        for i in range(2):
                            for kc in range(KC):
                                link(e.tensor_tensor(prod[:], WG[q][:, kc, 0:C], att_bc[q][i][:], ALU.mult))
                                link(e.tensor_reduce(WG[q][:, kc, C + i * H:C + (i + 1) * H],
                                                     prod[:].rearrange("p (h c) -> p h c", h=H),
                                                     axis=AX, op=ALU.add))

            for key in range(2):
                with nc.Block() as block:
                    base = key * J

                    @block.vector
                    def _(e):
                        with e.Fori(0, J // 2) as r:
                            for u in range(2):
                                n = base + r * 2 + u + 1
                                e.wait_ge(sem("rank_added"), n - 2 + 2)
                                e.tensor_scalar(hit[u][:], iota_t[:], tile_of[key][:, bass.ds(r * 2 + u, 1)], None,
                                                ALU.is_equal).then_inc(sem("rank_hit"), 1)
                                e.wait_ge(sem("rank_hit"), n)
                                e.wait_ge(sem("rank_counted"), n)
                                e.scalar_tensor_tensor(out=picked[u][:], in0=bank[u][:, 0:T], scalar=1.0,
                                                       in1=hit[u][:], op0=ALU.mult, op1=ALU.mult,
                                                       accum_out=rank[key][:, bass.ds(r * 2 + u, 1)])\
                                    .then_inc(sem("rank_read"), 1)
                        e.wait_ge(sem("rank_added"), base + J + 2)
                        e.tensor_reduce(most[:, 0:1], bank[0][:, 0:T], axis=AX, op=ALU.max).then_inc(sem("dve_levels"), 1)
                        e.wait_ge(sem("dve_levels"), key * 7 + 1)
                        e.tensor_scalar(most[:, 1:2], most[:, 0:1], 1.0, 127.0, ALU.max, ALU.add)\
                            .then_inc(sem("dve_levels"), 1)
                        e.wait_ge(sem("dve_levels"), key * 7 + 2)
                        e.tensor_copy(tab_c[:, 0:1], most[:, 1:2]).then_inc(sem("dve_levels"), 1)
                        e.tensor_scalar(tab_d[:, 0:1], most[:, 1:2], -128.0, None, ALU.add)\
                            .then_inc(sem("dve_levels"), 1)
                        e.wait_ge(sem("dve_levels"), key * 7 + 4)
                        e.tensor_scalar(n_levels[:, key:key + 1], tab_c[:, 0:1], 7, None, ALU.logical_shift_right)\
                            .then_inc(sem("dve_levels"), 1)
                        e.tensor_scalar(n_further[:, key:key + 1], tab_d[:, 0:1], 7, None, ALU.logical_shift_right)\
                            .then_inc(sem("dve_levels"), 1)
                        e.tensor_copy(level_rank[:], rank[key][:]).then_inc(sem("dve_levels"), 1)

                    @block.tensor
                    def _(e):
                        if key == 0:
                            e.sem_inc(sem("rank_added"), 2)
                        def count(n, u, first):
                            e.wait_ge(sem("rank_hit"), n)
                            e.matmul(bank[u][:, 0:T], before[:], hit[u][:], start=first, stop=True,
                                     skip_group_check=True).then_inc(sem("rank_counted"), 1)

                        def add(n, u, first):
                            e.matmul(bank[1 - u][:, 0:T], ones16[:], hit[u][:], start=first, stop=True,
                                     skip_group_check=True)
                            e.wait_ge(sem("rank_read"), n)
                            e.matmul(bank[u][:, 0:T], not_before[:], hit[u][:], start=False, stop=True,
                                     skip_group_check=True).then_inc(sem("rank_added"), 1)

                        for u in range(2):
                            count(base + u + 1, u, u == 0)
                            add(base + u + 1, u, u == 0)
                        with e.Fori(1, J // 2) as r:
                            for u in range(2):
                                count(base + r * 2 + u + 1, u, False)
                                add(base + r * 2 + u + 1, u, False)

                with nc.Block() as block:
                    def levels(e):
                        return e.value_load(n_levels[0:1, key:key + 1], min_val=1, max_val=LEVELS)

                    @block.vector
                    def _(e):
                        nl = levels(e)
                        e.sem_inc(sem("pl_table_full"), 2)
                        with e.Fori(0, nl) as L:
                            with e.Fori(0, J // 2) as r:
                                for u in range(2):
                                    j = bass.ds(r * 2 + u, 1)
                                    n = L * J + r * 2 + u + 1
                                    e.wait_ge(sem("pl_placed"), n)
                                    e.tensor_scalar(hit[u][:], iota_t[:], tile_of[key][:, j], None, ALU.is_equal)\
                                        .then_inc(sem("pl_place_hit"), 1)
                                    e.tensor_scalar(slot1[u][:], iota_n[:], level_rank[:, j], None, ALU.is_equal)\
                                        .then_inc(sem("pl_place_slot"), 1)
                                    e.wait_ge(sem("pl_place_slot"), n)
                                    e.tensor_scalar(slot[u][0][:], slot1[u][:], piece[key][0][:, j], None, ALU.mult)\
                                        .then_inc(sem("pl_place_hit"), 1)
                            e.wait_ge(sem("pl_placed"), (L + 1) * J + 2)
                            e.wait_ge(sem("pl_table_free"), L + 1)
                            e.tensor_copy(tab_f[:], bank[2][:, 0:T]).then_inc(sem("pl_table_full"), 1)
                            e.tensor_scalar(level_rank[:], level_rank[:], -128.0, None, ALU.add)\
                                .then_inc(sem("pl_table_full"), 1)
                            e.wait_ge(sem("pl_table_full"), (L + 2) * 2)
                            settled(e)

                    @block.scalar
                    def _(e):
                        nl = levels(e)
                        with e.Fori(0, nl) as L:
                            with e.Fori(0, J // 2) as r:
                                for u in range(2):
                                    j = bass.ds(r * 2 + u, 1)
                                    n = L * J + r * 2 + u + 1
                                    e.wait_ge(sem("pl_place_slot"), n)
                                    for i in range(1, 3):
                                        e.activation(slot[u][i][:], slot1[u][:], ACT.Copy, scale=piece[key][i][:, j])\
                                            .then_inc(sem("pl_place_pieces"), 1)

                    @block.tensor
                    def _(e):
                        nl = levels(e)
                        e.sem_inc(sem("pl_placed"), 2)
                        with e.Fori(0, nl) as L:
                            e.wait_ge(sem("pl_table_full"), L * 2 + 2)
                            def place(r, u, first):
                                n = L * J + r * 2 + u + 1
                                e.wait_ge(sem("pl_place_hit"), n * 2)
                                e.wait_ge(sem("pl_place_pieces"), n * 2)
                                for i in range(3):
                                    last = e.matmul(bank[2][:, 0:T], slot[u][i][:], hit[u][:],
                                                    start=(first and i == 0), stop=True, skip_group_check=True)
                                last.then_inc(sem("pl_placed"), 1)

                            place(0, 0, True)
                            place(0, 1, False)
                            with e.Fori(1, J // 2) as r:
                                for u in range(2):
                                    place(r, u, False)

                    @block.sync
                    def _(e):
                        nl = levels(e)
                        e.sem_inc(sem("pl_table_free"), 1)
                        with e.Fori(0, nl) as L:
                            e.wait_ge(sem("pl_table_full"), L * 2 + 4)
                            e.dma_start(table_dram[key][bass.ds(L * P, P), :], tab_f[:])\
                                .then_inc(sem("pl_table_out"), 16)
                            e.wait_ge(sem("pl_table_out"), L * 16 + 16)
                            e.sem_inc(sem("pl_table_free"), 1)
                clear("pl_")

                if key == 0:
                    with nc.Block() as block:
                        @block.vector
                        def _(e):
                            with e.Fori(0, J // 2) as r:
                                for u in range(2):
                                    n = r * 2 + u + 1
                                    e.wait_ge(sem("self_added"), n)
                                    e.tensor_scalar(hit_all[u][:], iota_t[:], dst_tile[:, bass.ds(r * 2 + u, 1)], None,
                                                    ALU.is_equal).then_inc(sem("self_hit"), 1)
                                    e.tensor_scalar(slot1[u][:], iota_n[:], dst_loc[:, bass.ds(r * 2 + u, 1)], None,
                                                    ALU.is_equal).then_inc(sem("self_loc"), 1)
                                    e.wait_ge(sem("self_loc"), n)
                                    e.tensor_scalar(slot[u][0][:], slot1[u][:], itself[:, bass.ds(r * 2 + u, 1)], None,
                                                    ALU.mult).then_inc(sem("self_hit"), 1)

                        @block.tensor
                        def _(e):
                            e.sem_inc(sem("self_added"), 2)
                            def add(r, u, first):
                                e.wait_ge(sem("self_hit"), (r * 2 + u + 1) * 2)
                                e.matmul(bank[3][:, 0:T], slot[u][0][:], hit_all[u][:], start=first, stop=True,
                                         skip_group_check=True).then_inc(sem("self_added"), 1)
                            add(0, 0, True)
                            add(0, 1, False)
                            with e.Fori(1, J // 2) as r:
                                for u in range(2):
                                    add(r, u, False)

            def decode(e, link, tab, idx, loc, scratch_i):
                link(e.tensor_copy(scratch_i, tab))
                link(e.tensor_scalar(idx, scratch_i, 8, None, ALU.logical_shift_right))
                link(e.tensor_scalar(scratch_i, scratch_i, 255, None, ALU.bitwise_and))
                link(e.tensor_copy(loc, scratch_i))
                link(e.tensor_scalar(loc, loc, -1.0, None, ALU.add))

            with nc.Block() as block:
                @block.sync
                def _(e):
                    for key in range(2):
                        if key:
                            e.wait_ge(sem("dve_tables"), 5)
                        e.dma_start(tab_f[:], table_dram[key][0:P, :]).then_inc(sem("table_in"), 16)

                @block.vector
                def _(e):
                    k = [0]

                    def link(ins):
                        k[0] += 1
                        ins.then_inc(sem("dve_tables"), 1)
                        e.wait_ge(sem("dve_tables"), k[0])

                    for key in range(2):
                        e.wait_ge(sem("table_in"), 16 * (key + 1))
                        decode(e, link, tab_f[:], tab_idx[key][:], tab_loc[key][:], tab_c[:])
                    link(e.tensor_copy(loops[0][:], bank[3][:, 0:T]))
                    link(e.tensor_tensor(loops[1][:], loops[1][:], loops[0][:], ALU.add))
                    link(e.tensor_scalar(loops[2][:], loops[0][:], 1.0, None, ALU.add))
                    for i in range(3):
                        link(e.tensor_scalar(gone[i][:], loops[i][:], 0.0, -FAR, ALU.is_equal, ALU.mult))
                    link(e.tensor_scalar(eps_bc[:], eps_bc[:], 1.0, None, ALU.add))
                    link(e.tensor_scalar(fac[:], loops[0][:], eps_bc[:, 0:1], None, ALU.add))

        ix = bufs("ix", [P, 1], I32)
        own = bufs("own", [P, RWMAX])
        got = bufs("got", [P, RWMAX])
        hot = bufs("hot", [P, P])
        hotT = bufs("hotT", [P, P])
        off = bufs("off", [P, P], n=4)
        cand = bufs("cand", [P, 4, P], n=4)
        small = bufs("small", [P, 16 * 4])
        norms = bufs("norms", [P, 16])
        wide = bufs("wide", [P, C + 4])
        mess = bufs("mess", [P, C + 4])
        conv = bufs("conv", [P, C])
        res = bufs("res", [P, C])
        xn = bufs("xn", [P, C])
        xT = bufs("xT", [P, KC, P])
        row = bufs("row", [P, RWMAX])
        ov_tab = sb("ov_tab", [P, T])
        ov_idx = sb("ov_idx", [P, T], I32)
        ov_loc = sb("ov_loc", [P, T])
        ov_sc = sb("ov_sc", [P, T], I32)

        def S(u, i, H):
            return small[u][:, 4 * i:4 * i + H]
        (S_S, S_LK, S_MN, S_DF, S_WI, S_A, S_A2, S_Z, S_W, S_RD, S_WC, S_DG) = range(12)

        def heads_of(ap, H):
            return ap.rearrange("p (h c) -> p h c", h=H)

        def over(ap, H, n):
            return ap.unsqueeze(2).to_broadcast([P, H, n])

        def further_of(e, key):
            return e.value_load(n_further[0:1, key:key + 1], min_val=0, max_val=LEVELS - 1)

        def overflow(tag, key, table, src_rows, state, H):
            W = src_rows.shape[1]
            D = C // H if H else 0
            HD = C + H
            with nc.Block() as block:
                def when(e, body, level_start=None):
                    nf = further_of(e, key)
                    with e.If(nf > 0):
                        with e.Fori(0, nf) as L:
                            if level_start:
                                level_start(L)
                            with e.Fori(0, T) as t:
                                body(L, t, L * T + t)
                        e.nop()

                def s(name):
                    return sem(f"got_ov{tag}" if name == "got" else f"ov_{name}")

                @block.sync
                def _(e):
                    def level(L):
                        e.dma_start(ov_tab[:], table_dram[key][bass.ds(L * P + P, P), :]).then_inc(s("table"), 16)

                    def body(L, t, g):
                        at = bass.ds(t * P, P)
                        with e.If(L < 1):
                            e.dma_start(own[0][:, 0:W], src_rows[at, :]).then_inc(s("own"), 16)
                        with e.Else():
                            e.dma_start(own[0][:, 0:W], state[at, :]).then_inc(s("own"), 16)
                        e.wait_ge(s("state"), g + 2)
                        e.dma_start(state[at, :], own[0][:, 0:W]).then_inc(s("stored"), 16)
                        e.wait_ge(s("stored"), g * 16 + 16)
                        settled(e)
                    when(e, body, level)

                @block.gpsimd
                def _(e):
                    def body(L, t, g):
                        e.wait_ge(s("decoded"), L * 5 + 5)
                        settled(e)
                        e.wait_ge(s("state"), g + 1)
                        settled(e)
                        e.tensor_copy(ix[0][:], ov_idx[:, bass.ds(t, 1)]).then_inc(s("ix"), 1)
                        e.wait_ge(s("ix"), g + 1)
                        settled(e)
                        e.indirect_dma_start(got[0][:, 0:W], None, table,
                                             bass.IndirectOffsetOnAxis(ap=ix[0][:], axis=0)).then_inc(s("got"), 16)
                    when(e, body)

                @block.vector
                def _(e):
                    e.sem_inc(s("state"), 1)

                    def level(L):
                        e.wait_ge(s("table"), L * 16 + 16)
                        k = [0]

                        def link(ins):
                            k[0] += 1
                            ins.then_inc(s("decoded"), 1)
                            e.wait_ge(s("decoded"), L * 5 + k[0])
                        decode(e, link, ov_tab[:], ov_idx[:], ov_loc[:], ov_sc[:])
                        settled(e)

                    def body(L, t, g):
                        k = [0]
                        n_links = 11 if H else 1

                        def link(ins):
                            k[0] += 1
                            ins.then_inc(s("dve"), 1)
                            e.wait_ge(s("dve"), g * n_links + k[0])

                        e.tensor_scalar(hot[0][:], iota_n[:], ov_loc[:, bass.ds(t, 1)], None, ALU.is_equal)\
                            .then_inc(s("hot"), 1)
                        e.wait_ge(s("own"), (g + 1) * 16)
                        if not H:
                            settled(e)
                            with e.If(L < 1):
                                e.tensor_scalar(own[0][:, 0:C], own[0][:, 0:C], fac[:, bass.ds(t, 1)], None, ALU.mult)\
                                    .then_inc(s("dve"), 1)
                            with e.Else():
                                e.tensor_scalar(own[0][:, 0:C], own[0][:, 0:C], 1.0, None, ALU.mult)\
                                    .then_inc(s("dve"), 1)
                            e.wait_ge(s("dve"), g + 1)
                            e.wait_ge(s("sums"), g + 1)
                            e.tensor_tensor(own[0][:, 0:C], own[0][:, 0:C], bank[2][:, 0:C], ALU.add)\
                                .then_inc(s("state"), 1)
                            return
                        e.wait_ge(s("turned"), g + 1)
                        mx = bank[0][:, 0:H * P].rearrange("p (h e) -> p h e", h=H)
                        es, ed, m = (own[0][:, HD + i * H:HD + (i + 1) * H] for i in range(3))
                        link(e.tensor_reduce(S(0, S_S, H), mx, axis=AX, op=ALU.max))
                        link(e.tensor_tensor(S(0, S_S, H), S(0, S_S, H), ed, ALU.add))
                        link(e.scalar_tensor_tensor(out=S(0, S_LK, H), in0=S(0, S_S, H), scalar=SLOPE, in1=S(0, S_S, H),
                                                    op0=ALU.mult, op1=ALU.max))
                        link(e.tensor_tensor(S(0, S_MN, H), S(0, S_LK, H), m, ALU.max))
                        link(e.tensor_tensor(S(0, S_DF, H), m, S(0, S_MN, H), ALU.subtract))
                        e.wait_ge(s("edge_cols"), g + 1)
                        link(e.tensor_tensor(S(0, S_A, H), got[0][:, HD:HD + H], bank[1][:, P:P + H], ALU.add))
                        link(e.scalar_tensor_tensor(out=S(0, S_A2, H), in0=S(0, S_A, H), scalar=SLOPE, in1=S(0, S_A, H),
                                                    op0=ALU.mult, op1=ALU.max))
                        link(e.tensor_tensor(S(0, S_Z, H), S(0, S_A2, H), bank[1][:, P + 4:P + 4 + H], ALU.subtract))
                        e.wait_ge(s("exps"), (g + 1) * 2)
                        e.scalar_tensor_tensor(out=heads_of(mess[0][:, 0:HD], H), in0=over(S(0, S_W, H), H, D + 1),
                                               scalar=1.0, in1=heads_of(got[0][:, 0:HD], H),
                                               op0=ALU.min, op1=ALU.mult).then_inc(s("mess"), 1)
                        link(e.tensor_scalar(S(0, S_WC, H), S(0, S_WI, H), own[0][:, W - 1:W], None, ALU.mult))
                        link(e.tensor_tensor(heads_of(wide[0][:, 0:HD], H), heads_of(own[0][:, 0:HD], H),
                                             over(S(0, S_WC, H), H, D + 1), ALU.mult))
                        link(e.tensor_copy(m, S(0, S_MN, H)))
                        e.tensor_scalar(own[0][:, W - 1:W], S(0, S_WC, 1), 0.0, 1.0, ALU.mult, ALU.add)\
                            .then_inc(s("count1"), 1)
                        e.wait_ge(s("count1"), g + 1)
                        e.wait_ge(s("sums"), g + 1)
                        e.tensor_tensor(own[0][:, 0:HD], wide[0][:, 0:HD], bank[2][:, 0:HD], ALU.add)\
                            .then_inc(s("state"), 1)
                    when(e, body, level)

                if H:
                    @block.scalar
                    def _(e):
                        def body(L, t, g):
                            e.wait_ge(s("hot"), g + 1)
                            e.activation(off[0][:], hot[0][:], ACT.Copy, scale=FAR, bias=-FAR).then_inc(s("off"), 1)
                            e.wait_ge(s("off"), g + 1)
                            e.wait_ge(s("got"), (g + 1) * 16)
                            for h in range(H):
                                last = e.activation(cand[0][:, h, :], off[0][:], ACT.Identity,
                                                    bias=got[0][:, HD + h:HD + h + 1])
                            last.then_inc(s("cand"), 1)
                            e.wait_ge(s("turned"), g + 1)
                            e.activation(hotT[0][:], bank[1][:, 0:P], ACT.Copy).then_inc(s("hotT"), 1)
                            e.wait_ge(s("dve"), g * 11 + 5)
                            e.activation(S(0, S_WI, H), S(0, S_DF, H), ACT.Exp).then_inc(s("exps"), 1)
                            e.wait_ge(s("dve"), g * 11 + 8)
                            e.activation(S(0, S_W, H), S(0, S_Z, H), ACT.Exp).then_inc(s("exps"), 1)
                        when(e, body)

                @block.tensor
                def _(e):
                    def body(L, t, g):
                        if not H:
                            e.wait_ge(s("hot"), g + 1)
                            e.wait_ge(s("got"), (g + 1) * 16)
                            e.wait_ge(s("state"), g + 1)
                            e.matmul(bank[2][:, 0:C], hot[0][:], got[0][:, 0:C], start=True, stop=True)\
                                .then_inc(s("sums"), 1)
                            return
                        e.wait_ge(s("cand"), g + 1)
                        for h in range(H):
                            e.transpose(bank[0][:, h * P:(h + 1) * P], cand[0][:, h, :], ident[:])
                        e.transpose(bank[1][:, 0:P], hot[0][:], ident[:]).then_inc(s("turned"), 1)
                        e.wait_ge(s("hotT"), g + 1)
                        e.wait_ge(s("dve"), g * 11 + 4)
                        e.matmul(bank[1][:, P:P + H], hotT[0][:], own[0][:, HD + H:HD + 2 * H], start=True, stop=True)
                        e.matmul(bank[1][:, P + 4:P + 4 + H], hotT[0][:], S(0, S_MN, H), start=True, stop=True)\
                            .then_inc(s("edge_cols"), 1)
                        e.wait_ge(s("mess"), g + 1)
                        e.matmul(bank[2][:, 0:HD], hot[0][:], mess[0][:, 0:HD], start=True, stop=True)\
                            .then_inc(s("sums"), 1)
                    when(e, body)

            clear("ov_")

        overflow('x', 0, x_in, x_in, xstate_dram, 0)
        hotd = bufs("hotd", [P, P], n=4)
        hidT = bufs("hidT", [P, FC, P], n=2)
        with nc.Block() as block:
            ps_hT = [bank[0], bank[1]]
            ps_hid = [bank[2], bank[3]]
            ps_out = [bank[4], bank[5]]

            @block.sync
            def _(e):
                nf = further_of(e, 0)

                def load(g, u):
                    wait(e, "a_hT", g, u, 8, settle=True)
                    with e.If(nf > 0):
                        inc_dma(e.dma_start(own[u][:, 0:C], rows_of(xstate_dram, g, u)), "own_in", u)
                    with e.Else():
                        inc_dma(e.dma_start(own[u][:, 0:C], rows_of(x_in, g, u)), "own_in", u)

                def store(g, u):
                    wait(e, "a_out", g, u)
                    inc_dma(e.dma_start(rows_of(h_dram, g, u), conv[u][:]), "conv_out", u)
                skewed(e, [(6, store), (0, load)], True)
                for u in range(NB):
                    e.wait_ge(sem(f"conv_out{u}"), upto("conv_out", 16 * G))

            @block.gpsimd
            def _(e):
                def gather(g, u):
                    wait(e, "a_hT", g, u, 8)
                    inc(e.tensor_copy(ix[u][:], col(tab_idx[0], g, u)), "ix_made")
                    wait(e, "ix_made", g, u)
                    inc_dma(e.indirect_dma_start(got[u][:, 0:C], None, x_in,
                                                 bass.IndirectOffsetOnAxis(ap=ix[u][:], axis=0)), "got_in", u)

                def squares(g, u):
                    wait(e, "a_sq", g, u)
                    wait(e, "a_sum_hh", g, u, 1)
                    inc(e.tensor_tensor(sum_hh[:], sum_hh[:], xn[u][:], ALU.add), "a_sum_hh")

                def plus_b2(g, u):
                    wait(e, "a_z", g, u)
                    wait_dma(e, "conv_out", g, u, 1)
                    inc(e.tensor_tensor(conv[u][:], mess[u][:, 0:C], b2_bc[:], ALU.add), "a_out")
                skewed(e, [(6, plus_b2), (6, squares), (0, gather)], True)

            @block.vector
            def _(e):
                nf = further_of(e, 0)
                with e.If(nf > 0):
                    e.memset(fac[:], 1.0).then_inc(sem("a_fac"), 1)
                with e.Else():
                    e.tensor_scalar(fac[:], fac[:], 1.0, None, ALU.mult).then_inc(sem("a_fac"), 1)
                e.wait_ge(sem("a_fac"), 1)

                def onehot(g, u):
                    wait(e, "a_hT", g, u, 4)
                    inc(e.tensor_scalar(hot[u][:], iota_n[:], col(tab_loc[0], g, u), None, ALU.is_equal), "a_hot")
                    inc(e.tensor_scalar(hotd[u % 4][:], ident[:], col(fac, g, u), None, ALU.mult), "a_hotd")

                def out_h(g, u):
                    wait(e, "a_mlp", g, u)
                    wait(e, "a_out", g, u, 8)
                    wait(e, "a_sq", g, u, 8)
                    inc(e.tensor_scalar(mess[u][:, 0:C], ps_out[u % 2][:, 0:C], col(valid, g, u), None, ALU.mult), "a_z")

                def sum_up(g, u):
                    wait(e, "a_z", g, u)
                    wait(e, "a_sum_h", g, u, 1)
                    inc(e.tensor_tensor(sum_h[:], sum_h[:], mess[u][:, 0:C], ALU.add), "a_sum_h")
                skewed(e, [(4, out_h), (0, onehot), (4, sum_up)], True)

            @block.scalar
            def _(e):
                def evac_hT(g, u):
                    wait(e, "a_hT", g, u)
                    wait(e, "a_hid_mm", g, u, 8)
                    inc(e.activation(xT[u][:], ps_hT[u % 2][:, 0:C].rearrange("p (k n) -> p k n", k=KC), ACT.Copy),
                        "a_hT_sb")

                def relu(g, u):
                    wait(e, "a_hid_mm", g, u)
                    wait(e, "a_mlp", g, u, 2)
                    for f in range(FC):
                        last = e.activation(hidT[u % 2][:, f, :], ps_hid[u % 2][:, f * P:(f + 1) * P], ACT.Relu,
                                            bias=b1_col[:, f:f + 1])
                    inc(last, "a_hid")

                def square(g, u):
                    wait(e, "a_z", g, u)
                    wait(e, "a_sum_hh", g, u, 8)
                    inc(e.activation(xn[u][:], mess[u][:, 0:C], ACT.Square), "a_sq")
                skewed(e, [(2, square), (1, relu), (0, evac_hT)], True)

            @block.tensor
            def _(e):
                def hT(g, u):
                    wait(e, "a_hotd", g, u)
                    wait_dma(e, "got_in", g, u)
                    wait_dma(e, "own_in", g, u)
                    wait(e, "a_hT_sb", g, u, 2)
                    for k in range(KC):
                        ks = slice(k * P, (k + 1) * P)
                        e.matmul(ps_hT[u % 2][:, ks], got[u][:, ks], hot[u][:], start=True, stop=False)
                        last = e.matmul(ps_hT[u % 2][:, ks], own[u][:, ks], hotd[u % 4][:], start=False, stop=True)
                    inc(last, "a_hT")

                def hidden(g, u):
                    wait(e, "a_hT_sb", g, u)
                    wait(e, "a_hid", g, u, 2)
                    for f in range(FC):
                        for k in range(KC):
                            last = e.matmul(ps_hid[u % 2][:, f * P:(f + 1) * P], W1[:, k, f * P:(f + 1) * P],
                                            xT[u][:, k, :], start=(k == 0), stop=(k == KC - 1))
                    inc(last, "a_hid_mm")

                def out_mm(g, u):
                    wait(e, "a_hid", g, u)
                    wait(e, "a_z", g, u, 2)
                    for f in range(FC):
                        last = e.matmul(ps_out[u % 2][:, 0:C], hidT[u % 2][:, f, :], W2[:, f, :],
                                        start=(f == 0), stop=(f == FC - 1))
                    inc(last, "a_mlp")
                skewed(e, [(0, hT), (2, out_mm), (1, hidden)], True)
        pass_over(["ix_made", "a_hT", "a_out", "a_sq", "a_sum_hh", "a_hot", "a_hotd", "a_z", "a_mlp", "a_sum_h", "a_hT_sb",
                   "a_hid_mm", "a_hid"], ["own_in", "conv_out", "got_in"])

        bn_mul = sb("bn_mul", [P, C])
        bn_add = sb("bn_add", [P, C])
        bn_t = sb("bn_t", [P, C])
        bn_m = sb("bn_m", [P, C])
        with nc.Block() as block:
            @block.tensor
            def _(e):
                e.matmul(bank[0][:, 0:C], ones[:], sum_h[:], start=True, stop=True)
                e.matmul(bank[1][:, 0:C], ones[:], sum_hh[:], start=True, stop=True).then_inc(sem("bn_sums"), 1)

            @block.vector
            def _(e):
                k = [0]

                def link(ins):
                    k[0] += 1
                    ins.then_inc(sem("bn_dve"), 1)
                    e.wait_ge(sem("bn_dve"), k[0])
                e.wait_ge(sem("bn_sums"), 1)
                link(e.tensor_scalar(bn_m[:], bank[0][:, 0:C], 1.0 / n_nodes, None, ALU.mult))
                link(e.tensor_tensor(bn_t[:], bn_m[:], bn_m[:], ALU.mult))
                link(e.scalar_tensor_tensor(out=bn_t[:], in0=bank[1][:, 0:C], scalar=1.0 / n_nodes, in1=bn_t[:],
                                            op0=ALU.mult, op1=ALU.subtract))
                link(e.tensor_scalar(bn_t[:], bn_t[:], 0.0, EPS, ALU.max, ALU.add))
                e.wait_ge(sem("bn_act"), 1)
                link(e.reciprocal(bn_mul[:], bn_add[:]))
                link(e.tensor_tensor(bn_mul[:], bn_mul[:], gam_bc[:], ALU.mult))
                link(e.tensor_tensor(bn_m[:], bn_m[:], b2_bc[:], ALU.add))
                link(e.tensor_tensor(bn_m[:], bn_m[:], bn_mul[:], ALU.mult))
                link(e.tensor_tensor(bn_add[:], bet_bc[:], bn_m[:], ALU.subtract))

            @block.scalar
            def _(e):
                e.wait_ge(sem("bn_dve"), 4)
                e.activation(bn_add[:], bn_t[:], ACT.Sqrt).then_inc(sem("bn_act"), 1)

        ps_x = bank[5]
        ps_rows = [bank[6], bank[7]]
        N_BN, N_MV, N_VE, N_RS, N_NB = 0, 6, 8, 9, 10

        def dve_stats(e):
            def stats(g, u):
                wait(e, "v", g, u)
                inc(e.bn_stats(norms[u][:, N_BN:N_BN + 6], conv[u][:]), "n_stats")

            def aggr(g, u):
                wait(e, "n_stats", g, u, settle=True)
                inc(e.bn_aggr(norms[u][:, N_MV:N_MV + 2], norms[u][:, N_BN:N_BN + 6]), "n_mv")

            def add_eps(g, u):
                wait(e, "n_mv", g, u)
                inc(e.tensor_scalar(norms[u][:, N_VE:N_VE + 1], norms[u][:, N_MV + 1:N_MV + 2], EPS, None, ALU.add),
                    "n_ve")

            def shift(g, u):
                wait(e, "n_rstd", g, u)
                inc(e.tensor_scalar(norms[u][:, N_NB:N_NB + 1], norms[u][:, N_MV:N_MV + 1],
                                    norms[u][:, N_RS:N_RS + 1], -1.0, ALU.mult, ALU.mult), "n_shift")
            return stats, aggr, add_eps, shift

        def pool_rstd(e):
            def rstd(g, u):
                wait(e, "n_ve", g, u)
                inc(e.tensor_tensor(norms[u][:, N_RS:N_RS + 1], norms[u][:, N_VE:N_VE + 1], minus_half[:], ALU.pow),
                    "n_rstd")
            return rstd

        def act_tail(e, stored, q, relu_affine):
            def norm(g, u):
                wait(e, "n_shift", g, u)
                if stored:
                    wait_dma(e, "xn_out", g, u, 1)
                if q is not None:
                    wait(e, "x_turned", g, u, 8)
                inc(e.activation(xn[u][:], conv[u][:], ACT.Identity, bias=norms[u][:, N_NB:N_NB + 1],
                                 scale=norms[u][:, N_RS:N_RS + 1]), "x_normed")

            def evac_xT(g, u):
                wait(e, "x_turned", g, u)
                wait(e, "rows_mm", g, u, 8)
                half = ps_x[:, 0:C]
                if relu_affine:
                    for k in range(KC):
                        last = e.activation(xT[u][:, k, :], half[:, k * P:(k + 1) * P], ACT.Relu,
                                            bias=lnb_col[:, k:k + 1], scale=lng_col[:, k:k + 1])
                    inc(last, "xT_sb")
                else:
                    inc(e.activation(xT[u][:], half.rearrange("p (k n) -> p k n", k=KC), ACT.Copy), "xT_sb")

            def evac_rows(g, u):
                H = heads[q]
                D, HD = C // H, C + H
                wait(e, "rows_mm", g, u)
                wait_dma(e, "rows_out", g, u, 1)
                e.activation(heads_of(row[u][:, 0:HD], H)[:, :, 0:D],
                             ps_rows[u % 2][:, 0:C].rearrange("p (h c) -> p h c", h=H), ACT.Copy)
                inc(e.activation(row[u][:, HD:HD + 2 * H], ps_rows[u % 2][:, C:C + 2 * H], ACT.Copy), "rows_sb")
            return norm, evac_xT, evac_rows

        def pe_tail(e, q):
            def turn(g, u):
                wait(e, "x_normed", g, u)
                wait(e, "xT_sb", g, u, 1)
                half = ps_x[:, 0:C]
                for k in range(KC):
                    last = e.transpose(half[:, k * P:(k + 1) * P], xn[u][:, k * P:(k + 1) * P], ident[:])
                inc(last, "x_turned")

            def rows(g, u):
                W = C + 2 * heads[q]
                wait(e, "xT_sb", g, u)
                wait(e, "rows_sb", g, u, 2)
                for k in range(KC):
                    last = e.matmul(ps_rows[u % 2][:, 0:W], xT[u][:, k, :], WG[q][:, k, :],
                                    start=(k == 0), stop=(k == KC - 1))
                inc(last, "rows_mm")
            return turn, rows

        def pool_rows(e, q):
            H = heads[q]
            HD = C + H
            i = [1, 1, 2, 0][q]

            def finish(g, u):
                r = row[u]
                es, ed, m = (r[:, HD + k * H:HD + (k + 1) * H] for k in range(3))
                s1, s2 = norms[u][:, 12:12 + H], small[u][:, 60:60 + H]
                wait(e, "rows_sb", g, u)
                inc(e.tensor_copy(r[:, HD + 3 * H:HD + 3 * H + 1], col(loops[i], g, u)), "row_count")
                inc(e.tensor_tensor(s1, es, ed, ALU.add), "row_s1")
                wait(e, "row_s1", g, u)
                inc(e.tensor_scalar(s2, s1, 0.0, 1.0 - SLOPE, ALU.max, ALU.mult), "row_s2")
                inc(e.tensor_scalar(m, s1, SLOPE, None, ALU.mult), "row_s2")
                wait(e, "row_s2", g, u, scale=2)
                inc(e.tensor_tensor(s2, s2, m, ALU.add), "row_s3")
                wait(e, "row_s3", g, u)
                inc(e.tensor_tensor(m, s2, col(gone[i], g, u).to_broadcast([P, H]), ALU.add), "row_done")
            return finish

        def fresh_rows(e):
            for u in range(NB):
                e.memset(row[u][:], 1.0).then_inc(sem("rows_fresh"), 1)
            stands["rows_fresh"] = stands.get("rows_fresh", 0) + NB

        TAIL = ["n_stats", "n_mv", "n_ve", "n_shift", "n_rstd", "v", "x_normed"]
        ROWS = ["xT_sb", "rows_sb", "x_turned", "rows_mm", "row_count", "row_s1", "row_s2", "row_s2", "row_s3", "row_done"]

        with nc.Block() as block:
            @block.gpsimd
            def _(e):
                fresh_rows(e)

        with nc.Block() as block:
            @block.sync
            def _(e):
                def load(g, u):
                    wait(e, "b_mul", g, u, 8)
                    inc_dma(e.dma_start(own[u][:, 0:C], rows_of(h_dram, g, u)), "own_in", u)
                    wait(e, "v", g, u, 8)
                    inc_dma(e.dma_start(res[u][:], rows_of(x_in, g, u)), "res_in", u)

                def store_x(g, u):
                    wait(e, "x_normed", g, u)
                    inc_dma(e.dma_start(rows_of(x1_dram, g, u), xn[u][:]), "xn_out", u)

                def store_rows(g, u):
                    wait(e, "row_done", g, u)
                    inc_dma(e.dma_start(rows_of(rows_dram[0], g, u), row[u][:, 0:row_w[0]]), "rows_out", u)
                skewed(e, [(0, load), (5, store_x), (7, store_rows)], True)
                for u in range(NB):
                    e.wait_ge(sem(f"xn_out{u}"), upto("xn_out", 16 * G))
                    e.wait_ge(sem(f"rows_out{u}"), upto("rows_out", 16 * G))

            @block.gpsimd
            def _(e):
                def plus_shift(g, u):
                    wait_dma(e, "res_in", g, u)
                    wait(e, "v", g, u, 8)
                    inc(e.tensor_tensor(wide[u][:, 0:C], res[u][:], bn_add[:], ALU.add), "b_xs")
                skewed(e, [(6, pool_rows(e, 0)), (2, pool_rstd(e)), (0, plus_shift)], True)

            @block.vector
            def _(e):
                stats, aggr, add_eps, shift = dve_stats(e)

                def mul(g, u):
                    wait_dma(e, "own_in", g, u)
                    wait(e, "v", g, u, 8)
                    inc(e.tensor_tensor(mess[u][:, 0:C], own[u][:, 0:C], bn_mul[:], ALU.mult), "b_mul")

                def add(g, u):
                    wait(e, "b_mul", g, u)
                    wait(e, "b_xs", g, u)
                    wait(e, "x_normed", g, u, 8)
                    inc(e.tensor_tensor(conv[u][:], mess[u][:, 0:C], wide[u][:, 0:C], ALU.add), "v")
                skewed(e, [(2, aggr), (1, add), (2, add_eps), (0, mul), (1, stats), (3, shift)], True)

            @block.scalar
            def _(e):
                norm, evac_xT, evac_rows = act_tail(e, True, 0, False)
                skewed(e, [(2, evac_rows), (1, evac_xT), (0, norm)], True)

            @block.tensor
            def _(e):
                turn, rows = pe_tail(e, 0)
                skewed(e, [(1, rows), (0, turn)], True)
        pass_over(TAIL + ROWS + ["b_mul", "b_xs"], ["own_in", "res_in", "xn_out", "rows_out"])

        def gat(q, key, kind, res_dram, xn_dram, nxt):
            H = heads[q]
            D, HD, W = C // H, C + H, row_w[q]
            overflow(q, key, rows_dram[q], rows_dram[q], state_dram[q], H)
            if nxt is not None:
                with nc.Block() as block:
                    @block.gpsimd
                    def _(e):
                        fresh_rows(e)
            ps_c = [bank[0], bank[1]]
            turned_hot = bank[2][:, 0:P]
            ps_a = bank[4]

            def edge_cols(i):
                return bank[3][:, 4 * i:4 * i + H]

            with nc.Block() as block:
                @block.sync
                def _(e):
                    nf = further_of(e, key)

                    def load(g, u):
                        wait(e, "sums", g, u, 8, settle=True)
                        with e.If(nf > 0):
                            inc_dma(e.dma_start(own[u][:, 0:W], rows_of(state_dram[q], g, u)), "own_in", u)
                        with e.Else():
                            inc_dma(e.dma_start(own[u][:, 0:W], rows_of(rows_dram[q], g, u)), "own_in", u)

                    def load_res(g, u):
                        wait(e, "v", g, u, 8)
                        inc_dma(e.dma_start(res[u][:], rows_of(res_dram, g, u)), "res_in", u)

                    def store_x(g, u):
                        wait(e, "x_normed", g, u)
                        inc_dma(e.dma_start(rows_of(xn_dram, g, u), xn[u][:]), "xn_out", u)

                    def store_rows(g, u):
                        wait(e, "row_done", g, u)
                        inc_dma(e.dma_start(rows_of(rows_dram[nxt], g, u), row[u][:, 0:row_w[nxt]]), "rows_out", u)
                    st = [(0, load)]
                    if res_dram is not None:
                        st.append((2, load_res))
                    if xn_dram is not None:
                        st.append((9, store_x))
                    if nxt is not None:
                        st.append((11, store_rows))
                    skewed(e, st, q == 0)
                    for u in range(NB):
                        if xn_dram is not None:
                            e.wait_ge(sem(f"xn_out{u}"), upto("xn_out", 16 * G))
                        if nxt is not None:
                            e.wait_ge(sem(f"rows_out{u}"), upto("rows_out", 16 * G))

                @block.gpsimd
                def _(e):
                    def gather(g, u):
                        wait(e, "sums", g, u, 8)
                        inc(e.tensor_copy(ix[u][:], col(tab_idx[key], g, u)), "ix_made")
                        wait(e, "ix_made", g, u)
                        inc_dma(e.indirect_dma_start(got[u][:, 0:W], None, rows_dram[q],
                                                     bass.IndirectOffsetOnAxis(ap=ix[u][:], axis=0)), "got_in", u)

                    def own_weight(g, u):
                        wait(e, "w_own", g, u)
                        inc(e.tensor_tensor(S(u, S_WC, H), S(u, S_WI, H),
                                            own[u][:, W - 1:W].to_broadcast([P, H]), ALU.mult), "wc")

                    def own_part(g, u):
                        wait(e, "wc", g, u)
                        inc(e.tensor_tensor(heads_of(wide[u][:, 0:HD], H), heads_of(own[u][:, 0:HD], H),
                                            over(S(u, S_WC, H), H, D + 1), ALU.mult), "own_part")

                    def res_bias(g, u):
                        wait_dma(e, "res_in", g, u)
                        inc(e.tensor_tensor(res[u][:], res[u][:], bias_bc[q][:], ALU.add), "res_bias")
                    st = []
                    if nxt is not None:
                        st.append((11, pool_rows(e, nxt)))
                    st += [(8, pool_rstd(e)), (5, own_weight)]
                    if kind == "residual":
                        st.append((5, res_bias))
                    st += [(5, own_part), (0, gather)]
                    skewed(e, st, q == 0)

                @block.vector
                def _(e):
                    stats, aggr, add_eps, shift = dve_stats(e)

                    def onehot(g, u):
                        inc(e.tensor_scalar(hot[u][:], iota_n[:], col(tab_loc[key], g, u), None, ALU.is_equal), "hot")

                    def maxima(g, u):
                        wait(e, "turned", g, u)
                        inc(e.tensor_reduce(S(u, S_S, H), ps_c[u % 2][:, 0:H * P].rearrange("p (h e) -> p h e", h=H),
                                            axis=AX, op=ALU.max), "m0")

                    def max_ed(g, u):
                        wait(e, "m0", g, u)
                        wait_dma(e, "own_in", g, u)
                        inc(e.tensor_tensor(S(u, S_S, H), S(u, S_S, H), own[u][:, HD + H:HD + 2 * H], ALU.add), "m1")

                    def max_leaky(g, u):
                        wait(e, "m1", g, u)
                        inc(e.scalar_tensor_tensor(out=S(u, S_LK, H), in0=S(u, S_S, H), scalar=SLOPE, in1=S(u, S_S, H),
                                                   op0=ALU.mult, op1=ALU.max), "m2")

                    def max_own(g, u):
                        wait(e, "m2", g, u)
                        inc(e.tensor_tensor(S(u, S_MN, H), S(u, S_LK, H), own[u][:, HD + 2 * H:HD + 3 * H], ALU.max),
                            "m3")

                    def own_diff(g, u):
                        wait(e, "m3", g, u)
                        inc(e.tensor_tensor(S(u, S_DF, H), own[u][:, HD + 2 * H:HD + 3 * H], S(u, S_MN, H),
                                            ALU.subtract), "m4")

                    def edge_sum(g, u):
                        wait(e, "edge_cols", g, u)
                        inc(e.tensor_tensor(S(u, S_A, H), got[u][:, HD:HD + H], edge_cols(0), ALU.add), "z1")

                    def edge_leaky(g, u):
                        wait(e, "z1", g, u)
                        inc(e.scalar_tensor_tensor(out=S(u, S_A2, H), in0=S(u, S_A, H), scalar=SLOPE, in1=S(u, S_A, H),
                                                   op0=ALU.mult, op1=ALU.max), "z2")

                    def edge_diff(g, u):
                        wait(e, "z2", g, u)
                        inc(e.tensor_tensor(S(u, S_Z, H), S(u, S_A2, H), edge_cols(1), ALU.subtract), "z3")

                    def messages(g, u):
                        wait(e, "w_edge", g, u)
                        inc(e.scalar_tensor_tensor(out=heads_of(mess[u][:, 0:HD], H), in0=over(S(u, S_W, H), H, D + 1),
                                                   scalar=1.0, in1=heads_of(got[u][:, 0:HD], H),
                                                   op0=ALU.min, op1=ALU.mult), "mess")

                    def sums(g, u):
                        wait(e, "own_part", g, u)
                        wait(e, "edge_sums", g, u)
                        inc(e.tensor_tensor(wide[u][:, 0:HD], wide[u][:, 0:HD], ps_a[:, 0:HD], ALU.add), "sums")

                    def guard(g, u):
                        wait(e, "sums", g, u)
                        den = heads_of(wide[u][:, 0:HD], H)[:, :, D]
                        if q == 2:
                            inc(e.tensor_scalar(S(u, S_DG, H), den, 1e-16, None, ALU.add), "r1")
                        else:
                            inc(e.tensor_scalar(S(u, S_DG, H), den, 1e-16, None, ALU.max), "r1")

                    def recip(g, u):
                        wait(e, "r1", g, u)
                        inc(e.reciprocal(S(u, S_RD, H), S(u, S_DG, H)), "r2")

                    def plus(g, u):
                        wait(e, "scaled", g, u)
                        if kind == "relu_norm":
                            inc(e.tensor_tensor(conv[u][:], conv[u][:], bias_bc[q][:], ALU.add), "v")
                        elif kind == "residual":
                            wait(e, "res_bias", g, u)
                            inc(e.tensor_tensor(conv[u][:], conv[u][:], res[u][:], ALU.add), "v")
                        else:
                            inc(e.tensor_tensor(conv[u][:], conv[u][:], bias_bc[q][:], ALU.add), "v0")

                    def relu_plus(g, u):
                        wait(e, "v0", g, u)
                        wait_dma(e, "res_in", g, u)
                        inc(e.scalar_tensor_tensor(out=conv[u][:], in0=conv[u][:], scalar=0.0, in1=res[u][:],
                                                   op0=ALU.max, op1=ALU.add), "v")
                    st = [(3, edge_sum), (4, sums), (3, edge_leaky), (5, plus), (3, edge_diff), (4, guard),
                          (2, maxima), (4, recip)]
                    if kind == "relu_residual":
                        st.append((5, relu_plus))
                    st += [(2, max_ed), (5, stats), (2, max_leaky), (0, onehot), (2, max_own), (5, aggr),
                           (3, messages), (2, own_diff), (5, add_eps), (6, shift)]
                    skewed(e, st, q == 0)

                @block.scalar
                def _(e):
                    norm, evac_xT, evac_rows = act_tail(e, xn_dram is not None, nxt, kind == "relu_norm")

                    def offsets(g, u):
                        wait(e, "hot", g, u)
                        wait(e, "turned", g, u, 4)
                        inc(e.activation(off[u % 4][:], hot[u][:], ACT.Copy, scale=FAR, bias=-FAR), "off")

                    def candidates(g, u):
                        wait(e, "off", g, u)
                        wait_dma(e, "got_in", g, u)
                        wait(e, "turned", g, u, 4)
                        for h in range(H):
                            last = e.activation(cand[u % 4][:, h, :], off[u % 4][:], ACT.Identity,
                                                bias=got[u][:, HD + h:HD + h + 1])
                        inc(last, "cand")

                    def evac_hot(g, u):
                        wait(e, "turned", g, u)
                        inc(e.activation(hotT[u][:], turned_hot, ACT.Copy), "hotT")

                    def exp_own(g, u):
                        wait(e, "m4", g, u)
                        inc(e.activation(S(u, S_WI, H), S(u, S_DF, H), ACT.Exp), "w_own")

                    def exp_edge(g, u):
                        wait(e, "z3", g, u)
                        inc(e.activation(S(u, S_W, H), S(u, S_Z, H), ACT.Exp), "w_edge")

                    def scale(g, u):
                        wait(e, "r2", g, u)
                        wait(e, "x_normed", g, u, 8)
                        for h in range(H):
                            last = e.activation(conv[u][:, h * D:(h + 1) * D],
                                                wide[u][:, h * (D + 1):h * (D + 1) + D], ACT.Copy,
                                                scale=S(u, S_RD, H)[:, h:h + 1])
                        inc(last, "scaled")
                    st = []
                    if nxt is not None:
                        st += [(8, evac_rows), (7, evac_xT)]
                    st += [(3, exp_edge), (6, norm), (2, evac_hot), (4, scale), (2, exp_own),
                           (1, candidates), (0, offsets)]
                    skewed(e, st, q == 0)

                @block.tensor
                def _(e):
                    turn, rows = pe_tail(e, nxt)

                    def turn_cand(g, u):
                        wait(e, "cand", g, u)
                        wait(e, "m0", g, u, 2)
                        wait(e, "hotT", g, u, 1)
                        for h in range(H):
                            e.transpose(ps_c[u % 2][:, h * P:(h + 1) * P], cand[u % 4][:, h, :], ident[:])
                        inc(e.transpose(turned_hot, hot[u][:], ident[:]), "turned")

                    def to_edges(g, u):
                        wait(e, "hotT", g, u)
                        wait(e, "m3", g, u)
                        wait(e, "z3", g, u, 1)
                        e.matmul(edge_cols(0), hotT[u][:], own[u][:, HD + H:HD + 2 * H], start=True, stop=True)
                        inc(e.matmul(edge_cols(1), hotT[u][:], S(u, S_MN, H), start=True, stop=True), "edge_cols")

                    def to_nodes(g, u):
                        wait(e, "mess", g, u)
                        wait(e, "sums", g, u, 1)
                        inc(e.matmul(ps_a[:, 0:HD], hot[u][:], mess[u][:, 0:HD], start=True, stop=True),
                            "edge_sums")
                    st = []
                    if nxt is not None:
                        st += [(6, rows)]
                    st += [(1, to_edges)]
                    if nxt is not None:
                        st += [(5, turn)]
                    st += [(2, to_nodes), (0, turn_cand)]
                    skewed(e, st, q == 0)

            steps = TAIL + ["ix_made", "wc", "own_part", "hot", "m0", "m1", "m2", "m3", "m4", "z1", "z2", "z3", "mess",
                            "sums", "r1", "r2", "off", "cand", "hotT", "w_own", "w_edge", "scaled", "turned",
                            "edge_cols", "edge_sums"]
            dmas = ["own_in", "got_in"]
            if kind == "residual":
                steps.append("res_bias")
            if kind == "relu_residual":
                steps.append("v0")
            if res_dram is not None:
                dmas.append("res_in")
            if xn_dram is not None:
                dmas.append("xn_out")
            if nxt is not None:
                steps += ROWS
                dmas.append("rows_out")
            pass_over(steps, dmas)

        gat(0, 0, "relu_norm", None, None, 1)
        gat(1, 0, "residual", x1_dram, x2_dram, 2)
        gat(2, 0, "relu_residual", x2_dram, x3_dram, 3)
        gat(3, 1, "residual", x3_dram, out, None)


_NAMES = ['x', 'src', 'dst', 'L0_gnn_eps', 'L0_gnn_W1', 'L0_gnn_b1', 'L0_gnn_W2', 'L0_gnn_b2', 'L0_gnn_gamma',
          'L0_gnn_beta', 'L1_gnn_W1', 'L1_gnn_a1_src', 'L1_gnn_a1_dst', 'L1_gnn_b1', 'L1_gnn_ln_g', 'L1_gnn_ln_b',
          'L1_gnn_W2', 'L1_gnn_a2_src', 'L1_gnn_a2_dst', 'L1_gnn_b2', 'L2_gnn_W', 'L2_gnn_att_src', 'L2_gnn_att_dst',
          'L2_gnn_bias', 'L3_gnn_weight', 'L3_gnn_att_src', 'L3_gnn_att_dst', 'L3_gnn_bias']


def kernel(_n_loops=20000, **inputs):
    import numpy as _np
    import concourse.bacc as _bacc
    from concourse import mybir as _mybir
    from concourse.bass_utils import run_bass_kernel_spmd as _run

    arrays = {n: _np.ascontiguousarray(inputs[n]) for n in _NAMES}
    n_nodes = arrays["x"].shape[0]
    n_pad = -(-(n_nodes + 1) // (P * NB)) * (P * NB)
    x = _np.zeros((n_pad, C), arrays["x"].dtype)
    x[:n_nodes] = arrays["x"]
    arrays["x"] = x
    for n in ("src", "dst"):
        e = arrays[n]
        padded = _np.full(-(-e.shape[0] // (2 * P)) * (2 * P), n_nodes, e.dtype)
        padded[:e.shape[0]] = e
        arrays[n] = padded

    nc = _bacc.Bacc("TRN2", target_bir_lowering=False, num_devices=1)
    aps = {n: nc.dram_tensor(n, v.shape, _mybir.dt.from_np(v.dtype), kind="ExternalInput").ap()
           for n, v in arrays.items()}
    out = nc.dram_tensor("out", (n_pad, C), _mybir.dt.float32, kind="ExternalOutput").ap()
    graph_layers(nc, aps, out, n_nodes, _n_loops)
    r = _run(nc, [arrays], core_ids=[0])
    return r.results[0]["out"][:n_nodes]
```

```python
import concourse.bass as bass
from concourse import mybir
from contextlib import ExitStack

F32 = mybir.dt.float32
F16 = mybir.dt.float16
BF16 = mybir.dt.bfloat16
I32 = mybir.dt.int32
ALU = mybir.AluOpType
ACT = mybir.ActivationFunctionType
AX = mybir.AxisListType.X

P = 128
C = 256
KC = C // P
HID = 2 * C
FC = HID // P
NB = 8
EB = 4
EPS = 1e-5
FAR = 1e30
SLOPE = 0.2


def graph_layers(nc, a, out, n_nodes, n_loops):
    NP = a["x"].shape[0]
    T = NP // P
    G = T // NB
    J = a["src"].shape[0] // P
    LEVELS = (J * P) // P + 1
    assert T % NB == 0 and G >= 3 and J % EB == 0 and J > EB and T <= 512
    x_in = a["x"]

    def dram(name, rows, cols):
        return nc.dram_tensor(name, (rows, cols), F32).ap()

    RWMAX = C + 4 + 3 * 4 + 1
    h_dram = dram("h_dram", NP, C)
    x1_dram = dram("x1_dram", NP, C)
    x2_dram = dram("x2_dram", NP, C)
    x3_dram = dram("x3_dram", NP, C)
    heads = [4, 1, 4, 4]
    row_w = [C + 4 * h + 1 for h in heads]
    LOOPS_OF = [1, 1, 2, 0]
    rows_dram = [dram(f"rows{q}_dram", NP, row_w[q]) for q in range(4)]
    state_dram = [dram(f"state{q}_dram", NP, row_w[q]) for q in range(4)]
    xstate_dram = dram("xstate_dram", NP, C)
    table_dram = [dram(f"table{k}_dram", LEVELS * P, T) for k in range(2)]

    ctx = ExitStack()
    with ctx:
        def sb(name, shape, dt=F32):
            return ctx.enter_context(nc.sbuf_tensor(name, shape, dt))

        def bufs(name, shape, dt=F32, n=NB):
            return [sb(f"{name}{i}", shape, dt) for i in range(n)]

        sems = {}

        def sem(name):
            if name not in sems:
                sems[name] = ctx.enter_context(nc.semaphore(name))
            return sems[name]

        ident = sb("ident", [P, P])
        iota_n = sb("iota_n", [P, P])
        iota_t = sb("iota_t", [P, T], F16)
        before = sb("before", [P, P], F16)
        not_before = sb("not_before", [P, P], F16)
        ones16 = sb("ones16", [P, P], F16)
        ones = sb("ones", [P, P])
        minus_half = sb("minus_half", [P, 1])
        tab_idx = [sb(f"tab_idx{k}", [P, T], I32) for k in range(2)]
        tab_loc = [sb(f"tab_loc{k}", [P, T]) for k in range(2)]
        loops = [sb(f"loops{i}", [P, T]) for i in range(3)]
        gone = [sb(f"gone{i}", [P, T]) for i in range(3)]
        valid = sb("valid", [P, T])
        fac = sb("fac", [P, T])
        n_levels = sb("n_levels", [P, 2], I32)
        n_further = sb("n_further", [P, 2], I32)
        W1 = sb("W1", [P, KC, HID])
        W2 = sb("W2", [P, FC, C])
        b1_col = sb("b1_col", [P, FC])
        b2_bc = sb("b2_bc", [P, C])
        WG = [sb(f"WG{q}", [P, KC, C + 2 * heads[q]]) for q in range(4)]
        bias_bc = [sb(f"bias_bc{q}", [P, C]) for q in range(4)]
        gam_bc = sb("gam_bc", [P, C])
        bet_bc = sb("bet_bc", [P, C])
        lng_col = sb("lng_col", [P, KC])
        lnb_col = sb("lnb_col", [P, KC])
        sum_h = sb("sum_h", [P, C])
        sum_hh = sb("sum_hh", [P, C])

        bank = [ctx.enter_context(nc.psum_tensor(f"bank{i}", [P, 512], F32)) for i in range(8)]

        stands = {}

        def upto(name, n):
            return stands.get(name, 0) + n

        def settled(e):
            e.sem_inc(sem("settled"), 1)

        def wait(e, name, g, u, back=0, scale=1, settle=False):
            n = (g * NB + u + 1 - back) * scale
            if isinstance(n, int) and n <= 0:
                return
            e.wait_ge(sem(name), n + stands.get(name, 0))
            if settle or e.engine == nc.gpsimd.engine:
                settled(e)

        def wait_dma(e, name, g, u, back=0):
            n = g + 1 - back
            if isinstance(n, int) and n <= 0:
                return
            e.wait_ge(sem(f"{name}{u}"), n * 16 + stands.get(name, 0))
            if e.engine == nc.gpsimd.engine:
                settled(e)

        def clear(prefix):
            with nc.Block() as block:
                @block.gpsimd
                def _(e):
                    for name in sorted(sems):
                        if name.startswith(prefix):
                            e.sem_clear(sems[name])

        def inc(ins, name):
            ins.then_inc(sem(name), 1)

        def inc_dma(ins, name, u):
            ins.then_inc(sem(f"{name}{u}"), 16)

        def pass_over(steps, dmas):
            for name in steps:
                stands[name] = stands.get(name, 0) + T
            for name in dmas:
                stands[name] = stands.get(name, 0) + 16 * G

        def skewed(e, stages, fresh=False):
            deepest = max(d for d, _ in stages)
            first = max(1, -(-(deepest + NB * fresh) // NB))
            for s in range(first * NB):
                for d, f in stages:
                    if s >= d:
                        f((s - d) // NB, (s - d) % NB)
            with e.Fori(first, G) as g:
                for u in range(NB):
                    for d, f in stages:
                        f(g + (u - d) // NB, (u - d) % NB)
            for s in range(T, T + deepest):
                for d, f in stages:
                    if s - d < T:
                        f((s - d) // NB, (s - d) % NB)

        def rows_of(dr, g, u):
            return dr[bass.ds((g * NB + u) * P, P), :]

        def col(t_sb, g, u):
            return t_sb[:, bass.ds(g * NB + u, 1)]

        prep = ExitStack()
        with prep:
            def pb(name, shape, dt=F32):
                return prep.enter_context(nc.sbuf_tensor(name, shape, dt))

            src_i = pb("src_i", [P, J], I32)
            dst_i = pb("dst_i", [P, J], I32)
            src_f = pb("src_f", [P, J])
            dst_f = pb("dst_f", [P, J])
            other = pb("other", [P, J])
            itself = pb("itself", [P, J])
            tmp_i = pb("tmp_i", [P, J], I32)
            tmp_f = pb("tmp_f", [P, J])
            code = pb("code", [P, J])
            code_i = pb("code_i", [P, J], I32)
            dst_loc = pb("dst_loc", [P, J])
            dst_tile = pb("dst_tile", [P, J])
            tile_of = [pb(f"tile_of{k}", [P, J]) for k in range(2)]
            piece = [[pb(f"piece{k}{i}", [P, J]) for i in range(3)] for k in range(2)]
            rank = [pb(f"rank{k}", [P, J]) for k in range(2)]
            level_rank = pb("level_rank", [P, J])
            hit = [pb(f"hit{i}", [P, T], F16) for i in range(EB)]
            picked = [pb(f"picked{i}", [P, T]) for i in range(EB)]
            slot_f = [pb(f"slot_f{i}", [P, P]) for i in range(EB)]
            slot = [[pb(f"slot{i}{k}", [P, P], BF16) for k in range(3)] for i in range(EB)]
            self_loc = [pb(f"self_loc{i}", [P, P], BF16) for i in range(EB)]
            counts = pb("counts", [P, T])
            most = pb("most", [P, 2])
            tab_f = pb("tab_f", [P, T])
            tab_c = pb("tab_c", [P, T], I32)
            tab_d = pb("tab_d", [P, 1], I32)
            node_i = pb("node_i", [P, T], I32)
            node_f = pb("node_f", [P, T])
            iota_i = pb("iota_i", [P, max(T, P)], I32)
            eps_bc = pb("eps_bc", [P, 1])
            att_bc = [[pb(f"att_bc{q}{i}", [P, C]) for i in range(2)] for q in range(4)]
            prod = pb("prod", [P, C])

            gat_w = [a["L1_gnn_W1"], a["L1_gnn_W2"], a["L2_gnn_W"], None]
            gat_b = [a["L1_gnn_b1"], a["L1_gnn_b2"], a["L2_gnn_bias"], a["L3_gnn_bias"]]
            gat_a = [(a["L1_gnn_a1_src"], a["L1_gnn_a1_dst"]), (a["L1_gnn_a2_src"], a["L1_gnn_a2_dst"]),
                     (a["L2_gnn_att_src"], a["L2_gnn_att_dst"]), (a["L3_gnn_att_dst"], a["L3_gnn_att_src"])]

            def bcast(v):
                if len(v.shape) == 3:
                    v = v.rearrange("a h c -> (a h c)")
                elif len(v.shape) == 2:
                    v = v.rearrange("h c -> (h c)")
                return v.partition_broadcast(P)

            with nc.Block() as block:
                @block.sync
                def _(e):
                    e.dma_start(src_i[:], a["src"].rearrange("(p j) -> p j", p=P)).then_inc(sem("edges_in"), 16)
                    e.dma_start(dst_i[:], a["dst"].rearrange("(p j) -> p j", p=P)).then_inc(sem("edges_in"), 16)
                    n = 0
                    for dst, s in ([(W1[:], a["L0_gnn_W1"].rearrange("(k p) n -> p k n", p=P)),
                                    (W2[:], a["L0_gnn_W2"].rearrange("(k p) n -> p k n", p=P)),
                                    (b2_bc[:], bcast(a["L0_gnn_b2"])), (gam_bc[:], bcast(a["L0_gnn_gamma"])),
                                    (bet_bc[:], bcast(a["L0_gnn_beta"])), (eps_bc[:], bcast(a["L0_gnn_eps"]))]
                                   + [(bias_bc[q][:], bcast(gat_b[q])) for q in range(4)]
                                   + [(att_bc[q][i][:], bcast(gat_a[q][i])) for q in range(4) for i in range(2)]
                                   + [(WG[q][:, :, 0:C], gat_w[q].rearrange("(k p) n -> p k n", p=P)) for q in range(3)]
                                   + [(WG[3][:, k, 0:C].rearrange("p (h c) -> p h c", h=4),
                                       a["L3_gnn_weight"][:, k * P:(k + 1) * P, :].rearrange("h p c -> p h c"))
                                      for k in range(KC)]):
                        e.dma_start(dst, s).then_inc(sem("weights_in"), 16)
                        n += 16
                    with nc.allow_non_contiguous_dma("a few columns of 128"):
                        for dst, s in [(b1_col[:], a["L0_gnn_b1"].rearrange("(k p) -> p k", p=P)),
                                       (lng_col[:], a["L1_gnn_ln_g"].rearrange("(k p) -> p k", p=P)),
                                       (lnb_col[:], a["L1_gnn_ln_b"].rearrange("(k p) -> p k", p=P))]:
                            e.dma_start(dst, s).then_inc(sem("weights_in"), 16)
                            n += 16
                    e.wait_ge(sem("edges_in"), 32)
                    e.wait_ge(sem("weights_in"), n)

                @block.gpsimd
                def _(e):
                    e.memset(ident[:], 0.0).then_inc(sem("consts"), 1)
                    e.memset(ones[:], 1.0).then_inc(sem("consts"), 1)
                    e.memset(ones16[:], 1.0).then_inc(sem("consts"), 1)
                    e.memset(minus_half[:], -0.5).then_inc(sem("consts"), 1)
                    e.memset(sum_h[:], 0.0).then_inc(sem("consts"), 1)
                    e.memset(sum_hh[:], 0.0).then_inc(sem("consts"), 1)
                    e.iota(iota_i[:], pattern=[[1, max(T, P)]], base=0, channel_multiplier=0).then_inc(sem("consts"), 1)
                    e.iota(node_i[:], pattern=[[P, T]], base=0, channel_multiplier=1).then_inc(sem("consts"), 1)
                    e.wait_ge(sem("consts"), 8)
                    e.affine_select(out=ident[:], in_=ident[:], compare_op=ALU.not_equal, fill=1.0,
                                    base=0, pattern=[[-1, P]], channel_multiplier=1).then_inc(sem("consts"), 1)
                    e.affine_select(out=before[:], in_=ones16[:], compare_op=ALU.is_ge, fill=0.0,
                                    base=-1, pattern=[[1, P]], channel_multiplier=-1).then_inc(sem("consts"), 1)
                    e.affine_select(out=not_before[:], in_=ones16[:], compare_op=ALU.is_ge, fill=0.0,
                                    base=0, pattern=[[-1, P]], channel_multiplier=1).then_inc(sem("consts"), 1)

            with nc.Block() as block:
                @block.vector
                def _(e):
                    k = [0]

                    def link(ins):
                        k[0] += 1
                        ins.then_inc(sem("dve_setup"), 1)
                        e.wait_ge(sem("dve_setup"), k[0])

                    link(e.tensor_copy(iota_t[:], iota_i[:, 0:T]))
                    link(e.tensor_copy(iota_n[:], iota_i[:, 0:P]))
                    link(e.tensor_copy(node_f[:], node_i[:]))
                    link(e.tensor_scalar(valid[:], node_f[:], float(n_nodes), None, ALU.is_lt))
                    link(e.tensor_scalar(loops[1][:], node_f[:], float(n_loops), None, ALU.is_lt))
                    link(e.tensor_copy(src_f[:], src_i[:]))
                    link(e.tensor_copy(dst_f[:], dst_i[:]))
                    link(e.tensor_tensor(other[:], src_f[:], dst_f[:], ALU.not_equal))
                    link(e.tensor_tensor(itself[:], src_f[:], dst_f[:], ALU.is_equal))
                    for key, own, far in ((0, dst_i, src_f), (1, src_i, dst_f)):
                        link(e.tensor_scalar(tmp_i[:], own[:], 127, None, ALU.bitwise_and))
                        link(e.tensor_copy(tmp_f[:], tmp_i[:]))
                        if key == 0:
                            link(e.tensor_copy(dst_loc[:], tmp_f[:]))
                        link(e.scalar_tensor_tensor(out=code[:], in0=far[:], scalar=256.0, in1=tmp_f[:],
                                                    op0=ALU.mult, op1=ALU.add))
                        link(e.scalar_tensor_tensor(out=code[:], in0=code[:], scalar=1.0, in1=other[:],
                                                    op0=ALU.add, op1=ALU.mult))
                        link(e.tensor_copy(code_i[:], code[:]))
                        for i in range(3):
                            link(e.tensor_scalar(tmp_i[:], code_i[:], 0xFF << (8 * i), None, ALU.bitwise_and))
                            link(e.tensor_copy(piece[key][i][:], tmp_i[:]))
                        link(e.tensor_scalar(tmp_i[:], own[:], 7, None, ALU.logical_shift_right))
                        link(e.tensor_copy(tmp_f[:], tmp_i[:]))
                        if key == 0:
                            link(e.tensor_copy(dst_tile[:], tmp_f[:]))
                        link(e.scalar_tensor_tensor(out=tile_of[key][:], in0=itself[:], scalar=1024.0, in1=tmp_f[:],
                                                    op0=ALU.mult, op1=ALU.add))
                    for q in range(4):
                        H = heads[q]
                        for i in range(2):
                            for kc in range(KC):
                                link(e.tensor_tensor(prod[:], WG[q][:, kc, 0:C], att_bc[q][i][:], ALU.mult))
                                link(e.tensor_reduce(WG[q][:, kc, C + i * H:C + (i + 1) * H],
                                                     prod[:].rearrange("p (h c) -> p h c", h=H),
                                                     axis=AX, op=ALU.add))

            for key in range(2):
                with nc.Block() as block:
                    @block.vector
                    def _(e):
                        def mark(r, u):
                            n = r * EB + u
                            if not (isinstance(n, int) and n < EB):
                                e.wait_ge(sem("rk_added"), n - EB + 1)
                            e.tensor_scalar(hit[u][:], iota_t[:], tile_of[key][:, bass.ds(n, 1)], None,
                                            ALU.is_equal).then_inc(sem("rk_hit"), 1)

                        def read(r, u):
                            n = r * EB + u
                            e.wait_ge(sem("rk_hit"), n + 1)
                            e.wait_ge(sem("rk_counted"), n + 1)
                            e.scalar_tensor_tensor(out=picked[u][:], in0=bank[u % 2][:, 0:T], scalar=1.0,
                                                   in1=hit[u][:], op0=ALU.mult, op1=ALU.mult,
                                                   accum_out=rank[key][:, bass.ds(n, 1)])\
                                .then_inc(sem("rk_read"), 1)

                        for u in range(EB):
                            mark(0, u)
                            if u >= 2:
                                read(0, u - 2)
                        with e.Fori(1, J // EB) as r:
                            for u in range(EB):
                                mark(r, u)
                                read(r + (u - 2) // EB, (u - 2) % EB)
                        read(J // EB - 1, EB - 2)
                        read(J // EB - 1, EB - 1)
                        e.wait_ge(sem("rk_added"), J)
                        e.tensor_reduce(most[:, 0:1], bank[0][:, 0:T], axis=AX, op=ALU.max).then_inc(sem("dve_levels"), 1)
                        e.wait_ge(sem("dve_levels"), key * 7 + 1)
                        e.tensor_scalar(most[:, 1:2], most[:, 0:1], 1.0, 127.0, ALU.max, ALU.add)\
                            .then_inc(sem("dve_levels"), 1)
                        e.wait_ge(sem("dve_levels"), key * 7 + 2)
                        e.tensor_copy(tab_c[:, 0:1], most[:, 1:2]).then_inc(sem("dve_levels"), 1)
                        e.tensor_scalar(tab_d[:, 0:1], most[:, 1:2], -128.0, None, ALU.add)\
                            .then_inc(sem("dve_levels"), 1)
                        e.wait_ge(sem("dve_levels"), key * 7 + 4)
                        e.tensor_scalar(n_levels[:, key:key + 1], tab_c[:, 0:1], 7, None, ALU.logical_shift_right)\
                            .then_inc(sem("dve_levels"), 1)
                        e.tensor_scalar(n_further[:, key:key + 1], tab_d[:, 0:1], 7, None, ALU.logical_shift_right)\
                            .then_inc(sem("dve_levels"), 1)
                        e.tensor_copy(level_rank[:], rank[key][:]).then_inc(sem("dve_levels"), 1)

                    @block.tensor
                    def _(e):
                        def add(b, first, second, n):
                            if first is not None:
                                e.wait_ge(sem("rk_read"), n - 1)
                                e.matmul(bank[b][:, 0:T], not_before[:], hit[first][:], start=False, stop=True,
                                         skip_group_check=True).then_inc(sem("rk_added"), 1)
                            if second is not None:
                                e.matmul(bank[b][:, 0:T], ones16[:], hit[second][:], start=first is None, stop=True,
                                         skip_group_check=True)

                        def count(n, u, first=False):
                            e.wait_ge(sem("rk_hit"), n + 1)
                            e.matmul(bank[u % 2][:, 0:T], before[:], hit[u][:], start=first, stop=True,
                                     skip_group_check=True).then_inc(sem("rk_counted"), 1)

                        count(0, 0, True)
                        add(1, None, 0, 1)
                        count(1, 1)
                        for u in range(2, EB):
                            add(u % 2, u - 2, u - 1, u)
                            count(u, u)
                        with e.Fori(1, J // EB) as r:
                            for u in range(EB):
                                n = r * EB + u
                                add(u % 2, (u - 2) % EB, (u - 1) % EB, n)
                                count(n, u)
                        add(0, EB - 2, EB - 1, J)
                        add(1, EB - 1, None, J + 1)

                tile_hit = dst_tile if key == 0 else tile_of[key]
                with nc.Block() as block:
                    def levels(e):
                        return e.value_load(n_levels[0:1, key:key + 1], min_val=1, max_val=LEVELS)

                    @block.vector
                    def _(e):
                        nl = levels(e)
                        e.sem_inc(sem("pl_table_full"), 2)
                        with e.Fori(0, nl) as L:
                            with e.Fori(0, J // EB) as r:
                                for u in range(EB):
                                    j = bass.ds(r * EB + u, 1)
                                    e.wait_ge(sem("pl_placed"), L * J + r * EB + u + 1)
                                    e.tensor_scalar(slot_f[u][:], iota_n[:], level_rank[:, j], None, ALU.is_equal)\
                                        .then_inc(sem("pl_slot"), 1)
                                    if key == 0:
                                        e.tensor_scalar(self_loc[u][:], iota_n[:], dst_loc[:, j], itself[:, j],
                                                        ALU.is_equal, ALU.mult).then_inc(sem("pl_hit"), 1)
                                    e.tensor_scalar(hit[u][:], iota_t[:], tile_hit[:, j], None, ALU.is_equal)\
                                        .then_inc(sem("pl_hit"), 2 - (key == 0))
                            e.wait_ge(sem("pl_placed"), (L + 1) * J + EB)
                            e.wait_ge(sem("pl_table_free"), L + 1)
                            e.tensor_copy(tab_f[:], bank[2][:, 0:T]).then_inc(sem("pl_table_full"), 1)
                            e.tensor_scalar(level_rank[:], level_rank[:], -128.0, None, ALU.add)\
                                .then_inc(sem("pl_table_full"), 1)
                            e.wait_ge(sem("pl_table_full"), (L + 2) * 2)
                            settled(e)
                        if key == 0:
                            e.tensor_copy(loops[0][:], bank[3][:, 0:T]).then_inc(sem("loops_counted"), 1)

                    @block.scalar
                    def _(e):
                        nl = levels(e)
                        with e.Fori(0, nl) as L:
                            with e.Fori(0, J // EB) as r:
                                for u in range(EB):
                                    n = L * J + r * EB + u + 1
                                    e.wait_ge(sem("pl_slot"), n)
                                    for i in range(1, 3):
                                        last = e.activation(slot[u][i][:], slot_f[u][:], ACT.Copy,
                                                            scale=piece[key][i][:, bass.ds(r * EB + u, 1)])
                                    last.then_inc(sem("pl_pieces"), 1)

                    @block.gpsimd
                    def _(e):
                        nl = levels(e)
                        with e.Fori(0, nl) as L:
                            with e.Fori(0, J // EB) as r:
                                for u in range(EB):
                                    e.wait_ge(sem("pl_slot"), L * J + r * EB + u + 1)
                                    settled(e)
                                    e.tensor_tensor(slot[u][0][:], slot_f[u][:],
                                                    piece[key][0][:, bass.ds(r * EB + u, 1)].to_broadcast([P, P]),
                                                    ALU.mult).then_inc(sem("pl_piece0"), 1)

                    @block.tensor
                    def _(e):
                        nl = levels(e)
                        e.sem_inc(sem("pl_placed"), EB)

                        def place(L, r, u, first):
                            n = L * J + r * EB + u + 1
                            e.wait_ge(sem("pl_hit"), n * 2)
                            if key == 0:
                                e.matmul(bank[3][:, 0:T], self_loc[u][:], hit[u][:], start=first, stop=True,
                                         skip_group_check=True)
                            e.wait_ge(sem("pl_pieces"), n)
                            e.wait_ge(sem("pl_piece0"), n)
                            for i in range(3):
                                last = e.matmul(bank[2][:, 0:T], slot[u][i][:], hit[u][:],
                                                start=(first and i == 0), stop=True, skip_group_check=True)
                            last.then_inc(sem("pl_placed"), 1)

                        with e.Fori(0, nl) as L:
                            e.wait_ge(sem("pl_table_full"), L * 2 + 2)
                            for u in range(EB):
                                place(L, 0, u, u == 0)
                            with e.Fori(1, J // EB) as r:
                                for u in range(EB):
                                    place(L, r, u, False)

                    @block.sync
                    def _(e):
                        nl = levels(e)
                        e.sem_inc(sem("pl_table_free"), 1)
                        with e.Fori(0, nl) as L:
                            e.wait_ge(sem("pl_table_full"), L * 2 + 4)
                            e.dma_start(table_dram[key][bass.ds(L * P, P), :], tab_f[:])\
                                .then_inc(sem("pl_table_out"), 16)
                            e.wait_ge(sem("pl_table_out"), L * 16 + 16)
                            e.sem_inc(sem("pl_table_free"), 1)
                clear("rk_")
                clear("pl_")

            def decode(e, link, tab, idx, loc, scratch_i):
                link(e.tensor_copy(scratch_i, tab))
                link(e.tensor_scalar(idx, scratch_i, 8, None, ALU.logical_shift_right))
                link(e.tensor_scalar(scratch_i, scratch_i, 255, None, ALU.bitwise_and))
                link(e.tensor_copy(loc, scratch_i))
                link(e.tensor_scalar(loc, loc, -1.0, None, ALU.add))

            with nc.Block() as block:
                @block.sync
                def _(e):
                    for key in range(2):
                        if key:
                            e.wait_ge(sem("dve_tables"), 5)
                        e.dma_start(tab_f[:], table_dram[key][0:P, :]).then_inc(sem("table_in"), 16)

                @block.vector
                def _(e):
                    k = [0]

                    def link(ins):
                        k[0] += 1
                        ins.then_inc(sem("dve_tables"), 1)
                        e.wait_ge(sem("dve_tables"), k[0])

                    for key in range(2):
                        e.wait_ge(sem("table_in"), 16 * (key + 1))
                        decode(e, link, tab_f[:], tab_idx[key][:], tab_loc[key][:], tab_c[:])
                    link(e.tensor_tensor(loops[1][:], loops[1][:], loops[0][:], ALU.add))
                    link(e.tensor_scalar(loops[2][:], loops[0][:], 1.0, None, ALU.add))
                    for i in range(3):
                        link(e.tensor_scalar(gone[i][:], loops[i][:], 0.0, -FAR, ALU.is_equal, ALU.mult))
                    link(e.tensor_scalar(eps_bc[:], eps_bc[:], 1.0, None, ALU.add))
                    link(e.tensor_scalar(fac[:], loops[0][:], eps_bc[:, 0:1], None, ALU.add))

        ix = bufs("ix", [P, 1], I32)
        own = bufs("own", [P, RWMAX])
        got = bufs("got", [P, RWMAX])
        hot = bufs("hot", [P, P])
        hotT = bufs("hotT", [P, P])
        off = bufs("off", [P, P], n=4)
        cand = bufs("cand", [P, 4, P], n=4)
        small = bufs("small", [P, 16 * 4])
        norms = bufs("norms", [P, 16])
        wide = bufs("wide", [P, C + 4])
        mess = bufs("mess", [P, C + 4])
        conv = bufs("conv", [P, C])
        res = bufs("res", [P, C])
        xn = bufs("xn", [P, C])
        xT = bufs("xT", [P, KC, P])
        row = bufs("row", [P, RWMAX])
        ov_tab = sb("ov_tab", [P, T])
        ov_idx = sb("ov_idx", [P, T], I32)
        ov_loc = sb("ov_loc", [P, T])
        ov_sc = sb("ov_sc", [P, T], I32)

        def S(u, i, H):
            return small[u][:, 4 * i:4 * i + H]
        (S_S, S_LK, S_MN, S_DF, S_WI, S_A, S_A2, S_Z, S_W, S_RD, S_WC, S_DG) = range(12)

        def heads_of(ap, H):
            return ap.rearrange("p (h c) -> p h c", h=H)

        def over(ap, H, n):
            return ap.unsqueeze(2).to_broadcast([P, H, n])

        def further_of(e, key):
            return e.value_load(n_further[0:1, key:key + 1], min_val=0, max_val=LEVELS - 1)

        def overflow(tag, key, table, src_rows, state, H):
            W = src_rows.shape[1]
            D = C // H if H else 0
            HD = C + H
            with nc.Block() as block:
                def when(e, body, level_start=None):
                    nf = further_of(e, key)
                    with e.If(nf > 0):
                        with e.Fori(0, nf) as L:
                            if level_start:
                                level_start(L)
                            with e.Fori(0, T) as t:
                                body(L, t, L * T + t)
                        e.nop()

                def s(name):
                    return sem(f"got_ov{tag}" if name == "got" else f"ov_{name}")

                @block.sync
                def _(e):
                    def level(L):
                        e.dma_start(ov_tab[:], table_dram[key][bass.ds(L * P + P, P), :]).then_inc(s("table"), 16)

                    def body(L, t, g):
                        at = bass.ds(t * P, P)
                        with e.If(L < 1):
                            e.dma_start(own[0][:, 0:W], src_rows[at, :]).then_inc(s("own"), 16)
                        with e.Else():
                            e.dma_start(own[0][:, 0:W], state[at, :]).then_inc(s("own"), 16)
                        e.wait_ge(s("state"), g + 2)
                        e.dma_start(state[at, :], own[0][:, 0:W]).then_inc(s("stored"), 16)
                        e.wait_ge(s("stored"), g * 16 + 16)
                        settled(e)
                    when(e, body, level)

                @block.gpsimd
                def _(e):
                    def body(L, t, g):
                        e.wait_ge(s("decoded"), L * 5 + 5)
                        settled(e)
                        e.wait_ge(s("state"), g + 1)
                        settled(e)
                        e.tensor_copy(ix[0][:], ov_idx[:, bass.ds(t, 1)]).then_inc(s("ix"), 1)
                        e.wait_ge(s("ix"), g + 1)
                        settled(e)
                        e.indirect_dma_start(got[0][:, 0:W], None, table,
                                             bass.IndirectOffsetOnAxis(ap=ix[0][:], axis=0)).then_inc(s("got"), 16)
                    when(e, body)

                @block.vector
                def _(e):
                    e.sem_inc(s("state"), 1)

                    def level(L):
                        e.wait_ge(s("table"), L * 16 + 16)
                        k = [0]

                        def link(ins):
                            k[0] += 1
                            ins.then_inc(s("decoded"), 1)
                            e.wait_ge(s("decoded"), L * 5 + k[0])
                        decode(e, link, ov_tab[:], ov_idx[:], ov_loc[:], ov_sc[:])
                        settled(e)

                    def body(L, t, g):
                        k = [0]
                        n_links = 11 if H else 1

                        def link(ins):
                            k[0] += 1
                            ins.then_inc(s("dve"), 1)
                            e.wait_ge(s("dve"), g * n_links + k[0])

                        e.tensor_scalar(hot[0][:], iota_n[:], ov_loc[:, bass.ds(t, 1)], None, ALU.is_equal)\
                            .then_inc(s("hot"), 1)
                        e.wait_ge(s("own"), (g + 1) * 16)
                        if not H:
                            settled(e)
                            with e.If(L < 1):
                                e.tensor_scalar(own[0][:, 0:C], own[0][:, 0:C], fac[:, bass.ds(t, 1)], None, ALU.mult)\
                                    .then_inc(s("dve"), 1)
                            with e.Else():
                                e.tensor_scalar(own[0][:, 0:C], own[0][:, 0:C], 1.0, None, ALU.mult)\
                                    .then_inc(s("dve"), 1)
                            e.wait_ge(s("dve"), g + 1)
                            e.wait_ge(s("sums"), g + 1)
                            e.tensor_tensor(own[0][:, 0:C], own[0][:, 0:C], bank[2][:, 0:C], ALU.add)\
                                .then_inc(s("state"), 1)
                            return
                        e.wait_ge(s("turned"), g + 1)
                        mx = bank[0][:, 0:H * P].rearrange("p (h e) -> p h e", h=H)
                        es, ed, m = (own[0][:, HD + i * H:HD + (i + 1) * H] for i in range(3))
                        link(e.tensor_reduce(S(0, S_S, H), mx, axis=AX, op=ALU.max))
                        link(e.tensor_tensor(S(0, S_S, H), S(0, S_S, H), ed, ALU.add))
                        link(e.scalar_tensor_tensor(out=S(0, S_LK, H), in0=S(0, S_S, H), scalar=SLOPE, in1=S(0, S_S, H),
                                                    op0=ALU.mult, op1=ALU.max))
                        link(e.tensor_tensor(S(0, S_MN, H), S(0, S_LK, H), m, ALU.max))
                        link(e.tensor_tensor(S(0, S_DF, H), m, S(0, S_MN, H), ALU.subtract))
                        e.wait_ge(s("edge_cols"), g + 1)
                        link(e.tensor_tensor(S(0, S_A, H), got[0][:, HD:HD + H], bank[1][:, P:P + H], ALU.add))
                        link(e.scalar_tensor_tensor(out=S(0, S_A2, H), in0=S(0, S_A, H), scalar=SLOPE, in1=S(0, S_A, H),
                                                    op0=ALU.mult, op1=ALU.max))
                        link(e.tensor_tensor(S(0, S_Z, H), S(0, S_A2, H), bank[1][:, P + 4:P + 4 + H], ALU.subtract))
                        e.wait_ge(s("exps"), (g + 1) * 2)
                        e.scalar_tensor_tensor(out=heads_of(mess[0][:, 0:HD], H), in0=over(S(0, S_W, H), H, D + 1),
                                               scalar=1.0, in1=heads_of(got[0][:, 0:HD], H),
                                               op0=ALU.min, op1=ALU.mult).then_inc(s("mess"), 1)
                        link(e.tensor_scalar(S(0, S_WC, H), S(0, S_WI, H), own[0][:, W - 1:W], None, ALU.mult))
                        link(e.tensor_tensor(heads_of(wide[0][:, 0:HD], H), heads_of(own[0][:, 0:HD], H),
                                             over(S(0, S_WC, H), H, D + 1), ALU.mult))
                        link(e.tensor_copy(m, S(0, S_MN, H)))
                        e.tensor_scalar(own[0][:, W - 1:W], S(0, S_WC, 1), 0.0, 1.0, ALU.mult, ALU.add)\
                            .then_inc(s("count1"), 1)
                        e.wait_ge(s("count1"), g + 1)
                        e.wait_ge(s("sums"), g + 1)
                        e.tensor_tensor(own[0][:, 0:HD], wide[0][:, 0:HD], bank[2][:, 0:HD], ALU.add)\
                            .then_inc(s("state"), 1)
                    when(e, body, level)

                if H:
                    @block.scalar
                    def _(e):
                        def body(L, t, g):
                            e.wait_ge(s("hot"), g + 1)
                            e.activation(off[0][:], hot[0][:], ACT.Copy, scale=FAR, bias=-FAR).then_inc(s("off"), 1)
                            e.wait_ge(s("off"), g + 1)
                            e.wait_ge(s("got"), (g + 1) * 16)
                            for h in range(H):
                                last = e.activation(cand[0][:, h, :], off[0][:], ACT.Identity,
                                                    bias=got[0][:, HD + h:HD + h + 1])
                            last.then_inc(s("cand"), 1)
                            e.wait_ge(s("turned"), g + 1)
                            e.activation(hotT[0][:], bank[1][:, 0:P], ACT.Copy).then_inc(s("hotT"), 1)
                            e.wait_ge(s("dve"), g * 11 + 5)
                            e.activation(S(0, S_WI, H), S(0, S_DF, H), ACT.Exp).then_inc(s("exps"), 1)
                            e.wait_ge(s("dve"), g * 11 + 8)
                            e.activation(S(0, S_W, H), S(0, S_Z, H), ACT.Exp).then_inc(s("exps"), 1)
                        when(e, body)

                @block.tensor
                def _(e):
                    def body(L, t, g):
                        if not H:
                            e.wait_ge(s("hot"), g + 1)
                            e.wait_ge(s("got"), (g + 1) * 16)
                            e.wait_ge(s("state"), g + 1)
                            e.matmul(bank[2][:, 0:C], hot[0][:], got[0][:, 0:C], start=True, stop=True)\
                                .then_inc(s("sums"), 1)
                            return
                        e.wait_ge(s("cand"), g + 1)
                        for h in range(H):
                            e.transpose(bank[0][:, h * P:(h + 1) * P], cand[0][:, h, :], ident[:])
                        e.transpose(bank[1][:, 0:P], hot[0][:], ident[:]).then_inc(s("turned"), 1)
                        e.wait_ge(s("hotT"), g + 1)
                        e.wait_ge(s("dve"), g * 11 + 4)
                        e.matmul(bank[1][:, P:P + H], hotT[0][:], own[0][:, HD + H:HD + 2 * H], start=True, stop=True)
                        e.matmul(bank[1][:, P + 4:P + 4 + H], hotT[0][:], S(0, S_MN, H), start=True, stop=True)\
                            .then_inc(s("edge_cols"), 1)
                        e.wait_ge(s("mess"), g + 1)
                        e.matmul(bank[2][:, 0:HD], hot[0][:], mess[0][:, 0:HD], start=True, stop=True)\
                            .then_inc(s("sums"), 1)
                    when(e, body)

            clear("ov_")

        overflow('x', 0, x_in, x_in, xstate_dram, 0)
        hotd = bufs("hotd", [P, P], n=4)
        hidT = bufs("hidT", [P, FC, P], n=2)
        with nc.Block() as block:
            ps_hT = [bank[0], bank[1]]
            ps_hid = [bank[2], bank[3]]
            ps_out = [bank[4], bank[5]]

            @block.sync
            def _(e):
                nf = further_of(e, 0)

                def load(g, u):
                    wait(e, "a_hT", g, u, 8, settle=True)
                    with e.If(nf > 0):
                        inc_dma(e.dma_start(own[u][:, 0:C], rows_of(xstate_dram, g, u)), "own_in", u)
                    with e.Else():
                        inc_dma(e.dma_start(own[u][:, 0:C], rows_of(x_in, g, u)), "own_in", u)

                def store(g, u):
                    wait(e, "a_out", g, u)
                    inc_dma(e.dma_start(rows_of(h_dram, g, u), conv[u][:]), "conv_out", u)
                skewed(e, [(6, store), (0, load)], True)
                for u in range(NB):
                    e.wait_ge(sem(f"conv_out{u}"), upto("conv_out", 16 * G))

            @block.gpsimd
            def _(e):
                def gather(g, u):
                    wait(e, "a_hT", g, u, 8)
                    inc(e.tensor_copy(ix[u][:], col(tab_idx[0], g, u)), "ix_made")
                    wait(e, "ix_made", g, u)
                    inc_dma(e.indirect_dma_start(got[u][:, 0:C], None, x_in,
                                                 bass.IndirectOffsetOnAxis(ap=ix[u][:], axis=0)), "got_in", u)

                def squares(g, u):
                    wait(e, "a_sq", g, u)
                    wait(e, "a_sum_hh", g, u, 1)
                    inc(e.tensor_tensor(sum_hh[:], sum_hh[:], xn[u][:], ALU.add), "a_sum_hh")

                def plus_b2(g, u):
                    wait(e, "a_z", g, u)
                    wait_dma(e, "conv_out", g, u, 1)
                    inc(e.tensor_tensor(conv[u][:], mess[u][:, 0:C], b2_bc[:], ALU.add), "a_out")
                skewed(e, [(6, plus_b2), (6, squares), (0, gather)], True)

            @block.vector
            def _(e):
                nf = further_of(e, 0)
                with e.If(nf > 0):
                    e.memset(fac[:], 1.0).then_inc(sem("a_fac"), 1)
                with e.Else():
                    e.tensor_scalar(fac[:], fac[:], 1.0, None, ALU.mult).then_inc(sem("a_fac"), 1)
                e.wait_ge(sem("a_fac"), 1)

                def onehot(g, u):
                    wait(e, "a_hT", g, u, 4)
                    inc(e.tensor_scalar(hot[u][:], iota_n[:], col(tab_loc[0], g, u), None, ALU.is_equal), "a_hot")
                    inc(e.tensor_scalar(hotd[u % 4][:], ident[:], col(fac, g, u), None, ALU.mult), "a_hotd")

                def out_h(g, u):
                    wait(e, "a_mlp", g, u)
                    wait(e, "a_out", g, u, 8)
                    wait(e, "a_sq", g, u, 8)
                    inc(e.tensor_scalar(mess[u][:, 0:C], ps_out[u % 2][:, 0:C], col(valid, g, u), None, ALU.mult), "a_z")

                def sum_up(g, u):
                    wait(e, "a_z", g, u)
                    wait(e, "a_sum_h", g, u, 1)
                    inc(e.tensor_tensor(sum_h[:], sum_h[:], mess[u][:, 0:C], ALU.add), "a_sum_h")
                skewed(e, [(4, out_h), (0, onehot), (4, sum_up)], True)

            @block.scalar
            def _(e):
                def evac_hT(g, u):
                    wait(e, "a_hT", g, u)
                    wait(e, "a_hid_mm", g, u, 8)
                    inc(e.activation(xT[u][:], ps_hT[u % 2][:, 0:C].rearrange("p (k n) -> p k n", k=KC), ACT.Copy),
                        "a_hT_sb")

                def relu(g, u):
                    wait(e, "a_hid_mm", g, u)
                    wait(e, "a_mlp", g, u, 2)
                    for f in range(FC):
                        last = e.activation(hidT[u % 2][:, f, :], ps_hid[u % 2][:, f * P:(f + 1) * P], ACT.Relu,
                                            bias=b1_col[:, f:f + 1])
                    inc(last, "a_hid")

                def square(g, u):
                    wait(e, "a_z", g, u)
                    wait(e, "a_sum_hh", g, u, 8)
                    inc(e.activation(xn[u][:], mess[u][:, 0:C], ACT.Square), "a_sq")
                skewed(e, [(1, relu), (0, evac_hT), (3, square)], True)

            @block.tensor
            def _(e):
                def hT(g, u):
                    wait(e, "a_hotd", g, u)
                    wait_dma(e, "got_in", g, u)
                    wait_dma(e, "own_in", g, u)
                    wait(e, "a_hT_sb", g, u, 2)
                    for k in range(KC):
                        ks = slice(k * P, (k + 1) * P)
                        e.matmul(ps_hT[u % 2][:, ks], got[u][:, ks], hot[u][:], start=True, stop=False)
                        last = e.matmul(ps_hT[u % 2][:, ks], own[u][:, ks], hotd[u % 4][:], start=False, stop=True)
                    inc(last, "a_hT")

                def hidden(g, u):
                    wait(e, "a_hT_sb", g, u)
                    wait(e, "a_hid", g, u, 2)
                    for f in range(FC):
                        for k in range(KC):
                            last = e.matmul(ps_hid[u % 2][:, f * P:(f + 1) * P], W1[:, k, f * P:(f + 1) * P],
                                            xT[u][:, k, :], start=(k == 0), stop=(k == KC - 1))
                    inc(last, "a_hid_mm")

                def out_mm(g, u):
                    wait(e, "a_hid", g, u)
                    wait(e, "a_z", g, u, 2)
                    for f in range(FC):
                        last = e.matmul(ps_out[u % 2][:, 0:C], hidT[u % 2][:, f, :], W2[:, f, :],
                                        start=(f == 0), stop=(f == FC - 1))
                    inc(last, "a_mlp")
                skewed(e, [(1, hidden), (0, hT), (2, out_mm)], True)
        pass_over(["ix_made", "a_hT", "a_out", "a_sq", "a_sum_hh", "a_hot", "a_hotd", "a_z", "a_mlp", "a_sum_h", "a_hT_sb",
                   "a_hid_mm", "a_hid"], ["own_in", "conv_out", "got_in"])

        bn_mul = sb("bn_mul", [P, C])
        bn_add = sb("bn_add", [P, C])
        bn_t = sb("bn_t", [P, C])
        bn_m = sb("bn_m", [P, C])
        with nc.Block() as block:
            @block.tensor
            def _(e):
                e.matmul(bank[0][:, 0:C], ones[:], sum_h[:], start=True, stop=True)
                e.matmul(bank[1][:, 0:C], ones[:], sum_hh[:], start=True, stop=True).then_inc(sem("bn_sums"), 1)

            @block.vector
            def _(e):
                k = [0]

                def link(ins):
                    k[0] += 1
                    ins.then_inc(sem("bn_dve"), 1)
                    e.wait_ge(sem("bn_dve"), k[0])
                e.wait_ge(sem("bn_sums"), 1)
                link(e.tensor_scalar(bn_m[:], bank[0][:, 0:C], 1.0 / n_nodes, None, ALU.mult))
                link(e.tensor_tensor(bn_t[:], bn_m[:], bn_m[:], ALU.mult))
                link(e.scalar_tensor_tensor(out=bn_t[:], in0=bank[1][:, 0:C], scalar=1.0 / n_nodes, in1=bn_t[:],
                                            op0=ALU.mult, op1=ALU.subtract))
                link(e.tensor_scalar(bn_t[:], bn_t[:], 0.0, EPS, ALU.max, ALU.add))
                e.wait_ge(sem("bn_act"), 1)
                link(e.reciprocal(bn_mul[:], bn_add[:]))
                link(e.tensor_tensor(bn_mul[:], bn_mul[:], gam_bc[:], ALU.mult))
                link(e.tensor_tensor(bn_m[:], bn_m[:], b2_bc[:], ALU.add))
                link(e.tensor_tensor(bn_m[:], bn_m[:], bn_mul[:], ALU.mult))
                link(e.tensor_tensor(bn_add[:], bet_bc[:], bn_m[:], ALU.subtract))

            @block.scalar
            def _(e):
                e.wait_ge(sem("bn_dve"), 4)
                e.activation(bn_add[:], bn_t[:], ACT.Sqrt).then_inc(sem("bn_act"), 1)

        ps_x = bank[5]
        N_BN, N_MV, N_VE, N_RS, N_NB = 0, 6, 8, 9, 10

        def dve_stats(e):
            def stats(g, u):
                wait(e, "v", g, u)
                inc(e.bn_stats(norms[u][:, N_BN:N_BN + 6], conv[u][:]), "n_stats")

            def aggr(g, u):
                wait(e, "n_stats", g, u, settle=True)
                inc(e.bn_aggr(norms[u][:, N_MV:N_MV + 2], norms[u][:, N_BN:N_BN + 6]), "n_mv")

            def add_eps(g, u):
                wait(e, "n_mv", g, u)
                inc(e.tensor_scalar(norms[u][:, N_VE:N_VE + 1], norms[u][:, N_MV + 1:N_MV + 2], EPS, None, ALU.add),
                    "n_ve")

            def shift(g, u):
                wait(e, "n_rstd", g, u)
                inc(e.tensor_scalar(norms[u][:, N_NB:N_NB + 1], norms[u][:, N_MV:N_MV + 1],
                                    norms[u][:, N_RS:N_RS + 1], -1.0, ALU.mult, ALU.mult), "n_shift")
            return stats, aggr, add_eps, shift

        def pool_rstd(e):
            def rstd(g, u):
                wait(e, "n_ve", g, u)
                inc(e.tensor_tensor(norms[u][:, N_RS:N_RS + 1], norms[u][:, N_VE:N_VE + 1], minus_half[:], ALU.pow),
                    "n_rstd")
            return rstd

        def act_tail(e, stored, q, relu_affine, ps_rows):
            def norm(g, u):
                wait(e, "n_shift", g, u)
                if stored:
                    wait_dma(e, "xn_out", g, u, 1)
                if q is not None:
                    wait(e, "x_turned", g, u, 8)
                inc(e.activation(xn[u][:], conv[u][:], ACT.Identity, bias=norms[u][:, N_NB:N_NB + 1],
                                 scale=norms[u][:, N_RS:N_RS + 1]), "x_normed")

            def evac_xT(g, u):
                wait(e, "x_turned", g, u)
                wait(e, "rows_mm", g, u, 8)
                half = ps_x[:, 0:C]
                if relu_affine:
                    for k in range(KC):
                        last = e.activation(xT[u][:, k, :], half[:, k * P:(k + 1) * P], ACT.Relu,
                                            bias=lnb_col[:, k:k + 1], scale=lng_col[:, k:k + 1])
                    inc(last, "xT_sb")
                else:
                    inc(e.activation(xT[u][:], half.rearrange("p (k n) -> p k n", k=KC), ACT.Copy), "xT_sb")

            def evac_rows(g, u):
                H = heads[q]
                D, HD = C // H, C + H
                wait(e, "rows_mm", g, u)
                wait_dma(e, "rows_out", g, u, 1)
                e.activation(row[u][:, HD + 3 * H:HD + 3 * H + 1], col(loops[LOOPS_OF[q]], g, u), ACT.Copy)
                e.activation(heads_of(row[u][:, 0:HD], H)[:, :, 0:D],
                             ps_rows[u % len(ps_rows)][:, 0:C].rearrange("p (h c) -> p h c", h=H), ACT.Copy)
                inc(e.activation(row[u][:, HD:HD + 2 * H], ps_rows[u % len(ps_rows)][:, C:C + 2 * H], ACT.Copy), "rows_sb")
            return norm, evac_xT, evac_rows

        def pe_tail(e, q, ps_rows):
            def turn(g, u):
                wait(e, "x_normed", g, u)
                wait(e, "xT_sb", g, u, 1)
                half = ps_x[:, 0:C]
                for k in range(KC):
                    last = e.transpose(half[:, k * P:(k + 1) * P], xn[u][:, k * P:(k + 1) * P], ident[:])
                inc(last, "x_turned")

            def rows(g, u):
                W = C + 2 * heads[q]
                wait(e, "xT_sb", g, u)
                wait(e, "rows_sb", g, u, len(ps_rows))
                for k in range(KC):
                    last = e.matmul(ps_rows[u % len(ps_rows)][:, 0:W], xT[u][:, k, :], WG[q][:, k, :],
                                    start=(k == 0), stop=(k == KC - 1))
                inc(last, "rows_mm")
            return turn, rows

        def dve_rows(e, q):
            H = heads[q]
            HD = C + H
            i = LOOPS_OF[q]

            def own_sum(g, u):
                wait(e, "rows_sb", g, u)
                inc(e.tensor_tensor(norms[u][:, 12:12 + H], row[u][:, HD:HD + H], row[u][:, HD + H:HD + 2 * H],
                                    ALU.add), "row_s1")

            def own_leaky(g, u):
                wait(e, "row_s1", g, u)
                inc(e.scalar_tensor_tensor(out=small[u][:, 60:60 + H], in0=norms[u][:, 12:12 + H], scalar=SLOPE,
                                           in1=norms[u][:, 12:12 + H], op0=ALU.mult, op1=ALU.max), "row_s2")

            def own_gone(g, u):
                wait(e, "row_s2", g, u)
                inc(e.tensor_scalar(row[u][:, HD + 2 * H:HD + 3 * H], small[u][:, 60:60 + H], col(gone[i], g, u),
                                    None, ALU.add), "row_done")
            return own_sum, own_leaky, own_gone

        def fresh_rows(e):
            for u in range(NB):
                e.memset(row[u][:], 1.0).then_inc(sem("rows_fresh"), 1)
            stands["rows_fresh"] = stands.get("rows_fresh", 0) + NB

        TAIL = ["n_stats", "n_mv", "n_ve", "n_shift", "n_rstd", "v", "x_normed"]
        ROWS = ["xT_sb", "rows_sb", "x_turned", "rows_mm", "row_s1", "row_s2", "row_done"]

        with nc.Block() as block:
            @block.gpsimd
            def _(e):
                fresh_rows(e)

        with nc.Block() as block:
            @block.sync
            def _(e):
                def load(g, u):
                    wait(e, "b_mul", g, u, 8)
                    inc_dma(e.dma_start(own[u][:, 0:C], rows_of(h_dram, g, u)), "own_in", u)
                    wait(e, "v", g, u, 8)
                    inc_dma(e.dma_start(res[u][:], rows_of(x_in, g, u)), "res_in", u)

                def store_x(g, u):
                    wait(e, "x_normed", g, u)
                    inc_dma(e.dma_start(rows_of(x1_dram, g, u), xn[u][:]), "xn_out", u)

                def store_rows(g, u):
                    wait(e, "row_done", g, u)
                    inc_dma(e.dma_start(rows_of(rows_dram[0], g, u), row[u][:, 0:row_w[0]]), "rows_out", u)
                skewed(e, [(0, load), (6, store_x), (10, store_rows)], True)
                for u in range(NB):
                    e.wait_ge(sem(f"xn_out{u}"), upto("xn_out", 16 * G))
                    e.wait_ge(sem(f"rows_out{u}"), upto("rows_out", 16 * G))

            @block.gpsimd
            def _(e):
                def plus_shift(g, u):
                    wait_dma(e, "res_in", g, u)
                    wait(e, "v", g, u, 8)
                    inc(e.tensor_tensor(wide[u][:, 0:C], res[u][:], bn_add[:], ALU.add), "b_xs")
                skewed(e, [(2, pool_rstd(e)), (0, plus_shift)], True)

            @block.vector
            def _(e):
                stats, aggr, add_eps, shift = dve_stats(e)

                def mul(g, u):
                    wait_dma(e, "own_in", g, u)
                    wait(e, "v", g, u, 8)
                    inc(e.tensor_tensor(mess[u][:, 0:C], own[u][:, 0:C], bn_mul[:], ALU.mult), "b_mul")

                def add(g, u):
                    wait(e, "b_mul", g, u)
                    wait(e, "b_xs", g, u)
                    wait(e, "x_normed", g, u, 8)
                    inc(e.tensor_tensor(conv[u][:], mess[u][:, 0:C], wide[u][:, 0:C], ALU.add), "v")
                own_sum, own_leaky, own_gone = dve_rows(e, 0)
                skewed(e, [(2, aggr), (8, own_sum), (1, add), (2, add_eps), (8, own_leaky), (0, mul), (8, own_gone),
                           (1, stats), (3, shift)], True)

            @block.scalar
            def _(e):
                norm, evac_xT, evac_rows = act_tail(e, True, 0, False, [bank[6], bank[7]])
                skewed(e, [(0, norm), (1, evac_xT), (3, evac_rows)], True)

            @block.tensor
            def _(e):
                turn, rows = pe_tail(e, 0, [bank[6], bank[7]])
                skewed(e, [(0, turn), (2, rows)], True)
        pass_over(TAIL + ROWS + ["b_mul", "b_xs"], ["own_in", "res_in", "xn_out", "rows_out"])

        def gat(q, key, kind, res_dram, xn_dram, nxt):
            H = heads[q]
            D, HD, W = C // H, C + H, row_w[q]
            overflow(q, key, rows_dram[q], rows_dram[q], state_dram[q], H)
            if nxt is not None:
                with nc.Block() as block:
                    @block.gpsimd
                    def _(e):
                        fresh_rows(e)
            own_on_act = H == 1
            assert H > 1 or kind == "residual"
            ps_c = [bank[0], bank[1]]
            turned_hot = bank[2][:, 0:P]
            ps_a = [bank[4], bank[6]]

            def edge_cols(i):
                return bank[3][:, 4 * i:4 * i + H]

            with nc.Block() as block:
                @block.sync
                def _(e):
                    nf = further_of(e, key)

                    def load(g, u):
                        wait(e, "edge_sums", g, u, 8, settle=True)
                        with e.If(nf > 0):
                            inc_dma(e.dma_start(own[u][:, 0:W], rows_of(state_dram[q], g, u)), "own_in", u)
                        with e.Else():
                            inc_dma(e.dma_start(own[u][:, 0:W], rows_of(rows_dram[q], g, u)), "own_in", u)

                    def load_res(g, u):
                        wait(e, "v", g, u, 8)
                        inc_dma(e.dma_start(res[u][:], rows_of(res_dram, g, u)), "res_in", u)

                    def store_x(g, u):
                        wait(e, "x_normed", g, u)
                        inc_dma(e.dma_start(rows_of(xn_dram, g, u), xn[u][:]), "xn_out", u)

                    def store_rows(g, u):
                        wait(e, "row_done", g, u)
                        inc_dma(e.dma_start(rows_of(rows_dram[nxt], g, u), row[u][:, 0:row_w[nxt]]), "rows_out", u)
                    st = [(0, load)]
                    if res_dram is not None:
                        st.append((3, load_res))
                    if xn_dram is not None:
                        st.append((12, store_x))
                    if nxt is not None:
                        st.append((16, store_rows))
                    skewed(e, st, q == 0)
                    for u in range(NB):
                        if xn_dram is not None:
                            e.wait_ge(sem(f"xn_out{u}"), upto("xn_out", 16 * G))
                        if nxt is not None:
                            e.wait_ge(sem(f"rows_out{u}"), upto("rows_out", 16 * G))

                @block.gpsimd
                def _(e):
                    def gather(g, u):
                        wait(e, "edge_sums", g, u, 8)
                        inc(e.tensor_copy(ix[u][:], col(tab_idx[key], g, u)), "ix_made")
                        wait(e, "ix_made", g, u)
                        inc_dma(e.indirect_dma_start(got[u][:, 0:W], None, rows_dram[q],
                                                     bass.IndirectOffsetOnAxis(ap=ix[u][:], axis=0)), "got_in", u)

                    def own_weight(g, u):
                        wait(e, "w_own", g, u)
                        inc(e.tensor_tensor(S(u, S_WC, H), S(u, S_WI, H),
                                            own[u][:, W - 1:W].to_broadcast([P, H]), ALU.mult), "wc")

                    def own_part(g, u):
                        wait(e, "wc", g, u)
                        inc(e.tensor_tensor(heads_of(wide[u][:, 0:HD], H), heads_of(own[u][:, 0:HD], H),
                                            over(S(u, S_WC, H), H, D + 1), ALU.mult), "own_part")

                    def plus_bias(g, u):
                        wait(e, "scaled", g, u)
                        inc(e.tensor_tensor(conv[u][:], conv[u][:], bias_bc[q][:], ALU.add),
                            "v" if kind == "relu_norm" else "v0")

                    def res_bias(g, u):
                        wait_dma(e, "res_in", g, u)
                        inc(e.tensor_tensor(res[u][:], res[u][:], bias_bc[q][:], ALU.add), "res_bias")
                    st = [(10, pool_rstd(e)), (0, gather)]
                    if not own_on_act:
                        st[1:1] = [(5, own_weight), (5, own_part)]
                    if kind == "residual":
                        st.insert(0, (5, res_bias))
                    else:
                        st.append((8, plus_bias))
                    skewed(e, st, q == 0)

                @block.vector
                def _(e):
                    stats, aggr, add_eps, shift = dve_stats(e)

                    def onehot(g, u):
                        inc(e.tensor_scalar(hot[u][:], iota_n[:], col(tab_loc[key], g, u), None, ALU.is_equal), "hot")

                    def maxima(g, u):
                        wait(e, "turned", g, u)
                        inc(e.tensor_reduce(S(u, S_S, H), ps_c[u % 2][:, 0:H * P].rearrange("p (h e) -> p h e", h=H),
                                            axis=AX, op=ALU.max), "m0")

                    def max_ed(g, u):
                        wait(e, "m0", g, u)
                        wait_dma(e, "own_in", g, u)
                        inc(e.tensor_tensor(S(u, S_S, H), S(u, S_S, H), own[u][:, HD + H:HD + 2 * H], ALU.add), "m1")

                    def max_leaky(g, u):
                        wait(e, "m1", g, u)
                        inc(e.scalar_tensor_tensor(out=S(u, S_LK, H), in0=S(u, S_S, H), scalar=SLOPE, in1=S(u, S_S, H),
                                                   op0=ALU.mult, op1=ALU.max), "m2")

                    def max_own(g, u):
                        wait(e, "m2", g, u)
                        inc(e.tensor_tensor(S(u, S_MN, H), S(u, S_LK, H), own[u][:, HD + 2 * H:HD + 3 * H], ALU.max),
                            "m3")

                    def own_diff(g, u):
                        wait(e, "m3", g, u)
                        inc(e.tensor_tensor(S(u, S_DF, H), own[u][:, HD + 2 * H:HD + 3 * H], S(u, S_MN, H),
                                            ALU.subtract), "m4")

                    def edge_sum(g, u):
                        wait(e, "edge_cols", g, u)
                        inc(e.tensor_tensor(S(u, S_A, H), got[u][:, HD:HD + H], edge_cols(0), ALU.add), "z1")

                    def edge_leaky(g, u):
                        wait(e, "z1", g, u)
                        inc(e.scalar_tensor_tensor(out=S(u, S_A2, H), in0=S(u, S_A, H), scalar=SLOPE, in1=S(u, S_A, H),
                                                   op0=ALU.mult, op1=ALU.max), "z2")

                    def edge_diff(g, u):
                        wait(e, "z2", g, u)
                        inc(e.tensor_tensor(S(u, S_Z, H), S(u, S_A2, H), edge_cols(1), ALU.subtract), "z3")

                    def messages(g, u):
                        wait(e, "w_edge", g, u)
                        inc(e.scalar_tensor_tensor(out=heads_of(mess[u][:, 0:HD], H), in0=over(S(u, S_W, H), H, D + 1),
                                                   scalar=1.0, in1=heads_of(got[u][:, 0:HD], H),
                                                   op0=ALU.min, op1=ALU.mult), "mess")

                    def guard(g, u):
                        wait(e, "edge_sums", g, u)
                        den = heads_of(ps_a[u % 2][:, 0:HD], H)[:, :, D]
                        if q == 2:
                            inc(e.tensor_scalar(S(u, S_DG, H), den, 1e-16, None, ALU.add), "r1")
                        else:
                            inc(e.tensor_scalar(S(u, S_DG, H), den, 1e-16, None, ALU.max), "r1")

                    def recip(g, u):
                        wait(e, "r1", g, u)
                        inc(e.reciprocal(S(u, S_RD, H), S(u, S_DG, H)), "r2")

                    def scale(g, u):
                        wait(e, "r2", g, u)
                        wait(e, "x_normed", g, u, 8)
                        inc(e.tensor_tensor(conv[u][:].rearrange("p (h c) -> p h c", h=H),
                                            heads_of(ps_a[u % 2][:, 0:HD], H)[:, :, 0:D],
                                            over(S(u, S_RD, H), H, D), ALU.mult), "scaled")

                    def plus(g, u):
                        wait(e, "scaled", g, u)
                        wait(e, "res_bias", g, u)
                        inc(e.tensor_tensor(conv[u][:], conv[u][:], res[u][:], ALU.add), "v")

                    def scale_plus(g, u):
                        wait(e, "r2", g, u)
                        wait(e, "res_bias", g, u)
                        wait(e, "x_normed", g, u, 8)
                        inc(e.scalar_tensor_tensor(out=conv[u][:], in0=ps_a[u % 2][:, 0:D], scalar=S(u, S_RD, H), in1=res[u][:],
                                                   op0=ALU.mult, op1=ALU.add), "v")

                    def relu_plus(g, u):
                        wait(e, "v0", g, u)
                        wait_dma(e, "res_in", g, u)
                        inc(e.scalar_tensor_tensor(out=conv[u][:], in0=conv[u][:], scalar=0.0, in1=res[u][:],
                                                   op0=ALU.max, op1=ALU.add), "v")
                    st = [(5, guard), (3, messages), (5, recip), (2, edge_sum),
                          (5, scale_plus if H == 1 else scale), (2, edge_leaky), (0, onehot),
                          (2, edge_diff), (1, maxima)]
                    if kind == "residual" and H > 1:
                        st.append((7, plus))
                    if kind == "relu_residual":
                        st.append((7, relu_plus))
                    if nxt is not None:
                        own_sum, own_leaky, own_gone = dve_rows(e, nxt)
                        st.append((12, own_sum))
                    st += [(1, max_ed), (7, stats), (1, max_leaky)]
                    if nxt is not None:
                        st.append((12, own_leaky))
                    st += [(7, aggr), (1, max_own)]
                    if nxt is not None:
                        st.append((12, own_gone))
                    st += [(7, add_eps), (1, own_diff)]
                    st.append((8, shift))
                    skewed(e, st, q == 0)

                @block.scalar
                def _(e):
                    norm, evac_xT, evac_rows = act_tail(e, xn_dram is not None, nxt, kind == "relu_norm", [bank[7]])

                    def offsets(g, u):
                        wait(e, "hot", g, u)
                        wait(e, "turned", g, u, 4)
                        inc(e.activation(off[u % 4][:], hot[u][:], ACT.Copy, bias=-FAR, scale=FAR), "off")

                    def candidates(g, u):
                        wait(e, "off", g, u)
                        wait_dma(e, "got_in", g, u)
                        wait(e, "turned", g, u, 4)
                        for h in range(H):
                            last = e.activation(cand[u % 4][:, h, :], off[u % 4][:], ACT.Identity,
                                                bias=got[u][:, HD + h:HD + h + 1])
                        inc(last, "cand")

                    def evac_hot(g, u):
                        wait(e, "turned", g, u)
                        inc(e.activation(hotT[u][:], turned_hot, ACT.Copy), "hotT")

                    def exp_own(g, u):
                        wait(e, "m4", g, u)
                        inc(e.activation(S(u, S_WI, H), S(u, S_DF, H), ACT.Exp), "w_own")

                    def exp_edge(g, u):
                        wait(e, "z3", g, u)
                        inc(e.activation(S(u, S_W, H), S(u, S_Z, H), ACT.Exp), "w_edge")

                    def own_weight(g, u):
                        wait(e, "w_own", g, u)
                        inc(e.activation(S(u, S_WC, H), S(u, S_WI, H), ACT.Copy, scale=own[u][:, W - 1:W]), "wc")

                    def own_part(g, u):
                        wait(e, "wc", g, u)
                        inc(e.activation(wide[u][:, 0:HD], own[u][:, 0:HD], ACT.Copy, scale=S(u, S_WC, H)), "own_part")
                    st = [(2, exp_own)]
                    if nxt is not None:
                        st.append((12, evac_rows))
                    st += [(9, norm), (1, evac_hot), (0, offsets), (2, exp_edge)]
                    if own_on_act:
                        st.append((2, own_weight))
                    st.append((0, candidates))
                    if own_on_act:
                        st.append((2, own_part))
                    if nxt is not None:
                        st.append((10, evac_xT))
                    skewed(e, st, q == 0)

                @block.tensor
                def _(e):
                    turn, rows = pe_tail(e, nxt, [bank[7]])
                    read_out = "v" if H == 1 else "scaled"

                    def turn_cand(g, u):
                        wait(e, "cand", g, u)
                        wait(e, "m0", g, u, 2)
                        wait(e, "hotT", g, u, 1)
                        for h in range(H):
                            e.transpose(ps_c[u % 2][:, h * P:(h + 1) * P], cand[u % 4][:, h, :], ident[:])
                        inc(e.transpose(turned_hot, hot[u][:], ident[:]), "turned")

                    def to_edges(g, u):
                        wait(e, "hotT", g, u)
                        wait(e, "m3", g, u)
                        wait(e, "z3", g, u, 1)
                        e.matmul(edge_cols(0), hotT[u][:], own[u][:, HD + H:HD + 2 * H], start=True, stop=True)
                        inc(e.matmul(edge_cols(1), hotT[u][:], S(u, S_MN, H), start=True, stop=True), "edge_cols")

                    def to_nodes(g, u):
                        wait(e, "mess", g, u)
                        wait(e, read_out, g, u, 2)
                        e.matmul(ps_a[u % 2][:, 0:HD], hot[u][:], mess[u][:, 0:HD], start=True, stop=False)
                        wait(e, "own_part", g, u)
                        inc(e.matmul(ps_a[u % 2][:, 0:HD], ident[:], wide[u][:, 0:HD], start=False, stop=True),
                            "edge_sums")
                    st = [(1, to_edges), (0, turn_cand), (2, to_nodes)]
                    if nxt is not None:
                        st += [(9, turn), (10, rows)]
                    skewed(e, st, q == 0)

            steps = TAIL + ["ix_made", "wc", "own_part", "hot", "m0", "m1", "m2", "m3", "m4", "z1", "z2", "z3", "mess",
                            "r1", "r2", "off", "cand", "hotT", "w_own", "w_edge", "turned", "edge_cols", "edge_sums"]
            dmas = ["own_in", "got_in"]
            if kind == "residual":
                steps.append("res_bias")
            if H > 1:
                steps.append("scaled")
            if kind == "relu_residual":
                steps.append("v0")
            if res_dram is not None:
                dmas.append("res_in")
            if xn_dram is not None:
                dmas.append("xn_out")
            if nxt is not None:
                steps += ROWS
                dmas.append("rows_out")
            pass_over(steps, dmas)

        gat(0, 0, "relu_norm", None, None, 1)
        gat(1, 0, "residual", x1_dram, x2_dram, 2)
        gat(2, 0, "relu_residual", x2_dram, x3_dram, 3)
        gat(3, 1, "residual", x3_dram, out, None)


_NAMES = ['x', 'src', 'dst', 'L0_gnn_eps', 'L0_gnn_W1', 'L0_gnn_b1', 'L0_gnn_W2', 'L0_gnn_b2', 'L0_gnn_gamma',
          'L0_gnn_beta', 'L1_gnn_W1', 'L1_gnn_a1_src', 'L1_gnn_a1_dst', 'L1_gnn_b1', 'L1_gnn_ln_g', 'L1_gnn_ln_b',
          'L1_gnn_W2', 'L1_gnn_a2_src', 'L1_gnn_a2_dst', 'L1_gnn_b2', 'L2_gnn_W', 'L2_gnn_att_src', 'L2_gnn_att_dst',
          'L2_gnn_bias', 'L3_gnn_weight', 'L3_gnn_att_src', 'L3_gnn_att_dst', 'L3_gnn_bias']


def kernel(_n_loops=20000, **inputs):
    import numpy as _np
    import concourse.bacc as _bacc
    from concourse import mybir as _mybir
    from concourse.bass_utils import run_bass_kernel_spmd as _run

    arrays = {n: _np.ascontiguousarray(inputs[n]) for n in _NAMES}
    n_nodes = arrays["x"].shape[0]
    n_pad = -(-(n_nodes + 1) // (P * NB)) * (P * NB)
    x = _np.zeros((n_pad, C), arrays["x"].dtype)
    x[:n_nodes] = arrays["x"]
    arrays["x"] = x
    for n in ("src", "dst"):
        e = arrays[n]
        padded = _np.full(-(-e.shape[0] // (EB * P)) * (EB * P), n_nodes, e.dtype)
        padded[:e.shape[0]] = e
        arrays[n] = padded

    nc = _bacc.Bacc("TRN2", target_bir_lowering=False, num_devices=1)
    aps = {n: nc.dram_tensor(n, v.shape, _mybir.dt.from_np(v.dtype), kind="ExternalInput").ap()
           for n, v in arrays.items()}
    out = nc.dram_tensor("out", (n_pad, C), _mybir.dt.float32, kind="ExternalOutput").ap()
    graph_layers(nc, aps, out, n_nodes, _n_loops)
    r = _run(nc, [arrays], core_ids=[0])
    return r.results[0]["out"][:n_nodes]
```

```python
import concourse.bass as bass
from concourse import mybir
from contextlib import ExitStack

F32 = mybir.dt.float32
F16 = mybir.dt.float16
BF16 = mybir.dt.bfloat16
I32 = mybir.dt.int32
ALU = mybir.AluOpType
ACT = mybir.ActivationFunctionType
AX = mybir.AxisListType.X

P = 128
C = 256
KC = C // P
HID = 2 * C
FC = HID // P
NB = 8
EB = 6
EPS = 1e-5
FAR = 1e30
SLOPE = 0.2


def graph_layers(nc, a, out, n_nodes, n_loops):
    NP = a["x"].shape[0]
    T = NP // P
    G = T // NB
    J = a["src"].shape[0] // P
    LEVELS = (J * P) // P + 1
    assert T % NB == 0 and G >= 3 and J % EB == 0 and J >= 4 * EB and T <= 512
    x_in = a["x"]

    def dram(name, rows, cols):
        return nc.dram_tensor(name, (rows, cols), F32).ap()

    RWMAX = C + 4 + 3 * 4 + 1
    h_dram = dram("h_dram", NP, C)
    x1_dram = dram("x1_dram", NP, C)
    x2_dram = dram("x2_dram", NP, C)
    x3_dram = dram("x3_dram", NP, C)
    heads = [4, 1, 4, 4]
    row_w = [C + 4 * h + 1 for h in heads]
    LOOPS_OF = [1, 1, 2, 0]
    rows_dram = [dram(f"rows{q}_dram", NP, row_w[q]) for q in range(4)]
    state_dram = [dram(f"state{q}_dram", NP, row_w[q]) for q in range(4)]
    xstate_dram = dram("xstate_dram", NP, C)
    table_dram = [dram(f"table{k}_dram", LEVELS * P, T) for k in range(2)]

    ctx = ExitStack()
    with ctx:
        def sb(name, shape, dt=F32):
            return ctx.enter_context(nc.sbuf_tensor(name, shape, dt))

        def bufs(name, shape, dt=F32, n=NB):
            return [sb(f"{name}{i}", shape, dt) for i in range(n)]

        sems = {}

        def sem(name):
            if name not in sems:
                sems[name] = ctx.enter_context(nc.semaphore(name))
            return sems[name]

        ident = sb("ident", [P, P])
        iota_n = sb("iota_n", [P, P])
        iota_t = sb("iota_t", [P, T], F16)
        iota_16 = sb("iota_16", [P, P], F16)
        before = sb("before", [P, P], F16)
        not_before = sb("not_before", [P, P], F16)
        ones16 = sb("ones16", [P, P], F16)
        ones = sb("ones", [P, P])
        minus_half = sb("minus_half", [P, 1])
        tab_idx = [sb(f"tab_idx{k}", [P, T], I32) for k in range(2)]
        tab_loc = [sb(f"tab_loc{k}", [P, T]) for k in range(2)]
        loops = [sb(f"loops{i}", [P, T]) for i in range(3)]
        gone = [sb(f"gone{i}", [P, T]) for i in range(3)]
        valid = sb("valid", [P, T])
        fac = sb("fac", [P, T])
        n_further = sb("n_further", [P, 2], I32)
        W1 = sb("W1", [P, KC, HID])
        W2 = sb("W2", [P, FC, C])
        b1_col = sb("b1_col", [P, FC])
        b2_bc = sb("b2_bc", [P, C])
        WG = [sb(f"WG{q}", [P, KC, C + 2 * heads[q]]) for q in range(4)]
        bias_bc = [sb(f"bias_bc{q}", [P, C]) for q in range(4)]
        gam_bc = sb("gam_bc", [P, C])
        bet_bc = sb("bet_bc", [P, C])
        lng_col = sb("lng_col", [P, KC])
        lnb_col = sb("lnb_col", [P, KC])
        sum_h = sb("sum_h", [P, C])
        sum_hh = sb("sum_hh", [P, C])

        bank = [ctx.enter_context(nc.psum_tensor(f"bank{i}", [P, 512], F32)) for i in range(8)]

        stands = {}

        def upto(name, n):
            return stands.get(name, 0) + n

        def settled(e):
            e.sem_inc(sem("settled"), 1)

        def wait(e, name, g, u, back=0, scale=1, settle=False):
            n = (g * NB + u + 1 - back) * scale
            if isinstance(n, int) and n <= 0:
                return
            e.wait_ge(sem(name), n + stands.get(name, 0))
            if settle or e.engine == nc.gpsimd.engine:
                settled(e)

        def wait_dma(e, name, g, u, back=0):
            n = g + 1 - back
            if isinstance(n, int) and n <= 0:
                return
            e.wait_ge(sem(f"{name}{u}"), n * 16 + stands.get(name, 0))
            if e.engine == nc.gpsimd.engine:
                settled(e)

        def clear(prefix):
            with nc.Block() as block:
                @block.gpsimd
                def _(e):
                    for name in sorted(sems):
                        if name.startswith(prefix):
                            e.sem_clear(sems[name])

        def inc(ins, name):
            ins.then_inc(sem(name), 1)

        def inc_dma(ins, name, u):
            ins.then_inc(sem(f"{name}{u}"), 16)

        def pass_over(steps, dmas):
            for name in steps:
                stands[name] = stands.get(name, 0) + T
            for name in dmas:
                stands[name] = stands.get(name, 0) + 16 * G

        def skewed(e, stages, fresh=False, n=T, nb=NB):
            deepest = max(d for d, _ in stages)
            first = max(1, -(-(deepest + nb * fresh) // nb))
            for s in range(first * nb):
                for d, f in stages:
                    if s >= d:
                        f((s - d) // nb, (s - d) % nb)
            with e.Fori(first, n // nb) as g:
                for u in range(nb):
                    for d, f in stages:
                        f(g + (u - d) // nb, (u - d) % nb)
            for s in range(n, n + deepest):
                for d, f in stages:
                    if s - d < n:
                        f((s - d) // nb, (s - d) % nb)

        def rows_of(dr, g, u):
            return dr[bass.ds((g * NB + u) * P, P), :]

        def col(t_sb, g, u):
            return t_sb[:, bass.ds(g * NB + u, 1)]

        prep = ExitStack()
        with prep:
            def pb(name, shape, dt=F32):
                return prep.enter_context(nc.sbuf_tensor(name, shape, dt))

            src_i = pb("src_i", [P, J], I32)
            dst_i = pb("dst_i", [P, J], I32)
            src_f = pb("src_f", [P, J])
            dst_f = pb("dst_f", [P, J])
            other = pb("other", [P, J])
            itself = pb("itself", [P, J])
            tmp_i = pb("tmp_i", [P, J], I32)
            tmp_f = pb("tmp_f", [P, J])
            code = pb("code", [P, J])
            code_i = pb("code_i", [P, J], I32)
            dst_loc = pb("dst_loc", [P, J])
            dst_tile = pb("dst_tile", [P, J])
            tile_of = [pb(f"tile_of{k}", [P, J]) for k in range(2)]
            piece = [[pb(f"piece{k}{i}", [P, J]) for i in range(3)] for k in range(2)]
            rank = [pb(f"rank{k}", [P, J]) for k in range(2)]
            level_rank = pb("level_rank", [P, J])
            hit = [pb(f"hit{i}", [P, T], F16) for i in range(EB)]
            hit_other = [pb(f"hit_other{i}", [P, T], F16) for i in range(EB)]
            picked = [pb(f"picked{i}", [P, T]) for i in range(2)]
            slot_f = [pb(f"slot_f{i}", [P, P], F16) for i in range(EB)]
            slot = [[pb(f"slot{i}{k}", [P, P], BF16) for k in range(3)] for i in range(EB)]
            self_loc = [pb(f"self_loc{i}", [P, P], BF16) for i in range(EB)]
            most = pb("most", [P, 2])
            first_level = [pb(f"first_level{k}", [P, T]) for k in range(2)]
            tab_f = pb("tab_f", [P, T])
            tab_c = pb("tab_c", [P, T], I32)
            tab_d = pb("tab_d", [P, 1], I32)
            node_i = pb("node_i", [P, T], I32)
            node_f = pb("node_f", [P, T])
            iota_i = pb("iota_i", [P, max(T, P)], I32)
            eps_bc = pb("eps_bc", [P, 1])
            att_bc = [[pb(f"att_bc{q}{i}", [P, C]) for i in range(2)] for q in range(4)]
            prod = pb("prod", [P, C])

            gat_w = [a["L1_gnn_W1"], a["L1_gnn_W2"], a["L2_gnn_W"], None]
            gat_b = [a["L1_gnn_b1"], a["L1_gnn_b2"], a["L2_gnn_bias"], a["L3_gnn_bias"]]
            gat_a = [(a["L1_gnn_a1_src"], a["L1_gnn_a1_dst"]), (a["L1_gnn_a2_src"], a["L1_gnn_a2_dst"]),
                     (a["L2_gnn_att_src"], a["L2_gnn_att_dst"]), (a["L3_gnn_att_dst"], a["L3_gnn_att_src"])]

            def bcast(v):
                if len(v.shape) == 3:
                    v = v.rearrange("a h c -> (a h c)")
                elif len(v.shape) == 2:
                    v = v.rearrange("h c -> (h c)")
                return v.partition_broadcast(P)

            with nc.Block() as block:
                @block.sync
                def _(e):
                    e.dma_start(src_i[:], a["src"].rearrange("(p j) -> p j", p=P)).then_inc(sem("edges_in"), 16)
                    e.dma_start(dst_i[:], a["dst"].rearrange("(p j) -> p j", p=P)).then_inc(sem("edges_in"), 16)
                    n = 0
                    for dst, s in ([(W1[:], a["L0_gnn_W1"].rearrange("(k p) n -> p k n", p=P)),
                                    (W2[:], a["L0_gnn_W2"].rearrange("(k p) n -> p k n", p=P)),
                                    (b2_bc[:], bcast(a["L0_gnn_b2"])), (gam_bc[:], bcast(a["L0_gnn_gamma"])),
                                    (bet_bc[:], bcast(a["L0_gnn_beta"])), (eps_bc[:], bcast(a["L0_gnn_eps"]))]
                                   + [(bias_bc[q][:], bcast(gat_b[q])) for q in range(4)]
                                   + [(att_bc[q][i][:], bcast(gat_a[q][i])) for q in range(4) for i in range(2)]
                                   + [(WG[q][:, :, 0:C], gat_w[q].rearrange("(k p) n -> p k n", p=P)) for q in range(3)]
                                   + [(WG[3][:, k, 0:C].rearrange("p (h c) -> p h c", h=4),
                                       a["L3_gnn_weight"][:, k * P:(k + 1) * P, :].rearrange("h p c -> p h c"))
                                      for k in range(KC)]):
                        e.dma_start(dst, s).then_inc(sem("weights_in"), 16)
                        n += 16
                    with nc.allow_non_contiguous_dma("a few columns of 128"):
                        for dst, s in [(b1_col[:], a["L0_gnn_b1"].rearrange("(k p) -> p k", p=P)),
                                       (lng_col[:], a["L1_gnn_ln_g"].rearrange("(k p) -> p k", p=P)),
                                       (lnb_col[:], a["L1_gnn_ln_b"].rearrange("(k p) -> p k", p=P))]:
                            e.dma_start(dst, s).then_inc(sem("weights_in"), 16)
                            n += 16
                    e.wait_ge(sem("edges_in"), 32)
                    e.wait_ge(sem("weights_in"), n)

                @block.gpsimd
                def _(e):
                    e.memset(ident[:], 0.0).then_inc(sem("consts"), 1)
                    e.memset(ones[:], 1.0).then_inc(sem("consts"), 1)
                    e.memset(ones16[:], 1.0).then_inc(sem("consts"), 1)
                    e.memset(minus_half[:], -0.5).then_inc(sem("consts"), 1)
                    e.memset(sum_h[:], 0.0).then_inc(sem("consts"), 1)
                    e.memset(sum_hh[:], 0.0).then_inc(sem("consts"), 1)
                    e.iota(iota_i[:], pattern=[[1, max(T, P)]], base=0, channel_multiplier=0).then_inc(sem("consts"), 1)
                    e.iota(node_i[:], pattern=[[P, T]], base=0, channel_multiplier=1).then_inc(sem("consts"), 1)
                    e.wait_ge(sem("consts"), 8)
                    e.affine_select(out=ident[:], in_=ident[:], compare_op=ALU.not_equal, fill=1.0,
                                    base=0, pattern=[[-1, P]], channel_multiplier=1).then_inc(sem("consts"), 1)
                    e.affine_select(out=before[:], in_=ones16[:], compare_op=ALU.is_ge, fill=0.0,
                                    base=-1, pattern=[[1, P]], channel_multiplier=-1).then_inc(sem("consts"), 1)
                    e.affine_select(out=not_before[:], in_=ones16[:], compare_op=ALU.is_ge, fill=0.0,
                                    base=0, pattern=[[-1, P]], channel_multiplier=1).then_inc(sem("consts"), 1)

            with nc.Block() as block:
                @block.vector
                def _(e):
                    k = [0]

                    def link(ins):
                        k[0] += 1
                        ins.then_inc(sem("dve_setup"), 1)
                        e.wait_ge(sem("dve_setup"), k[0])

                    link(e.tensor_copy(iota_t[:], iota_i[:, 0:T]))
                    link(e.tensor_copy(iota_n[:], iota_i[:, 0:P]))
                    link(e.tensor_copy(iota_16[:], iota_i[:, 0:P]))
                    link(e.tensor_copy(node_f[:], node_i[:]))
                    link(e.tensor_scalar(valid[:], node_f[:], float(n_nodes), None, ALU.is_lt))
                    link(e.tensor_scalar(loops[1][:], node_f[:], float(n_loops), None, ALU.is_lt))
                    link(e.tensor_copy(src_f[:], src_i[:]))
                    link(e.tensor_copy(dst_f[:], dst_i[:]))
                    link(e.tensor_tensor(other[:], src_f[:], dst_f[:], ALU.not_equal))
                    link(e.tensor_tensor(itself[:], src_f[:], dst_f[:], ALU.is_equal))
                    for key, own, far in ((0, dst_i, src_f), (1, src_i, dst_f)):
                        link(e.tensor_scalar(tmp_i[:], own[:], 127, None, ALU.bitwise_and))
                        link(e.tensor_copy(tmp_f[:], tmp_i[:]))
                        if key == 0:
                            link(e.tensor_copy(dst_loc[:], tmp_f[:]))
                        link(e.scalar_tensor_tensor(out=code[:], in0=far[:], scalar=256.0, in1=tmp_f[:],
                                                    op0=ALU.mult, op1=ALU.add))
                        link(e.scalar_tensor_tensor(out=code[:], in0=code[:], scalar=1.0, in1=other[:],
                                                    op0=ALU.add, op1=ALU.mult))
                        link(e.tensor_copy(code_i[:], code[:]))
                        for i in range(3):
                            link(e.tensor_scalar(tmp_i[:], code_i[:], 0xFF << (8 * i), None, ALU.bitwise_and))
                            link(e.tensor_copy(piece[key][i][:], tmp_i[:]))
                        link(e.tensor_scalar(tmp_i[:], own[:], 7, None, ALU.logical_shift_right))
                        link(e.tensor_copy(tmp_f[:], tmp_i[:]))
                        if key == 0:
                            link(e.tensor_copy(dst_tile[:], tmp_f[:]))
                        link(e.scalar_tensor_tensor(out=tile_of[key][:], in0=itself[:], scalar=1024.0, in1=tmp_f[:],
                                                    op0=ALU.mult, op1=ALU.add))
                    for q in range(4):
                        H = heads[q]
                        for i in range(2):
                            for kc in range(KC):
                                link(e.tensor_tensor(prod[:], WG[q][:, kc, 0:C], att_bc[q][i][:], ALU.mult))
                                link(e.tensor_reduce(WG[q][:, kc, C + i * H:C + (i + 1) * H],
                                                     prod[:].rearrange("p (h c) -> p h c", h=H),
                                                     axis=AX, op=ALU.add))

            def after(e, name, n):
                if isinstance(n, int) and n <= 0:
                    return
                e.wait_ge(sem(name), n)
                if e.engine == nc.gpsimd.engine:
                    settled(e)

            for key in range(2):
                by_dst = key == 0
                ranked_hit = hit_other if by_dst else hit
                with nc.Block() as block:
                    @block.vector
                    def _(e):
                        def mark(r, u):
                            n = r * EB + u
                            after(e, "tb_placed", n - EB + 1)
                            e.tensor_scalar(hit[u][:], iota_t[:], (dst_tile if by_dst else tile_of[key])[:, bass.ds(n, 1)],
                                            None, ALU.is_equal).then_inc(sem("tb_hit"), 1)

                        def mark_self(r, u):
                            n = r * EB + u
                            e.tensor_scalar(self_loc[u][:], iota_16[:], dst_loc[:, bass.ds(n, 1)],
                                            itself[:, bass.ds(n, 1)], ALU.is_equal, ALU.mult)\
                                .then_inc(sem("tb_self"), 1)

                        def read(r, u):
                            n = r * EB + u
                            after(e, "tb_counted", n + 1)
                            after(e, "tb_read", n - 1)
                            e.scalar_tensor_tensor(out=picked[u % 2][:], in0=bank[u % 2][:, 0:T], scalar=1.0,
                                                   in1=hit[u][:], op0=ALU.mult, op1=ALU.mult,
                                                   accum_out=rank[key][:, bass.ds(n, 1)])\
                                .then_inc(sem("tb_read"), 1)

                        def mark_slot(r, u):
                            n = r * EB + u
                            after(e, "tb_read", n + 1)
                            e.tensor_scalar(slot_f[u][:], iota_16[:], rank[key][:, bass.ds(n, 1)], None, ALU.is_equal)\
                                .then_inc(sem("tb_slot"), 1)
                        stages = [(2, read), (0, mark), (2, mark_slot)]
                        if by_dst:
                            stages.insert(2, (1, mark_self))
                        skewed(e, stages, True, J, EB)
                        e.wait_ge(sem("tb_all_added"), 1)
                        e.tensor_reduce(most[:, 0:1], bank[0][:, 0:T], axis=AX, op=ALU.max).then_inc(sem("tb_levels"), 1)
                        e.tensor_copy(first_level[key][:], bank[2][:, 0:T]).then_inc(sem("tb_taken"), 1)
                        if by_dst:
                            e.tensor_copy(loops[0][:], bank[3][:, 0:T]).then_inc(sem("tb_taken"), 1)
                        e.wait_ge(sem("tb_levels"), 1)
                        e.tensor_scalar(most[:, 1:2], most[:, 0:1], 1.0, -1.0, ALU.max, ALU.add)\
                            .then_inc(sem("tb_levels"), 1)
                        e.wait_ge(sem("tb_levels"), 2)
                        e.tensor_copy(tab_d[:, 0:1], most[:, 1:2]).then_inc(sem("tb_levels"), 1)
                        e.wait_ge(sem("tb_levels"), 3)
                        e.tensor_scalar(n_further[:, key:key + 1], tab_d[:, 0:1], 7, None, ALU.logical_shift_right)\
                            .then_inc(sem("tb_levels"), 1)
                        e.tensor_scalar(level_rank[:], rank[key][:], -128.0, None, ALU.add)\
                            .then_inc(sem("tb_levels"), 1)

                    @block.scalar
                    def _(e):
                        def others(r, u):
                            n = r * EB + u
                            after(e, "tb_hit", n + 1)
                            e.activation(hit_other[u][:], hit[u][:], ACT.Copy, scale=other[:, bass.ds(n, 1)])\
                                .then_inc(sem("tb_other"), 1)

                        def pieces(r, u):
                            n = r * EB + u
                            after(e, "tb_slot", n + 1)
                            for i in range(1 if not by_dst else 2, 3):
                                last = e.activation(slot[u][i][:], slot_f[u][:], ACT.Copy,
                                                    scale=piece[key][i][:, bass.ds(n, 1)])
                            last.then_inc(sem("tb_pieces"), 1)
                        stages = [(3, pieces)]
                        if by_dst:
                            stages.append((0, others))
                        skewed(e, stages, True, J, EB)

                    @block.gpsimd
                    def _(e):
                        def pieces(r, u):
                            n = r * EB + u
                            after(e, "tb_slot", n + 1)
                            for i in range(0, 2 if by_dst else 1):
                                last = e.tensor_tensor(slot[u][i][:], slot_f[u][:],
                                                       piece[key][i][:, bass.ds(n, 1)].to_broadcast([P, P]), ALU.mult)
                            last.then_inc(sem("tb_pieces_pool"), 1)
                        skewed(e, [(0, pieces)], True, J, EB)

                    @block.tensor
                    def _(e):
                        def add(b, first, second, n):
                            if first is not None:
                                e.wait_ge(sem("tb_read"), n - 1)
                                e.matmul(bank[b][:, 0:T], not_before[:], ranked_hit[first][:], start=False, stop=True,
                                         skip_group_check=True)
                            return e.matmul(bank[b][:, 0:T], ones16[:], ranked_hit[second][:], start=first is None,
                                            stop=True, skip_group_check=True)

                        def count(r, u):
                            n = r * EB + u
                            if not isinstance(n, int) or n > 1:
                                add(u % 2, (u - 2) % EB, (u - 1) % EB, n)
                            elif n == 1:
                                add(1, None, 0, 1)
                            e.wait_ge(sem("tb_other" if by_dst else "tb_hit"), n + 1)
                            e.matmul(bank[u % 2][:, 0:T], before[:], ranked_hit[u][:], start=isinstance(n, int) and n == 0,
                                     stop=True, skip_group_check=True).then_inc(sem("tb_counted"), 1)

                        def place(r, u):
                            n = r * EB + u
                            first = isinstance(n, int) and n == 0
                            if by_dst:
                                e.wait_ge(sem("tb_self"), n + 1)
                                e.matmul(bank[3][:, 0:T], self_loc[u][:], hit[u][:], start=first, stop=True,
                                         skip_group_check=True)
                            e.wait_ge(sem("tb_pieces"), n + 1)
                            e.wait_ge(sem("tb_pieces_pool"), n + 1)
                            for i in range(3):
                                last = e.matmul(bank[2][:, 0:T], slot[u][i][:], hit[u][:],
                                                start=(first and i == 0), stop=True, skip_group_check=True)
                            last.then_inc(sem("tb_placed"), 1)
                        skewed(e, [(0, count), (3, place)], True, J, EB)
                        add(0, EB - 2, EB - 1, J).then_inc(sem("tb_all_added"), 1)

                with nc.Block() as block:
                    def when_further(e, body):
                        nf = e.value_load(n_further[0:1, key:key + 1], min_val=0, max_val=LEVELS - 1)
                        with e.If(nf > 0):
                            body(nf)
                        e.nop()

                    @block.vector
                    def _(e):
                        def body(nf):
                            e.sem_inc(sem("pl_table_full"), 2)
                            with e.Fori(0, nf) as L:
                                with e.Fori(0, J // EB) as r:
                                    for u in range(EB):
                                        j = bass.ds(r * EB + u, 1)
                                        e.wait_ge(sem("pl_placed"), L * J + r * EB + u + 1)
                                        e.tensor_scalar(slot_f[u][:], iota_16[:], level_rank[:, j], None, ALU.is_equal)\
                                            .then_inc(sem("pl_slot"), 1)
                                        e.tensor_scalar(hit[u][:], iota_t[:], tile_of[key][:, j], None, ALU.is_equal)\
                                            .then_inc(sem("pl_hit"), 1)
                                e.wait_ge(sem("pl_placed"), (L + 1) * J + EB)
                                e.wait_ge(sem("pl_table_free"), L + 1)
                                e.tensor_copy(tab_f[:], bank[2][:, 0:T]).then_inc(sem("pl_table_full"), 1)
                                e.tensor_scalar(level_rank[:], level_rank[:], -128.0, None, ALU.add)\
                                    .then_inc(sem("pl_table_full"), 1)
                                e.wait_ge(sem("pl_table_full"), (L + 2) * 2)
                                settled(e)
                        when_further(e, body)

                    @block.scalar
                    def _(e):
                        def body(nf):
                            with e.Fori(0, nf) as L:
                                with e.Fori(0, J // EB) as r:
                                    for u in range(EB):
                                        e.wait_ge(sem("pl_slot"), L * J + r * EB + u + 1)
                                        for i in range(3):
                                            last = e.activation(slot[u][i][:], slot_f[u][:], ACT.Copy,
                                                                scale=piece[key][i][:, bass.ds(r * EB + u, 1)])
                                        last.then_inc(sem("pl_pieces"), 1)
                        when_further(e, body)

                    @block.tensor
                    def _(e):
                        def place(L, r, u, first):
                            n = L * J + r * EB + u + 1
                            e.wait_ge(sem("pl_hit"), n)
                            e.wait_ge(sem("pl_pieces"), n)
                            for i in range(3):
                                last = e.matmul(bank[2][:, 0:T], slot[u][i][:], hit[u][:],
                                                start=(first and i == 0), stop=True, skip_group_check=True)
                            last.then_inc(sem("pl_placed"), 1)

                        def body(nf):
                            e.sem_inc(sem("pl_placed"), EB)
                            with e.Fori(0, nf) as L:
                                e.wait_ge(sem("pl_table_full"), L * 2 + 2)
                                for u in range(EB):
                                    place(L, 0, u, u == 0)
                                with e.Fori(1, J // EB) as r:
                                    for u in range(EB):
                                        place(L, r, u, False)
                        when_further(e, body)

                    @block.sync
                    def _(e):
                        def body(nf):
                            e.sem_inc(sem("pl_table_free"), 1)
                            with e.Fori(0, nf) as L:
                                e.wait_ge(sem("pl_table_full"), L * 2 + 4)
                                e.dma_start(table_dram[key][bass.ds(L * P, P), :], tab_f[:])\
                                    .then_inc(sem("pl_table_out"), 16)
                                e.wait_ge(sem("pl_table_out"), L * 16 + 16)
                                e.sem_inc(sem("pl_table_free"), 1)
                        when_further(e, body)
                clear("tb_")
                clear("pl_")

            def decode(e, link, tab, idx, loc, scratch_i):
                link(e.tensor_copy(scratch_i, tab))
                link(e.tensor_scalar(idx, scratch_i, 8, None, ALU.logical_shift_right))
                link(e.tensor_scalar(scratch_i, scratch_i, 255, None, ALU.bitwise_and))
                link(e.tensor_copy(loc, scratch_i))
                link(e.tensor_scalar(loc, loc, -1.0, None, ALU.add))

            with nc.Block() as block:
                @block.vector
                def _(e):
                    k = [0]

                    def link(ins):
                        k[0] += 1
                        ins.then_inc(sem("dve_tables"), 1)
                        e.wait_ge(sem("dve_tables"), k[0])

                    for key in range(2):
                        decode(e, link, first_level[key][:], tab_idx[key][:], tab_loc[key][:], tab_c[:])
                    link(e.tensor_tensor(loops[1][:], loops[1][:], loops[0][:], ALU.add))
                    link(e.tensor_scalar(loops[2][:], loops[0][:], 1.0, None, ALU.add))
                    for i in range(3):
                        link(e.tensor_scalar(gone[i][:], loops[i][:], 0.0, -FAR, ALU.is_equal, ALU.mult))
                    link(e.tensor_scalar(eps_bc[:], eps_bc[:], 1.0, None, ALU.add))
                    link(e.tensor_scalar(fac[:], loops[0][:], eps_bc[:, 0:1], None, ALU.add))

        ix = bufs("ix", [P, 1], I32)
        own = bufs("own", [P, RWMAX])
        got = bufs("got", [P, RWMAX])
        hot = bufs("hot", [P, P])
        hotT = bufs("hotT", [P, P])
        off = bufs("off", [P, P], n=4)
        cand = bufs("cand", [P, 4, P], n=4)
        small = bufs("small", [P, 16 * 4])
        norms = bufs("norms", [P, 16])
        wide = bufs("wide", [P, C + 4])
        mess = bufs("mess", [P, C + 4])
        conv = bufs("conv", [P, C])
        res = bufs("res", [P, C])
        xn = bufs("xn", [P, C])
        xT = bufs("xT", [P, KC, P])
        row = bufs("row", [P, RWMAX])
        ov_tab = sb("ov_tab", [P, T])
        ov_idx = sb("ov_idx", [P, T], I32)
        ov_loc = sb("ov_loc", [P, T])
        ov_sc = sb("ov_sc", [P, T], I32)

        def S(u, i, H):
            return small[u][:, 4 * i:4 * i + H]
        (S_S, S_LK, S_MN, S_DF, S_WI, S_A, S_A2, S_Z, S_W, S_RD, S_WC, S_DG) = range(12)

        def heads_of(ap, H):
            return ap.rearrange("p (h c) -> p h c", h=H)

        def over(ap, H, n):
            return ap.unsqueeze(2).to_broadcast([P, H, n])

        def further_of(e, key):
            return e.value_load(n_further[0:1, key:key + 1], min_val=0, max_val=LEVELS - 1)

        def overflow(tag, key, table, src_rows, state, H):
            W = src_rows.shape[1]
            D = C // H if H else 0
            HD = C + H
            with nc.Block() as block:
                def when(e, body, level_start=None):
                    nf = further_of(e, key)
                    with e.If(nf > 0):
                        with e.Fori(0, nf) as L:
                            if level_start:
                                level_start(L)
                            with e.Fori(0, T) as t:
                                body(L, t, L * T + t)
                        e.nop()

                def s(name):
                    return sem(f"got_ov{tag}" if name == "got" else f"ov_{name}")

                @block.sync
                def _(e):
                    def level(L):
                        e.dma_start(ov_tab[:], table_dram[key][bass.ds(L * P, P), :]).then_inc(s("table"), 16)

                    def body(L, t, g):
                        at = bass.ds(t * P, P)
                        with e.If(L < 1):
                            e.dma_start(own[0][:, 0:W], src_rows[at, :]).then_inc(s("own"), 16)
                        with e.Else():
                            e.dma_start(own[0][:, 0:W], state[at, :]).then_inc(s("own"), 16)
                        e.wait_ge(s("state"), g + 2)
                        e.dma_start(state[at, :], own[0][:, 0:W]).then_inc(s("stored"), 16)
                        e.wait_ge(s("stored"), g * 16 + 16)
                        settled(e)
                    when(e, body, level)

                @block.gpsimd
                def _(e):
                    def body(L, t, g):
                        e.wait_ge(s("decoded"), L * 5 + 5)
                        settled(e)
                        e.wait_ge(s("state"), g + 1)
                        settled(e)
                        e.tensor_copy(ix[0][:], ov_idx[:, bass.ds(t, 1)]).then_inc(s("ix"), 1)
                        e.wait_ge(s("ix"), g + 1)
                        settled(e)
                        e.indirect_dma_start(got[0][:, 0:W], None, table,
                                             bass.IndirectOffsetOnAxis(ap=ix[0][:], axis=0)).then_inc(s("got"), 16)
                    when(e, body)

                @block.vector
                def _(e):
                    e.sem_inc(s("state"), 1)

                    def level(L):
                        e.wait_ge(s("table"), L * 16 + 16)
                        k = [0]

                        def link(ins):
                            k[0] += 1
                            ins.then_inc(s("decoded"), 1)
                            e.wait_ge(s("decoded"), L * 5 + k[0])
                        decode(e, link, ov_tab[:], ov_idx[:], ov_loc[:], ov_sc[:])
                        settled(e)

                    def body(L, t, g):
                        k = [0]
                        n_links = 11 if H else 1

                        def link(ins):
                            k[0] += 1
                            ins.then_inc(s("dve"), 1)
                            e.wait_ge(s("dve"), g * n_links + k[0])

                        e.tensor_scalar(hot[0][:], iota_n[:], ov_loc[:, bass.ds(t, 1)], None, ALU.is_equal)\
                            .then_inc(s("hot"), 1)
                        e.wait_ge(s("own"), (g + 1) * 16)
                        if not H:
                            settled(e)
                            with e.If(L < 1):
                                e.tensor_scalar(own[0][:, 0:C], own[0][:, 0:C], fac[:, bass.ds(t, 1)], None, ALU.mult)\
                                    .then_inc(s("dve"), 1)
                            with e.Else():
                                e.tensor_scalar(own[0][:, 0:C], own[0][:, 0:C], 1.0, None, ALU.mult)\
                                    .then_inc(s("dve"), 1)
                            e.wait_ge(s("dve"), g + 1)
                            e.wait_ge(s("sums"), g + 1)
                            e.tensor_tensor(own[0][:, 0:C], own[0][:, 0:C], bank[2][:, 0:C], ALU.add)\
                                .then_inc(s("state"), 1)
                            return
                        e.wait_ge(s("turned"), g + 1)
                        mx = bank[0][:, 0:H * P].rearrange("p (h e) -> p h e", h=H)
                        es, ed, m = (own[0][:, HD + i * H:HD + (i + 1) * H] for i in range(3))
                        link(e.tensor_reduce(S(0, S_S, H), mx, axis=AX, op=ALU.max))
                        link(e.tensor_tensor(S(0, S_S, H), S(0, S_S, H), ed, ALU.add))
                        link(e.scalar_tensor_tensor(out=S(0, S_LK, H), in0=S(0, S_S, H), scalar=SLOPE, in1=S(0, S_S, H),
                                                    op0=ALU.mult, op1=ALU.max))
                        link(e.tensor_tensor(S(0, S_MN, H), S(0, S_LK, H), m, ALU.max))
                        link(e.tensor_tensor(S(0, S_DF, H), m, S(0, S_MN, H), ALU.subtract))
                        e.wait_ge(s("edge_cols"), g + 1)
                        link(e.tensor_tensor(S(0, S_A, H), got[0][:, HD:HD + H], bank[1][:, P:P + H], ALU.add))
                        link(e.scalar_tensor_tensor(out=S(0, S_A2, H), in0=S(0, S_A, H), scalar=SLOPE, in1=S(0, S_A, H),
                                                    op0=ALU.mult, op1=ALU.max))
                        link(e.tensor_tensor(S(0, S_Z, H), S(0, S_A2, H), bank[1][:, P + 4:P + 4 + H], ALU.subtract))
                        e.wait_ge(s("exps"), (g + 1) * 2)
                        e.scalar_tensor_tensor(out=heads_of(mess[0][:, 0:HD], H), in0=over(S(0, S_W, H), H, D + 1),
                                               scalar=1.0, in1=heads_of(got[0][:, 0:HD], H),
                                               op0=ALU.min, op1=ALU.mult).then_inc(s("mess"), 1)
                        link(e.tensor_scalar(S(0, S_WC, H), S(0, S_WI, H), own[0][:, W - 1:W], None, ALU.mult))
                        link(e.tensor_tensor(heads_of(wide[0][:, 0:HD], H), heads_of(own[0][:, 0:HD], H),
                                             over(S(0, S_WC, H), H, D + 1), ALU.mult))
                        link(e.tensor_copy(m, S(0, S_MN, H)))
                        e.tensor_scalar(own[0][:, W - 1:W], S(0, S_WC, 1), 0.0, 1.0, ALU.mult, ALU.add)\
                            .then_inc(s("count1"), 1)
                        e.wait_ge(s("count1"), g + 1)
                        e.wait_ge(s("sums"), g + 1)
                        e.tensor_tensor(own[0][:, 0:HD], wide[0][:, 0:HD], bank[2][:, 0:HD], ALU.add)\
                            .then_inc(s("state"), 1)
                    when(e, body, level)

                if H:
                    @block.scalar
                    def _(e):
                        def body(L, t, g):
                            e.wait_ge(s("hot"), g + 1)
                            e.activation(off[0][:], hot[0][:], ACT.Copy, scale=FAR, bias=-FAR).then_inc(s("off"), 1)
                            e.wait_ge(s("off"), g + 1)
                            e.wait_ge(s("got"), (g + 1) * 16)
                            for h in range(H):
                                last = e.activation(cand[0][:, h, :], off[0][:], ACT.Identity,
                                                    bias=got[0][:, HD + h:HD + h + 1])
                            last.then_inc(s("cand"), 1)
                            e.wait_ge(s("turned"), g + 1)
                            e.activation(hotT[0][:], bank[1][:, 0:P], ACT.Copy).then_inc(s("hotT"), 1)
                            e.wait_ge(s("dve"), g * 11 + 5)
                            e.activation(S(0, S_WI, H), S(0, S_DF, H), ACT.Exp).then_inc(s("exps"), 1)
                            e.wait_ge(s("dve"), g * 11 + 8)
                            e.activation(S(0, S_W, H), S(0, S_Z, H), ACT.Exp).then_inc(s("exps"), 1)
                        when(e, body)

                @block.tensor
                def _(e):
                    def body(L, t, g):
                        if not H:
                            e.wait_ge(s("hot"), g + 1)
                            e.wait_ge(s("got"), (g + 1) * 16)
                            e.wait_ge(s("state"), g + 1)
                            e.matmul(bank[2][:, 0:C], hot[0][:], got[0][:, 0:C], start=True, stop=True)\
                                .then_inc(s("sums"), 1)
                            return
                        e.wait_ge(s("cand"), g + 1)
                        for h in range(H):
                            e.transpose(bank[0][:, h * P:(h + 1) * P], cand[0][:, h, :], ident[:])
                        e.transpose(bank[1][:, 0:P], hot[0][:], ident[:]).then_inc(s("turned"), 1)
                        e.wait_ge(s("hotT"), g + 1)
                        e.wait_ge(s("dve"), g * 11 + 4)
                        e.matmul(bank[1][:, P:P + H], hotT[0][:], own[0][:, HD + H:HD + 2 * H], start=True, stop=True)
                        e.matmul(bank[1][:, P + 4:P + 4 + H], hotT[0][:], S(0, S_MN, H), start=True, stop=True)\
                            .then_inc(s("edge_cols"), 1)
                        e.wait_ge(s("mess"), g + 1)
                        e.matmul(bank[2][:, 0:HD], hot[0][:], mess[0][:, 0:HD], start=True, stop=True)\
                            .then_inc(s("sums"), 1)
                    when(e, body)

            clear("ov_")

        overflow('x', 0, x_in, x_in, xstate_dram, 0)
        hidT = bufs("hidT", [P, FC, P], n=2)
        with nc.Block() as block:
            ps_hT = [bank[0], bank[1]]
            ps_hid = [bank[2], bank[3]]
            ps_out = [bank[4], bank[5]]
            ps_agg = [bank[6], bank[7]]

            @block.sync
            def _(e):
                nf = further_of(e, 0)

                def load(g, u):
                    wait(e, "a_hT", g, u, 8, settle=True)
                    with e.If(nf > 0):
                        inc_dma(e.dma_start(own[u][:, 0:C], rows_of(xstate_dram, g, u)), "own_in", u)
                    with e.Else():
                        inc_dma(e.dma_start(own[u][:, 0:C], rows_of(x_in, g, u)), "own_in", u)

                def store(g, u):
                    wait(e, "a_out", g, u)
                    inc_dma(e.dma_start(rows_of(h_dram, g, u), conv[u][:]), "conv_out", u)
                skewed(e, [(7, store), (0, load)], True)
                for u in range(NB):
                    e.wait_ge(sem(f"conv_out{u}"), upto("conv_out", 16 * G))

            @block.gpsimd
            def _(e):
                def gather(g, u):
                    wait(e, "a_hT", g, u, 8)
                    inc(e.tensor_copy(ix[u][:], col(tab_idx[0], g, u)), "ix_made")
                    wait(e, "ix_made", g, u)
                    inc_dma(e.indirect_dma_start(got[u][:, 0:C], None, x_in,
                                                 bass.IndirectOffsetOnAxis(ap=ix[u][:], axis=0)), "got_in", u)

                def squares(g, u):
                    wait(e, "a_sq", g, u)
                    wait(e, "a_sum_hh", g, u, 1)
                    inc(e.tensor_tensor(sum_hh[:], sum_hh[:], xn[u][:], ALU.add), "a_sum_hh")

                def plus_b2(g, u):
                    wait(e, "a_z", g, u)
                    wait_dma(e, "conv_out", g, u, 1)
                    inc(e.tensor_tensor(conv[u][:], mess[u][:, 0:C], b2_bc[:], ALU.add), "a_out")
                skewed(e, [(7, plus_b2), (7, squares), (0, gather)], True)

            @block.vector
            def _(e):
                nf = further_of(e, 0)
                with e.If(nf > 0):
                    e.memset(fac[:], 1.0).then_inc(sem("a_fac"), 1)
                with e.Else():
                    e.tensor_scalar(fac[:], fac[:], 1.0, None, ALU.mult).then_inc(sem("a_fac"), 1)
                e.wait_ge(sem("a_fac"), 1)

                def onehot(g, u):
                    wait(e, "a_hT", g, u, 8)
                    inc(e.tensor_scalar(hot[u][:], iota_n[:], col(tab_loc[0], g, u), None, ALU.is_equal), "a_hot")

                def plus_own(g, u):
                    wait(e, "a_agg", g, u)
                    wait_dma(e, "own_in", g, u)
                    wait(e, "a_hT", g, u, 8)
                    inc(e.scalar_tensor_tensor(out=res[u][:], in0=own[u][:, 0:C], scalar=col(fac, g, u),
                                               in1=ps_agg[u % 2][:, 0:C], op0=ALU.mult, op1=ALU.add), "a_own")

                def out_h(g, u):
                    wait(e, "a_mlp", g, u)
                    wait(e, "a_out", g, u, 8)
                    wait(e, "a_sq", g, u, 8)
                    inc(e.tensor_scalar(mess[u][:, 0:C], ps_out[u % 2][:, 0:C], col(valid, g, u), None, ALU.mult), "a_z")

                def sum_up(g, u):
                    wait(e, "a_z", g, u)
                    wait(e, "a_sum_h", g, u, 1)
                    inc(e.tensor_tensor(sum_h[:], sum_h[:], mess[u][:, 0:C], ALU.add), "a_sum_h")
                skewed(e, [(5, out_h), (0, onehot), (1, plus_own), (5, sum_up)], True)

            @block.scalar
            def _(e):
                def evac_hT(g, u):
                    wait(e, "a_hT", g, u)
                    wait(e, "a_hid_mm", g, u, 8)
                    inc(e.activation(xT[u][:], ps_hT[u % 2][:, 0:C].rearrange("p (k n) -> p k n", k=KC), ACT.Copy),
                        "a_hT_sb")

                def relu(g, u):
                    wait(e, "a_hid_mm", g, u)
                    wait(e, "a_mlp", g, u, 2)
                    for f in range(FC):
                        last = e.activation(hidT[u % 2][:, f, :], ps_hid[u % 2][:, f * P:(f + 1) * P], ACT.Relu,
                                            bias=b1_col[:, f:f + 1])
                    inc(last, "a_hid")

                def square(g, u):
                    wait(e, "a_z", g, u)
                    wait(e, "a_sum_hh", g, u, 8)
                    inc(e.activation(xn[u][:], mess[u][:, 0:C], ACT.Square), "a_sq")
                skewed(e, [(2, relu), (1, evac_hT), (4, square)], True)

            @block.tensor
            def _(e):
                def aggregate(g, u):
                    wait(e, "a_hot", g, u)
                    wait_dma(e, "got_in", g, u)
                    wait(e, "a_own", g, u, 2)
                    inc(e.matmul(ps_agg[u % 2][:, 0:C], hot[u][:], got[u][:, 0:C], start=True, stop=True), "a_agg")

                def hT(g, u):
                    wait(e, "a_own", g, u)
                    wait(e, "a_hT_sb", g, u, 2)
                    for k in range(KC):
                        ks = slice(k * P, (k + 1) * P)
                        last = e.transpose(ps_hT[u % 2][:, ks], res[u][:, ks], ident[:])
                    inc(last, "a_hT")

                def hidden(g, u):
                    wait(e, "a_hT_sb", g, u)
                    wait(e, "a_hid", g, u, 2)
                    for f in range(FC):
                        for k in range(KC):
                            last = e.matmul(ps_hid[u % 2][:, f * P:(f + 1) * P], W1[:, k, f * P:(f + 1) * P],
                                            xT[u][:, k, :], start=(k == 0), stop=(k == KC - 1))
                    inc(last, "a_hid_mm")

                def out_mm(g, u):
                    wait(e, "a_hid", g, u)
                    wait(e, "a_z", g, u, 2)
                    for f in range(FC):
                        last = e.matmul(ps_out[u % 2][:, 0:C], hidT[u % 2][:, f, :], W2[:, f, :],
                                        start=(f == 0), stop=(f == FC - 1))
                    inc(last, "a_mlp")
                skewed(e, [(2, hidden), (1, hT), (0, aggregate), (3, out_mm)], True)
        pass_over(["ix_made", "a_hT", "a_out", "a_sq", "a_sum_hh", "a_hot", "a_agg", "a_own", "a_z", "a_mlp", "a_sum_h", "a_hT_sb",
                   "a_hid_mm", "a_hid"], ["own_in", "conv_out", "got_in"])

        bn_mul = sb("bn_mul", [P, C])
        bn_add = sb("bn_add", [P, C])
        bn_t = sb("bn_t", [P, C])
        bn_m = sb("bn_m", [P, C])
        with nc.Block() as block:
            @block.tensor
            def _(e):
                e.matmul(bank[0][:, 0:C], ones[:], sum_h[:], start=True, stop=True)
                e.matmul(bank[1][:, 0:C], ones[:], sum_hh[:], start=True, stop=True).then_inc(sem("bn_sums"), 1)

            @block.vector
            def _(e):
                k = [0]

                def link(ins):
                    k[0] += 1
                    ins.then_inc(sem("bn_dve"), 1)
                    e.wait_ge(sem("bn_dve"), k[0])
                e.wait_ge(sem("bn_sums"), 1)
                link(e.tensor_scalar(bn_m[:], bank[0][:, 0:C], 1.0 / n_nodes, None, ALU.mult))
                link(e.tensor_tensor(bn_t[:], bn_m[:], bn_m[:], ALU.mult))
                link(e.scalar_tensor_tensor(out=bn_t[:], in0=bank[1][:, 0:C], scalar=1.0 / n_nodes, in1=bn_t[:],
                                            op0=ALU.mult, op1=ALU.subtract))
                link(e.tensor_scalar(bn_t[:], bn_t[:], 0.0, EPS, ALU.max, ALU.add))
                e.wait_ge(sem("bn_act"), 1)
                link(e.reciprocal(bn_mul[:], bn_add[:]))
                link(e.tensor_tensor(bn_mul[:], bn_mul[:], gam_bc[:], ALU.mult))
                link(e.tensor_tensor(bn_m[:], bn_m[:], b2_bc[:], ALU.add))
                link(e.tensor_tensor(bn_m[:], bn_m[:], bn_mul[:], ALU.mult))
                link(e.tensor_tensor(bn_add[:], bet_bc[:], bn_m[:], ALU.subtract))

            @block.scalar
            def _(e):
                e.wait_ge(sem("bn_dve"), 4)
                e.activation(bn_add[:], bn_t[:], ACT.Sqrt).then_inc(sem("bn_act"), 1)

        ps_x = bank[5]
        N_BN, N_MV, N_VE, N_RS, N_NB = 0, 6, 8, 9, 10

        def dve_stats(e):
            def stats(g, u):
                wait(e, "v", g, u)
                inc(e.bn_stats(norms[u][:, N_BN:N_BN + 6], conv[u][:]), "n_stats")

            def aggr(g, u):
                wait(e, "n_stats", g, u, settle=True)
                inc(e.bn_aggr(norms[u][:, N_MV:N_MV + 2], norms[u][:, N_BN:N_BN + 6]), "n_mv")

            def add_eps(g, u):
                wait(e, "n_mv", g, u)
                inc(e.tensor_scalar(norms[u][:, N_VE:N_VE + 1], norms[u][:, N_MV + 1:N_MV + 2], EPS, None, ALU.add),
                    "n_ve")

            def shift(g, u):
                wait(e, "n_rstd", g, u)
                inc(e.tensor_scalar(norms[u][:, N_NB:N_NB + 1], norms[u][:, N_MV:N_MV + 1],
                                    norms[u][:, N_RS:N_RS + 1], -1.0, ALU.mult, ALU.mult), "n_shift")
            return stats, aggr, add_eps, shift

        def pool_rstd(e):
            def rstd(g, u):
                wait(e, "n_ve", g, u)
                inc(e.tensor_tensor(norms[u][:, N_RS:N_RS + 1], norms[u][:, N_VE:N_VE + 1], minus_half[:], ALU.pow),
                    "n_rstd")
            return rstd

        def act_tail(e, stored, q, relu_affine, ps_rows):
            def norm(g, u):
                wait(e, "n_shift", g, u)
                if stored:
                    wait_dma(e, "xn_out", g, u, 1)
                if q is not None:
                    wait(e, "x_turned", g, u, 8)
                inc(e.activation(xn[u][:], conv[u][:], ACT.Identity, bias=norms[u][:, N_NB:N_NB + 1],
                                 scale=norms[u][:, N_RS:N_RS + 1]), "x_normed")

            def evac_xT(g, u):
                wait(e, "x_turned", g, u)
                wait(e, "rows_mm", g, u, 8)
                half = ps_x[:, 0:C]
                if relu_affine:
                    for k in range(KC):
                        last = e.activation(xT[u][:, k, :], half[:, k * P:(k + 1) * P], ACT.Relu,
                                            bias=lnb_col[:, k:k + 1], scale=lng_col[:, k:k + 1])
                    inc(last, "xT_sb")
                else:
                    inc(e.activation(xT[u][:], half.rearrange("p (k n) -> p k n", k=KC), ACT.Copy), "xT_sb")

            def evac_rows(g, u):
                H = heads[q]
                D, HD = C // H, C + H
                wait(e, "rows_mm", g, u)
                wait_dma(e, "rows_out", g, u, 1)
                e.activation(row[u][:, HD + 3 * H:HD + 3 * H + 1], col(loops[LOOPS_OF[q]], g, u), ACT.Copy)
                e.activation(heads_of(row[u][:, 0:HD], H)[:, :, 0:D],
                             ps_rows[u % len(ps_rows)][:, 0:C].rearrange("p (h c) -> p h c", h=H), ACT.Copy)
                inc(e.activation(row[u][:, HD:HD + 2 * H], ps_rows[u % len(ps_rows)][:, C:C + 2 * H], ACT.Copy), "rows_sb")
            return norm, evac_xT, evac_rows

        def pe_tail(e, q, ps_rows):
            def turn(g, u):
                wait(e, "x_normed", g, u)
                wait(e, "xT_sb", g, u, 1)
                half = ps_x[:, 0:C]
                for k in range(KC):
                    last = e.transpose(half[:, k * P:(k + 1) * P], xn[u][:, k * P:(k + 1) * P], ident[:])
                inc(last, "x_turned")

            def rows(g, u):
                W = C + 2 * heads[q]
                wait(e, "xT_sb", g, u)
                wait(e, "rows_sb", g, u, len(ps_rows))
                for k in range(KC):
                    last = e.matmul(ps_rows[u % len(ps_rows)][:, 0:W], xT[u][:, k, :], WG[q][:, k, :],
                                    start=(k == 0), stop=(k == KC - 1))
                inc(last, "rows_mm")
            return turn, rows

        def dve_rows(e, q):
            H = heads[q]
            HD = C + H
            i = LOOPS_OF[q]

            def own_sum(g, u):
                wait(e, "rows_sb", g, u)
                inc(e.tensor_tensor(norms[u][:, 12:12 + H], row[u][:, HD:HD + H], row[u][:, HD + H:HD + 2 * H],
                                    ALU.add), "row_s1")

            def own_leaky(g, u):
                wait(e, "row_s1", g, u)
                inc(e.scalar_tensor_tensor(out=small[u][:, 60:60 + H], in0=norms[u][:, 12:12 + H], scalar=SLOPE,
                                           in1=norms[u][:, 12:12 + H], op0=ALU.mult, op1=ALU.max), "row_s2")

            def own_gone(g, u):
                wait(e, "row_s2", g, u)
                inc(e.tensor_scalar(row[u][:, HD + 2 * H:HD + 3 * H], small[u][:, 60:60 + H], col(gone[i], g, u),
                                    None, ALU.add), "row_done")
            return own_sum, own_leaky, own_gone

        def fresh_rows(e):
            for u in range(NB):
                e.memset(row[u][:], 1.0).then_inc(sem("rows_fresh"), 1)
            stands["rows_fresh"] = stands.get("rows_fresh", 0) + NB

        TAIL = ["n_stats", "n_mv", "n_ve", "n_shift", "n_rstd", "v", "x_normed"]
        ROWS = ["xT_sb", "rows_sb", "x_turned", "rows_mm", "row_s1", "row_s2", "row_done"]

        with nc.Block() as block:
            @block.gpsimd
            def _(e):
                fresh_rows(e)

        with nc.Block() as block:
            @block.sync
            def _(e):
                def load(g, u):
                    wait(e, "b_mul", g, u, 8)
                    inc_dma(e.dma_start(own[u][:, 0:C], rows_of(h_dram, g, u)), "own_in", u)
                    wait(e, "v", g, u, 8)
                    inc_dma(e.dma_start(res[u][:], rows_of(x_in, g, u)), "res_in", u)

                def store_x(g, u):
                    wait(e, "x_normed", g, u)
                    inc_dma(e.dma_start(rows_of(x1_dram, g, u), xn[u][:]), "xn_out", u)

                def store_rows(g, u):
                    wait(e, "row_done", g, u)
                    inc_dma(e.dma_start(rows_of(rows_dram[0], g, u), row[u][:, 0:row_w[0]]), "rows_out", u)
                skewed(e, [(0, load), (8, store_x), (12, store_rows)], True)
                for u in range(NB):
                    e.wait_ge(sem(f"xn_out{u}"), upto("xn_out", 16 * G))
                    e.wait_ge(sem(f"rows_out{u}"), upto("rows_out", 16 * G))

            @block.gpsimd
            def _(e):
                def plus_shift(g, u):
                    wait_dma(e, "res_in", g, u)
                    wait(e, "v", g, u, 8)
                    inc(e.tensor_tensor(wide[u][:, 0:C], res[u][:], bn_add[:], ALU.add), "b_xs")
                skewed(e, [(2, pool_rstd(e)), (0, plus_shift)], True)

            @block.vector
            def _(e):
                stats, aggr, add_eps, shift = dve_stats(e)

                def mul(g, u):
                    wait_dma(e, "own_in", g, u)
                    wait(e, "v", g, u, 8)
                    inc(e.tensor_tensor(mess[u][:, 0:C], own[u][:, 0:C], bn_mul[:], ALU.mult), "b_mul")

                def add(g, u):
                    wait(e, "b_mul", g, u)
                    wait(e, "b_xs", g, u)
                    wait(e, "x_normed", g, u, 8)
                    inc(e.tensor_tensor(conv[u][:], mess[u][:, 0:C], wide[u][:, 0:C], ALU.add), "v")
                own_sum, own_leaky, own_gone = dve_rows(e, 0)
                skewed(e, [(2, aggr), (8, own_sum), (1, add), (2, add_eps), (8, own_leaky), (0, mul), (8, own_gone),
                           (1, stats), (3, shift)], True)

            @block.scalar
            def _(e):
                norm, evac_xT, evac_rows = act_tail(e, True, 0, False, [bank[6], bank[7]])
                skewed(e, [(0, norm), (1, evac_xT), (3, evac_rows)], True)

            @block.tensor
            def _(e):
                turn, rows = pe_tail(e, 0, [bank[6], bank[7]])
                skewed(e, [(0, turn), (2, rows)], True)
        pass_over(TAIL + ROWS + ["b_mul", "b_xs"], ["own_in", "res_in", "xn_out", "rows_out"])

        def gat(q, key, kind, res_dram, xn_dram, nxt):
            H = heads[q]
            D, HD, W = C // H, C + H, row_w[q]
            overflow(q, key, rows_dram[q], rows_dram[q], state_dram[q], H)
            if nxt is not None:
                with nc.Block() as block:
                    @block.gpsimd
                    def _(e):
                        fresh_rows(e)
            own_on_act = H == 1
            assert H > 1 or kind == "residual"
            ps_c = [bank[0], bank[1]]
            turned_hot = bank[2][:, 0:P]
            ps_a = [bank[4], bank[6]]

            def edge_cols(i):
                return bank[3][:, 4 * i:4 * i + H]

            with nc.Block() as block:
                @block.sync
                def _(e):
                    nf = further_of(e, key)

                    def load(g, u):
                        wait(e, "edge_sums", g, u, 8, settle=True)
                        with e.If(nf > 0):
                            inc_dma(e.dma_start(own[u][:, 0:W], rows_of(state_dram[q], g, u)), "own_in", u)
                        with e.Else():
                            inc_dma(e.dma_start(own[u][:, 0:W], rows_of(rows_dram[q], g, u)), "own_in", u)

                    def load_res(g, u):
                        wait(e, "v", g, u, 8)
                        inc_dma(e.dma_start(res[u][:], rows_of(res_dram, g, u)), "res_in", u)

                    def store_x(g, u):
                        wait(e, "x_normed", g, u)
                        inc_dma(e.dma_start(rows_of(xn_dram, g, u), xn[u][:]), "xn_out", u)

                    def store_rows(g, u):
                        wait(e, "row_done", g, u)
                        inc_dma(e.dma_start(rows_of(rows_dram[nxt], g, u), row[u][:, 0:row_w[nxt]]), "rows_out", u)
                    st = [(0, load)]
                    if res_dram is not None:
                        st.append((3, load_res))
                    if xn_dram is not None:
                        st.append((12, store_x))
                    if nxt is not None:
                        st.append((16, store_rows))
                    skewed(e, st, q == 0)
                    for u in range(NB):
                        if xn_dram is not None:
                            e.wait_ge(sem(f"xn_out{u}"), upto("xn_out", 16 * G))
                        if nxt is not None:
                            e.wait_ge(sem(f"rows_out{u}"), upto("rows_out", 16 * G))

                @block.gpsimd
                def _(e):
                    def gather(g, u):
                        wait(e, "edge_sums", g, u, 8)
                        inc(e.tensor_copy(ix[u][:], col(tab_idx[key], g, u)), "ix_made")
                        wait(e, "ix_made", g, u)
                        inc_dma(e.indirect_dma_start(got[u][:, 0:W], None, rows_dram[q],
                                                     bass.IndirectOffsetOnAxis(ap=ix[u][:], axis=0)), "got_in", u)

                    def own_weight(g, u):
                        wait(e, "w_own", g, u)
                        inc(e.tensor_tensor(S(u, S_WC, H), S(u, S_WI, H),
                                            own[u][:, W - 1:W].to_broadcast([P, H]), ALU.mult), "wc")

                    def own_part(g, u):
                        wait(e, "wc", g, u)
                        inc(e.tensor_tensor(heads_of(wide[u][:, 0:HD], H), heads_of(own[u][:, 0:HD], H),
                                            over(S(u, S_WC, H), H, D + 1), ALU.mult), "own_part")

                    def plus_bias(g, u):
                        wait(e, "scaled", g, u)
                        inc(e.tensor_tensor(conv[u][:], conv[u][:], bias_bc[q][:], ALU.add),
                            "v" if kind == "relu_norm" else "v0")

                    def res_bias(g, u):
                        wait_dma(e, "res_in", g, u)
                        inc(e.tensor_tensor(res[u][:], res[u][:], bias_bc[q][:], ALU.add), "res_bias")
                    st = [(10, pool_rstd(e)), (0, gather)]
                    if not own_on_act:
                        st[1:1] = [(5, own_weight), (5, own_part)]
                    if kind == "residual":
                        st.insert(0, (5, res_bias))
                    else:
                        st.append((8, plus_bias))
                    skewed(e, st, q == 0)

                @block.vector
                def _(e):
                    stats, aggr, add_eps, shift = dve_stats(e)

                    def onehot(g, u):
                        inc(e.tensor_scalar(hot[u][:], iota_n[:], col(tab_loc[key], g, u), None, ALU.is_equal), "hot")

                    def maxima(g, u):
                        wait(e, "turned", g, u)
                        inc(e.tensor_reduce(S(u, S_S, H), ps_c[u % 2][:, 0:H * P].rearrange("p (h e) -> p h e", h=H),
                                            axis=AX, op=ALU.max), "m0")

                    def max_ed(g, u):
                        wait(e, "m0", g, u)
                        wait_dma(e, "own_in", g, u)
                        inc(e.tensor_tensor(S(u, S_S, H), S(u, S_S, H), own[u][:, HD + H:HD + 2 * H], ALU.add), "m1")

                    def max_leaky(g, u):
                        wait(e, "m1", g, u)
                        inc(e.scalar_tensor_tensor(out=S(u, S_LK, H), in0=S(u, S_S, H), scalar=SLOPE, in1=S(u, S_S, H),
                                                   op0=ALU.mult, op1=ALU.max), "m2")

                    def max_own(g, u):
                        wait(e, "m2", g, u)
                        inc(e.tensor_tensor(S(u, S_MN, H), S(u, S_LK, H), own[u][:, HD + 2 * H:HD + 3 * H], ALU.max),
                            "m3")

                    def own_diff(g, u):
                        wait(e, "m3", g, u)
                        inc(e.tensor_tensor(S(u, S_DF, H), own[u][:, HD + 2 * H:HD + 3 * H], S(u, S_MN, H),
                                            ALU.subtract), "m4")

                    def edge_sum(g, u):
                        wait(e, "edge_cols", g, u)
                        inc(e.tensor_tensor(S(u, S_A, H), got[u][:, HD:HD + H], edge_cols(0), ALU.add), "z1")

                    def edge_leaky(g, u):
                        wait(e, "z1", g, u)
                        inc(e.scalar_tensor_tensor(out=S(u, S_A2, H), in0=S(u, S_A, H), scalar=SLOPE, in1=S(u, S_A, H),
                                                   op0=ALU.mult, op1=ALU.max), "z2")

                    def edge_diff(g, u):
                        wait(e, "z2", g, u)
                        inc(e.tensor_tensor(S(u, S_Z, H), S(u, S_A2, H), edge_cols(1), ALU.subtract), "z3")

                    def messages(g, u):
                        wait(e, "w_edge", g, u)
                        inc(e.scalar_tensor_tensor(out=heads_of(mess[u][:, 0:HD], H), in0=over(S(u, S_W, H), H, D + 1),
                                                   scalar=1.0, in1=heads_of(got[u][:, 0:HD], H),
                                                   op0=ALU.min, op1=ALU.mult), "mess")

                    def guard(g, u):
                        wait(e, "edge_sums", g, u)
                        den = heads_of(ps_a[u % 2][:, 0:HD], H)[:, :, D]
                        if q == 2:
                            inc(e.tensor_scalar(S(u, S_DG, H), den, 1e-16, None, ALU.add), "r1")
                        else:
                            inc(e.tensor_scalar(S(u, S_DG, H), den, 1e-16, None, ALU.max), "r1")

                    def recip(g, u):
                        wait(e, "r1", g, u)
                        inc(e.reciprocal(S(u, S_RD, H), S(u, S_DG, H)), "r2")

                    def scale(g, u):
                        wait(e, "r2", g, u)
                        wait(e, "x_normed", g, u, 8)
                        inc(e.tensor_tensor(conv[u][:].rearrange("p (h c) -> p h c", h=H),
                                            heads_of(ps_a[u % 2][:, 0:HD], H)[:, :, 0:D],
                                            over(S(u, S_RD, H), H, D), ALU.mult), "scaled")

                    def plus(g, u):
                        wait(e, "scaled", g, u)
                        wait(e, "res_bias", g, u)
                        inc(e.tensor_tensor(conv[u][:], conv[u][:], res[u][:], ALU.add), "v")

                    def scale_plus(g, u):
                        wait(e, "r2", g, u)
                        wait(e, "res_bias", g, u)
                        wait(e, "x_normed", g, u, 8)
                        inc(e.scalar_tensor_tensor(out=conv[u][:], in0=ps_a[u % 2][:, 0:D],
                                                   scalar=S(u, S_RD, H), in1=res[u][:], op0=ALU.mult, op1=ALU.add), "v")

                    def relu_plus(g, u):
                        wait(e, "v0", g, u)
                        wait_dma(e, "res_in", g, u)
                        inc(e.scalar_tensor_tensor(out=conv[u][:], in0=conv[u][:], scalar=0.0, in1=res[u][:],
                                                   op0=ALU.max, op1=ALU.add), "v")
                    st = [(5, guard), (3, messages), (5, recip), (2, edge_sum),
                          (5, scale_plus if H == 1 else scale), (2, edge_leaky), (0, onehot),
                          (2, edge_diff), (1, maxima)]
                    if kind == "residual" and H > 1:
                        st.append((7, plus))
                    if kind == "relu_residual":
                        st.append((7, relu_plus))
                    if nxt is not None:
                        own_sum, own_leaky, own_gone = dve_rows(e, nxt)
                        st.append((12, own_sum))
                    st += [(1, max_ed), (7, stats), (1, max_leaky)]
                    if nxt is not None:
                        st.append((12, own_leaky))
                    st += [(7, aggr), (1, max_own)]
                    if nxt is not None:
                        st.append((12, own_gone))
                    st += [(7, add_eps), (1, own_diff)]
                    st.append((8, shift))
                    skewed(e, st, q == 0)

                @block.scalar
                def _(e):
                    norm, evac_xT, evac_rows = act_tail(e, xn_dram is not None, nxt, kind == "relu_norm", [bank[7]])

                    def offsets(g, u):
                        wait(e, "hot", g, u)
                        wait(e, "turned", g, u, 4)
                        inc(e.activation(off[u % 4][:], hot[u][:], ACT.Copy, bias=-FAR, scale=FAR), "off")

                    def candidates(g, u):
                        wait(e, "off", g, u)
                        wait_dma(e, "got_in", g, u)
                        wait(e, "turned", g, u, 4)
                        for h in range(H):
                            last = e.activation(cand[u % 4][:, h, :], off[u % 4][:], ACT.Identity,
                                                bias=got[u][:, HD + h:HD + h + 1])
                        inc(last, "cand")

                    def evac_hot(g, u):
                        wait(e, "turned", g, u)
                        inc(e.activation(hotT[u][:], turned_hot, ACT.Copy), "hotT")

                    def exp_own(g, u):
                        wait(e, "m4", g, u)
                        inc(e.activation(S(u, S_WI, H), S(u, S_DF, H), ACT.Exp), "w_own")

                    def exp_edge(g, u):
                        wait(e, "z3", g, u)
                        inc(e.activation(S(u, S_W, H), S(u, S_Z, H), ACT.Exp), "w_edge")

                    def own_weight(g, u):
                        wait(e, "w_own", g, u)
                        inc(e.activation(S(u, S_WC, H), S(u, S_WI, H), ACT.Copy, scale=own[u][:, W - 1:W]), "wc")

                    def own_part(g, u):
                        wait(e, "wc", g, u)
                        inc(e.activation(wide[u][:, 0:HD], own[u][:, 0:HD], ACT.Copy, scale=S(u, S_WC, H)), "own_part")
                    st = [(2, exp_own)]
                    if nxt is not None:
                        st.append((12, evac_rows))
                    st += [(9, norm), (1, evac_hot), (0, offsets), (2, exp_edge)]
                    if own_on_act:
                        st.append((2, own_weight))
                    st.append((0, candidates))
                    if own_on_act:
                        st.append((2, own_part))
                    if nxt is not None:
                        st.append((10, evac_xT))
                    skewed(e, st, q == 0)

                @block.tensor
                def _(e):
                    turn, rows = pe_tail(e, nxt, [bank[7]])
                    read_out = "v" if H == 1 else "scaled"

                    def turn_cand(g, u):
                        wait(e, "cand", g, u)
                        wait(e, "m0", g, u, 2)
                        wait(e, "hotT", g, u, 1)
                        for h in range(H):
                            e.transpose(ps_c[u % 2][:, h * P:(h + 1) * P], cand[u % 4][:, h, :], ident[:])
                        inc(e.transpose(turned_hot, hot[u][:], ident[:]), "turned")

                    def to_edges(g, u):
                        wait(e, "hotT", g, u)
                        wait(e, "m3", g, u)
                        wait(e, "z3", g, u, 1)
                        e.matmul(edge_cols(0), hotT[u][:], own[u][:, HD + H:HD + 2 * H], start=True, stop=True)
                        inc(e.matmul(edge_cols(1), hotT[u][:], S(u, S_MN, H), start=True, stop=True), "edge_cols")

                    def to_nodes(g, u):
                        wait(e, "mess", g, u)
                        wait(e, read_out, g, u, 2)
                        e.matmul(ps_a[u % 2][:, 0:HD], hot[u][:], mess[u][:, 0:HD], start=True, stop=False)
                        wait(e, "own_part", g, u)
                        inc(e.matmul(ps_a[u % 2][:, 0:HD], ident[:], wide[u][:, 0:HD], start=False, stop=True),
                            "edge_sums")
                    st = [(1, to_edges), (0, turn_cand), (2, to_nodes)]
                    if nxt is not None:
                        st += [(9, turn), (10, rows)]
                    skewed(e, st, q == 0)

            steps = TAIL + ["ix_made", "wc", "own_part", "hot", "m0", "m1", "m2", "m3", "m4", "z1", "z2", "z3", "mess",
                            "r1", "r2", "off", "cand", "hotT", "w_own", "w_edge", "turned", "edge_cols", "edge_sums"]
            dmas = ["own_in", "got_in"]
            if kind == "residual":
                steps.append("res_bias")
            if H > 1:
                steps.append("scaled")
            if kind == "relu_residual":
                steps.append("v0")
            if res_dram is not None:
                dmas.append("res_in")
            if xn_dram is not None:
                dmas.append("xn_out")
            if nxt is not None:
                steps += ROWS
                dmas.append("rows_out")
            pass_over(steps, dmas)

        gat(0, 0, "relu_norm", None, None, 1)
        gat(1, 0, "residual", x1_dram, x2_dram, 2)
        gat(2, 0, "relu_residual", x2_dram, x3_dram, 3)
        gat(3, 1, "residual", x3_dram, out, None)


_NAMES = ['x', 'src', 'dst', 'L0_gnn_eps', 'L0_gnn_W1', 'L0_gnn_b1', 'L0_gnn_W2', 'L0_gnn_b2', 'L0_gnn_gamma',
          'L0_gnn_beta', 'L1_gnn_W1', 'L1_gnn_a1_src', 'L1_gnn_a1_dst', 'L1_gnn_b1', 'L1_gnn_ln_g', 'L1_gnn_ln_b',
          'L1_gnn_W2', 'L1_gnn_a2_src', 'L1_gnn_a2_dst', 'L1_gnn_b2', 'L2_gnn_W', 'L2_gnn_att_src', 'L2_gnn_att_dst',
          'L2_gnn_bias', 'L3_gnn_weight', 'L3_gnn_att_src', 'L3_gnn_att_dst', 'L3_gnn_bias']


def kernel(_n_loops=20000, **inputs):
    import numpy as _np
    import concourse.bacc as _bacc
    from concourse import mybir as _mybir
    from concourse.bass_utils import run_bass_kernel_spmd as _run

    arrays = {n: _np.ascontiguousarray(inputs[n]) for n in _NAMES}
    n_nodes = arrays["x"].shape[0]
    n_pad = -(-(n_nodes + 1) // (P * NB)) * (P * NB)
    x = _np.zeros((n_pad, C), arrays["x"].dtype)
    x[:n_nodes] = arrays["x"]
    arrays["x"] = x
    for n in ("src", "dst"):
        e = arrays[n]
        padded = _np.full(-(-e.shape[0] // (EB * P)) * (EB * P), n_nodes, e.dtype)
        padded[:e.shape[0]] = e
        arrays[n] = padded

    nc = _bacc.Bacc("TRN2", target_bir_lowering=False, num_devices=1)
    aps = {n: nc.dram_tensor(n, v.shape, _mybir.dt.from_np(v.dtype), kind="ExternalInput").ap()
           for n, v in arrays.items()}
    out = nc.dram_tensor("out", (n_pad, C), _mybir.dt.float32, kind="ExternalOutput").ap()
    graph_layers(nc, aps, out, n_nodes, _n_loops)
    r = _run(nc, [arrays], core_ids=[0])
    return r.results[0]["out"][:n_nodes]
```
